# Optimizing a Trainium2 kernel written in Bass

```python
import numpy as np
import jax
import jax.numpy as jnp

def _softmax(x, axis=-1):
    return jax.nn.softmax(x, axis=axis)

def _gelu(x):
    return jax.nn.gelu(x, approximate=True)

def _silu(x):
    return jax.nn.silu(x)

def _sigmoid(x):
    return jax.nn.sigmoid(x)

def _layernorm(x, axis=-1, eps=1e-05):
    m = jnp.mean(x, axis=axis, keepdims=True)
    v = jnp.var(x, axis=axis, keepdims=True)
    return (x - m) / jnp.sqrt(v + eps)

def _scatter_add(tgt, idx, src, axis=0):
    return tgt.at[idx].add(src)

def _segment_sum(src, seg, n):
    return jax.ops.segment_sum(src, seg, n)
kernel_name = 'mk_hybrid_d1_jaxref_r8_76cd62'

def setup_inputs(seed: int=0):
    np.random.seed(seed)
    _w = jnp.asarray

    def _L0_attn_a_setup():
        import jax, jax.numpy as jnp
        import numpy as np
        B, S, D = (1, 256, 512)
        H = 32
        QL = 192
        KVL = 64
        DN = 128
        DR = 64
        DV = 128
        BASE = 10000.0
        FACTOR = 40.0
        BFAST, BSLOW = (32.0, 1.0)
        OLD_CTX = 4096.0
        MSCALE = 1.0

        def _yarn_inv_freq():
            freqs = 1.0 / BASE ** (jnp.arange(0, DR, 2, dtype=jnp.float32) / DR)
            wavelengths = 2.0 * jnp.pi / freqs
            ramp = jnp.clip((wavelengths / OLD_CTX - BSLOW) / (BFAST - BSLOW), 0.0, 1.0)
            scale = 1.0 - ramp + ramp * FACTOR
            return (freqs / scale, MSCALE)

        def _apply_rope(x, inv_freq, mscale):
            seq = x.shape[-2]
            pos = jnp.arange(seq, dtype=jnp.float32)
            f = jnp.concatenate([pos[:, None] * inv_freq[None, :]] * 2, axis=-1)
            cos = jnp.cos(f) * mscale
            sin = jnp.sin(f) * mscale
            half = DR // 2
            x1, x2 = (x[..., :half], x[..., half:])
            c1, c2 = (cos[:, :half], cos[:, half:])
            s2 = sin[:, half:]
            return jnp.concatenate([x1 * c1 - x2 * s2, x1 * s2 + x2 * c2], axis=-1)
        key = jax.random.key(seed)
        ks = jax.random.split(key, 10)

        def glorot(k, shape):
            lim = np.sqrt(6.0 / (shape[0] + shape[1])).astype(np.float32)
            return jax.random.uniform(k, shape, jnp.float32, -lim, lim)
        return {'hidden_states': jax.random.normal(ks[0], (B, S, D), jnp.float32), 'w_q_down': glorot(ks[1], (D, QL)), 'w_q_up_nope': glorot(ks[2], (QL, H * DN)), 'w_q_up_rope': glorot(ks[3], (QL, H * DR)), 'w_kv_down': glorot(ks[4], (D, KVL)), 'w_k_rope': glorot(ks[5], (D, DR)), 'w_uk': glorot(ks[6], (H * DN, KVL)), 'w_uv': glorot(ks[7], (H * DV, KVL)), 'w_out': glorot(ks[8], (H * DV, D))}
    _L0_attn_a_in = _L0_attn_a_setup()

    def _L0_attn_b_setup():
        import jax, jax.numpy as jnp
        import numpy as np
        B, T, D = (1, 256, 512)
        H, G = (32, 8)
        HD = D // H
        REP = H // G
        KV_DIM = 2 * HD * G
        key = jax.random.key(seed)
        k0, k1, k2, k3 = jax.random.split(key, 4)
        x = jax.random.normal(k0, (B, T, D), dtype=jnp.float32)
        Wq = jax.random.normal(k1, (D, D), dtype=jnp.float32) * 0.02
        Wkv = jax.random.normal(k2, (D, KV_DIM), dtype=jnp.float32) * 0.02
        Wo = jax.random.normal(k3, (D, D), dtype=jnp.float32) * 0.02
        bo = jnp.zeros((D,), dtype=jnp.float32)
        return {'x': x, 'Wq': Wq, 'Wkv': Wkv, 'Wo': Wo, 'bo': bo}
    _L0_attn_b_in = _L0_attn_b_setup()

    def _L0_ffn_setup():
        import jax, jax.numpy as jnp
        import numpy as np
        HID, BOT, RDIM, NSLOT, K, VB = (512, 64, 48, 128, 8, 32)
        TAU_LOW, TAU_HIGH, EARLY_EXIT = (0.5, 2.0, 0.05)

        def _uncertainty(h, Wu1, bu1, Wu2, bu2):
            var = jnp.var(h, axis=-1)
            log_var = jnp.log1p(var)
            norm_var = log_var / (jnp.mean(log_var) + 1e-06)
            learned = (jax.nn.gelu(h @ Wu1.T + bu1) @ Wu2.T + bu2)[..., 0]
            return jnp.clip(norm_var * 0.5 + jax.nn.sigmoid(learned) * 2.5, 0.0, 5.0)
        key = jax.random.key(seed)
        ks = jax.random.split(key, 12)
        B, S = (2, 256)
        return {'hidden_states': jax.random.normal(ks[0], (B, S, HID), dtype=jnp.float32), 'Wq': jax.random.normal(ks[1], (BOT, HID), dtype=jnp.float32) / np.sqrt(HID), 'Wr': jax.random.normal(ks[2], (RDIM, BOT), dtype=jnp.float32) / np.sqrt(BOT), 'aux_keys': jax.random.normal(ks[3], (NSLOT, BOT), dtype=jnp.float32) * 0.01, 'aux_values': jax.random.normal(ks[4], (NSLOT, HID), dtype=jnp.float32) * 0.02, 'Wvd': jax.random.normal(ks[5], (VB, HID), dtype=jnp.float32) * 0.1 / np.sqrt(HID), 'Wvu': jax.random.normal(ks[6], (HID, VB), dtype=jnp.float32) * 0.1 / np.sqrt(VB), 'Wu1': jax.random.normal(ks[7], (HID // 4, HID), dtype=jnp.float32) / np.sqrt(HID), 'bu1': jnp.zeros((HID // 4,), dtype=jnp.float32), 'Wu2': jax.random.normal(ks[8], (1, HID // 4), dtype=jnp.float32) * 0.01, 'bu2': jnp.zeros((1,), dtype=jnp.float32), 'gate_w1': jnp.float32(0.5), 'gate_bias': jnp.float32(-1.0), 'log_rel': jnp.zeros((NSLOT,), dtype=jnp.float32)}
    _L0_ffn_in = _L0_ffn_setup()
    _d = {'L0_attn_a_hidden_states': _L0_attn_a_in['hidden_states'], 'L0_attn_a_w_q_down': _L0_attn_a_in['w_q_down'], 'L0_attn_a_w_q_up_nope': _L0_attn_a_in['w_q_up_nope'], 'L0_attn_a_w_q_up_rope': _L0_attn_a_in['w_q_up_rope'], 'L0_attn_a_w_kv_down': _L0_attn_a_in['w_kv_down'], 'L0_attn_a_w_k_rope': _L0_attn_a_in['w_k_rope'], 'L0_attn_a_w_uk': _L0_attn_a_in['w_uk'], 'L0_attn_a_w_uv': _L0_attn_a_in['w_uv'], 'L0_attn_a_w_out': _L0_attn_a_in['w_out'], 'L0_attn_b_Wq': _L0_attn_b_in['Wq'], 'L0_attn_b_Wkv': _L0_attn_b_in['Wkv'], 'L0_attn_b_Wo': _L0_attn_b_in['Wo'], 'L0_attn_b_bo': _L0_attn_b_in['bo'], 'L0_ffn_Wq': _L0_ffn_in['Wq'], 'L0_ffn_Wr': _L0_ffn_in['Wr'], 'L0_ffn_aux_keys': _L0_ffn_in['aux_keys'], 'L0_ffn_aux_values': _L0_ffn_in['aux_values'], 'L0_ffn_Wvd': _L0_ffn_in['Wvd'], 'L0_ffn_Wvu': _L0_ffn_in['Wvu'], 'L0_ffn_Wu1': _L0_ffn_in['Wu1'], 'L0_ffn_bu1': _L0_ffn_in['bu1'], 'L0_ffn_Wu2': _L0_ffn_in['Wu2'], 'L0_ffn_bu2': _L0_ffn_in['bu2'], 'L0_ffn_gate_w1': _L0_ffn_in['gate_w1'], 'L0_ffn_gate_bias': _L0_ffn_in['gate_bias'], 'L0_ffn_log_rel': _L0_ffn_in['log_rel']}
    _x0 = _d['L0_attn_a_hidden_states']
    _d['L0_attn_a_hidden_states'] = jax.random.normal(jax.random.fold_in(jax.random.key(seed), 1), (2, 1024, 512), dtype=_x0.dtype)
    del _x0
    return _d

def reference(L0_attn_a_hidden_states, L0_attn_a_w_q_down, L0_attn_a_w_q_up_nope, L0_attn_a_w_q_up_rope, L0_attn_a_w_kv_down, L0_attn_a_w_k_rope, L0_attn_a_w_uk, L0_attn_a_w_uv, L0_attn_a_w_out, L0_attn_b_Wq, L0_attn_b_Wkv, L0_attn_b_Wo, L0_attn_b_bo, L0_ffn_Wq, L0_ffn_Wr, L0_ffn_aux_keys, L0_ffn_aux_values, L0_ffn_Wvd, L0_ffn_Wvu, L0_ffn_Wu1, L0_ffn_bu1, L0_ffn_Wu2, L0_ffn_bu2, L0_ffn_gate_w1, L0_ffn_gate_bias, L0_ffn_log_rel):

    def _L0_attn_a_ref(hidden_states, w_q_down, w_q_up_nope, w_q_up_rope, w_kv_down, w_k_rope, w_uk, w_uv, w_out):
        import jax, jax.numpy as jnp
        import numpy as np
        B, S, D = (1, 256, 512)
        H = 32
        QL = 192
        KVL = 64
        DN = 128
        DR = 64
        DV = 128
        BASE = 10000.0
        FACTOR = 40.0
        BFAST, BSLOW = (32.0, 1.0)
        OLD_CTX = 4096.0
        MSCALE = 1.0

        def _yarn_inv_freq():
            freqs = 1.0 / BASE ** (jnp.arange(0, DR, 2, dtype=jnp.float32) / DR)
            wavelengths = 2.0 * jnp.pi / freqs
            ramp = jnp.clip((wavelengths / OLD_CTX - BSLOW) / (BFAST - BSLOW), 0.0, 1.0)
            scale = 1.0 - ramp + ramp * FACTOR
            return (freqs / scale, MSCALE)

        def _apply_rope(x, inv_freq, mscale):
            seq = x.shape[-2]
            pos = jnp.arange(seq, dtype=jnp.float32)
            f = jnp.concatenate([pos[:, None] * inv_freq[None, :]] * 2, axis=-1)
            cos = jnp.cos(f) * mscale
            sin = jnp.sin(f) * mscale
            half = DR // 2
            x1, x2 = (x[..., :half], x[..., half:])
            c1, c2 = (cos[:, :half], cos[:, half:])
            s2 = sin[:, half:]
            return jnp.concatenate([x1 * c1 - x2 * s2, x1 * s2 + x2 * c2], axis=-1)
        b, s, _ = hidden_states.shape
        c_q = hidden_states @ w_q_down
        q_nope = (c_q @ w_q_up_nope).reshape(b, s, H, DN).transpose(0, 2, 1, 3)
        q_rope = (c_q @ w_q_up_rope).reshape(b, s, H, DR).transpose(0, 2, 1, 3)
        c_kv = hidden_states @ w_kv_down
        k_rope = (hidden_states @ w_k_rope)[:, None]
        inv_freq, mscale = _yarn_inv_freq()
        q_rope = _apply_rope(q_rope, inv_freq, mscale)
        k_rope = _apply_rope(k_rope, inv_freq, mscale)
        wuk = w_uk.reshape(H, DN, KVL)
        q_lat = jnp.einsum('bhsd,hdr->bhsr', q_nope, wuk)
        scores = jnp.einsum('bhsr,btr->bhst', q_lat, c_kv) + jnp.einsum('bhsd,btd->bhst', q_rope, k_rope[:, 0])
        scores = scores / jnp.sqrt(jnp.float32(DN + DR))
        causal = jnp.tril(jnp.ones((s, s), dtype=bool))
        scores = jnp.where(causal, scores, jnp.finfo(scores.dtype).min)
        probs = jax.nn.softmax(scores, axis=-1)
        out_lat = jnp.einsum('bhst,btr->bhsr', probs, c_kv)
        wuv = w_uv.reshape(H, DV, KVL)
        out = jnp.einsum('bhsr,hdr->bhsd', out_lat, wuv)
        out = out.transpose(0, 2, 1, 3).reshape(b, s, H * DV)
        return out @ w_out

    def _L0_attn_b_ref(x, Wq, Wkv, Wo, bo):
        import jax, jax.numpy as jnp
        import numpy as np
        B, T, D = (1, 256, 512)
        H, G = (32, 8)
        HD = D // H
        REP = H // G
        KV_DIM = 2 * HD * G
        b, t, d = x.shape
        q = jnp.dot(x, Wq).reshape(b, t, H, HD).transpose(0, 2, 1, 3)
        kv = jnp.dot(x, Wkv).reshape(b, t, G, 2, HD).transpose(2, 3, 0, 1, 4)
        k, v = (kv[:, 0], kv[:, 1])
        k = jnp.broadcast_to(k[:, :, None], (G, b, REP, t, HD)).reshape(b, H, t, HD)
        v = jnp.broadcast_to(v[:, :, None], (G, b, REP, t, HD)).reshape(b, H, t, HD)
        scores = jnp.einsum('bhqd,bhkd->bhqk', q, k)
        causal = jnp.triu(jnp.ones((t, t), dtype=bool), 1)
        scores = jnp.where(causal[None, None], -jnp.inf, scores)
        weights = jax.nn.softmax(scores * (1.0 / HD ** 0.5), axis=-1)
        ctx = jnp.einsum('bhqk,bhkd->bhqd', weights, v)
        ctx = ctx.transpose(0, 2, 1, 3).reshape(b, t, d)
        return jnp.dot(ctx, Wo) + bo

    def _L0_ffn_ref(hidden_states, Wq, Wr, aux_keys, aux_values, Wvd, Wvu, Wu1, bu1, Wu2, bu2, gate_w1, gate_bias, log_rel):
        import jax, jax.numpy as jnp
        import numpy as np
        HID, BOT, RDIM, NSLOT, K, VB = (512, 64, 48, 128, 8, 32)
        TAU_LOW, TAU_HIGH, EARLY_EXIT = (0.5, 2.0, 0.05)

        def _uncertainty(h, Wu1, bu1, Wu2, bu2):
            var = jnp.var(h, axis=-1)
            log_var = jnp.log1p(var)
            norm_var = log_var / (jnp.mean(log_var) + 1e-06)
            learned = (jax.nn.gelu(h @ Wu1.T + bu1) @ Wu2.T + bu2)[..., 0]
            return jnp.clip(norm_var * 0.5 + jax.nn.sigmoid(learned) * 2.5, 0.0, 5.0)
        query = hidden_states @ Wq.T
        rq = query @ Wr.T
        rk = aux_keys @ Wr.T
        router_scores = jnp.einsum('bsr,nr->bsn', rq, rk) / np.sqrt(RDIM) + log_rel
        top_scores, top_idx = jax.lax.top_k(router_scores, K)
        sel_keys = aux_keys[top_idx]
        attn = jnp.einsum('bsd,bskd->bsk', query, sel_keys) / np.sqrt(BOT) + log_rel[top_idx]
        w = jax.nn.softmax(attn, axis=-1)
        sel_vals = aux_values[top_idx]
        aux_out = jnp.einsum('bsk,bskh->bsh', w, sel_vals)
        aux_out = aux_out @ Wvd.T @ Wvu.T
        u = _uncertainty(hidden_states, Wu1, bu1, Wu2, bu2)
        u_norm = jnp.clip((u - TAU_LOW) / (TAU_HIGH - TAU_LOW), 0.0, 1.0)
        gate = jax.nn.sigmoid(gate_w1 * u_norm + gate_bias)
        gate = jnp.where(gate < EARLY_EXIT, 0.0, gate)
        return hidden_states + gate[..., None] * aux_out
    x = L0_attn_a_hidden_states
    x = x + _L0_attn_a_ref(_layernorm(x, axis=-1), L0_attn_a_w_q_down, L0_attn_a_w_q_up_nope, L0_attn_a_w_q_up_rope, L0_attn_a_w_kv_down, L0_attn_a_w_k_rope, L0_attn_a_w_uk, L0_attn_a_w_uv, L0_attn_a_w_out)
    x = x + _L0_ffn_ref(_layernorm(x, axis=-1), L0_ffn_Wq, L0_ffn_Wr, L0_ffn_aux_keys, L0_ffn_aux_values, L0_ffn_Wvd, L0_ffn_Wvu, L0_ffn_Wu1, L0_ffn_bu1, L0_ffn_Wu2, L0_ffn_bu2, L0_ffn_gate_w1, L0_ffn_gate_bias, L0_ffn_log_rel)
    x = x + _L0_attn_b_ref(_layernorm(x, axis=-1), L0_attn_b_Wq, L0_attn_b_Wkv, L0_attn_b_Wo, L0_attn_b_bo)
    x = x + _L0_ffn_ref(_layernorm(x, axis=-1), L0_ffn_Wq, L0_ffn_Wr, L0_ffn_aux_keys, L0_ffn_aux_values, L0_ffn_Wvd, L0_ffn_Wvu, L0_ffn_Wu1, L0_ffn_bu1, L0_ffn_Wu2, L0_ffn_bu2, L0_ffn_gate_w1, L0_ffn_gate_bias, L0_ffn_log_rel)
    return x

_drawn_inputs = setup_inputs


def setup_inputs(seed=0):
    import zlib

    import numpy as np

    out = dict(_drawn_inputs(seed))
    spreads = {'L0_attn_b_bo': (0.0, 0.498), 'L0_ffn_bu1': (0.0, 2.0), 'L0_ffn_log_rel': (0.0, 2.0)}
    factors = {'L0_attn_a_w_q_down': 5.436,
     'L0_attn_a_w_q_up_nope': 8.0,
     'L0_attn_a_w_q_up_rope': 5.724,
     'L0_attn_a_w_k_rope': 5.734,
     'L0_attn_a_w_uk': 8.0,
     'L0_attn_b_Wq': 8.0,
     'L0_attn_b_Wkv': 6.313,
     'L0_attn_b_Wo': 5.768,
     'L0_ffn_Wq': 8.0,
     'L0_ffn_Wr': 8.0,
     'L0_ffn_aux_keys': 8.0,
     'L0_ffn_aux_values': 8.0,
     'L0_ffn_Wvd': 8.0,
     'L0_ffn_Wvu': 8.0,
     'L0_ffn_Wu1': 64.0,
     'L0_ffn_Wu2': 64.0}
    for name, (base, spread) in spreads.items():
        noise = np.random.default_rng([zlib.crc32(name.encode()), seed]).standard_normal(out[name].shape)
        drawn = base * np.exp(spread * noise) if base else spread * noise
        out[name] = jnp.asarray(drawn.astype(out[name].dtype))
    for name, factor in factors.items():
        out[name] = (out[name] * factor).astype(out[name].dtype)
    return out
```

```python
from contextlib import ExitStack

import numpy as np

import concourse.bass as bass
from concourse import mybir

F32 = mybir.dt.float32
BF16 = mybir.dt.bfloat16
ALU = mybir.AluOpType
ACT = mybir.ActivationFunctionType
AX = mybir.AxisListType.X

P = 128
D = 512
KD = D // P
NB = 2
S = 1024
T = NB * S
NT = T // P
TB = S // P
EPS = 1e-5
NEG = -1e30

H = 32
QL = 192
QC = QL // 2
KVL = 64
DN = 128
DR = 64
DV = 128
PAIRS = H // 2
SCALE_A = float(1.0 / np.sqrt(np.float32(DN + DR)))
G = 8
HD = 16
REP = H // G
BOT, RDIM, NSLOT, VB = 64, 48, 128, 32
UH = D // 4

RING_P = 4
LAG = 3


def groups_of(t):
    return [(0, t + 1)] if t < 4 else [(0, 4), (4, t + 1)]


class Shape:

    def __init__(self, heads, tiles_per_chunk, on_act):
        self.heads, self.tpc = heads, tiles_per_chunk
        self.units = [(b, t, h) for b in range(NB) for t in range(TB) for h in range(heads)]
        self.nu = len(self.units)
        self.chunks_per_batch = TB // tiles_per_chunk
        self.nchunk = NB * self.chunks_per_batch
        self.groups = []
        for u, (b, t, h) in enumerate(self.units):
            for j0, j1 in groups_of(t):
                self.groups.append((u, j0, j1, on_act(len(self.groups), u, j0, j1)))
        self.first_group = [next(n for n, g in enumerate(self.groups) if g[0] == u) for u in range(self.nu)]
        self.first_group.append(len(self.groups))
        assert len(self.groups) % 2 == 0

    def chunk_of(self, u):
        b, t, _ = self.units[u]
        return b * self.chunks_per_batch + t // self.tpc

    def last_unit(self, k):
        return (k + 1) * self.tpc * self.heads - 1

    def evacuated(self, n_groups, by_act):
        turn = sum(g[3] == by_act for g in self.groups)
        if n_groups < 0:
            return self.evacuated(n_groups + len(self.groups), by_act) - turn
        return sum(g[3] == by_act for g in self.groups[:n_groups])


def build(nc, io):
    top = ExitStack()
    with top:
        def keep(name, shape, dt=F32):
            return top.enter_context(nc.sbuf_tensor(name, shape, dt))

        X = keep("X", [P, NT, D])
        ident = keep("ident", [P, P])
        ident_b = keep("ident_b", [P, P], BF16)
        causal_b = keep("causal_b", [P, P], BF16)
        consts = dict(X=X, ident=ident, ident_b=ident_b, causal_b=causal_b)
        with ExitStack() as latent:
            kt = {n: latent.enter_context(nc.sbuf_tensor(n, s, F32)) for n, s in (
                ("cq", [QC, 2, T]), ("k_rl", [P, T]), ("k_lr", [P, T]), ("ktok", [P, NT, 192]))}
            latent_inputs(nc, io, consts, kt)
            latent_attention(nc, io, consts, kt)
        mem = {n: keep(n, s) for n, s in (
            ("logit_w", [P, KD, 3 * P]), ("value_w", [P, D]), ("logit_bias", [P, 3 * P]),
            ("u2", [P, UH]), ("bu2", [P, 1]), ("gw1", [P, 1]), ("gbias", [P, 1]))}
        memory_weights(nc, io, consts, mem)
        memory_block(nc, io, consts, mem, "f1", None)
        with ExitStack() as grouped:
            vtok = grouped.enter_context(nc.sbuf_tensor("vtok", [P, NB * G, TB, HD], F32))
            scratch = (nc.dram_tensor("query_parts", (3, D, T), BF16).ap(),
                       nc.dram_tensor("key_parts", (3, NB * G, HD, S), BF16).ap())
            grouped_inputs(nc, io, consts, vtok, scratch)
            grouped_attention(nc, io, consts, vtok, scratch)
        memory_block(nc, io, consts, mem, "f2", io["out"])


def scope(nc, ctx, tag):
    def sb(name, shape, dt=F32):
        return ctx.enter_context(nc.sbuf_tensor(f"{tag}_{name}", shape, dt))

    def ps(name, shape, dt=F32):
        return ctx.enter_context(nc.psum_tensor(f"{tag}_{name}", shape, dt))

    held = []

    def clear():
        nc.clear_and_free_semaphores(held)
        nc.all_engine_barrier()

    ctx.callback(clear)

    def sem(name):
        held.append(nc.alloc_semaphore(f"{tag}_{name}"))
        return held[-1]

    return sb, ps, sem


class Norm:

    def __init__(self, nc, ctx, tag, X, ident):
        sb, ps, sem = scope(nc, ctx, tag)
        self.X, self.ident = X, ident
        self.stats = sb("ln_stats", [P, NT, 6])
        self.mv = sb("ln_mv", [P, NT, 2])
        self.ve = sb("ln_ve", [P, NT])
        self.sd = sb("ln_sd", [P, NT])
        self.rstd = sb("ln_rstd", [P, NT])
        self.h = sb("ln_h", [P, 2, D])
        self.hT = sb("hT", [P, KD, T])
        self.pt = ps("ln_pt", [P, 2, KD, P])
        self.s_stats = sem("ln_stats_ready")
        self.s_mv = sem("ln_mv_ready")
        self.s_ve = sem("ln_ve_ready")
        self.s_sd = sem("ln_sd_ready")
        self.s_rstd = sem("ln_rstd_ready")
        self.s_h = sem("ln_h_ready")
        self.s_tr = sem("ln_transposed")
        self.s_hT = sem("ln_hT_ready")

    def vector_stats(self, dve, x_loaded=None):
        for t in range(NT):
            if x_loaded is not None:
                dve.wait_ge(x_loaded[t // 4], 16)
            dve.bn_stats(self.stats[:, t, :], self.X[:, t, :]).then_inc(self.s_stats, 1)
        for t in range(NT):
            dve.wait_ge(self.s_stats, t + 1)
            dve.bn_aggr(self.mv[:, t, :], self.stats[:, t, :]).then_inc(self.s_mv, 1)
        dve.wait_ge(self.s_mv, NT)
        dve.tensor_scalar(self.ve[:], self.mv[:, :, 1], EPS, None, ALU.add).then_inc(self.s_ve, 1)
        dve.wait_ge(self.s_sd, 1)
        dve.reciprocal(self.rstd[:], self.sd[:]).then_inc(self.s_rstd, 1)
        dve.wait_ge(self.s_rstd, 1)

    def scalar_sqrt(self, act):
        act.wait_ge(self.s_ve, 1)
        act.activation(self.sd[:], self.ve[:], ACT.Sqrt).then_inc(self.s_sd, 1)

    def vector_h(self, dve, t):
        if t >= 2:
            dve.wait_ge(self.s_tr, t - 1)
        dve.tensor_scalar(self.h[:, t % 2, :], self.X[:, t, :], self.mv[:, t, 0:1], self.rstd[:, t:t + 1],
                          ALU.subtract, ALU.mult).then_inc(self.s_h, 1)

    def tensor_transpose(self, pe, t):
        pe.wait_ge(self.s_h, t + 1)
        if t >= 2:
            pe.wait_ge(self.s_hT, t - 1)
        for k in range(KD):
            last = pe.transpose(self.pt[:, t % 2, k, :], self.h[:, t % 2, k * P:(k + 1) * P], self.ident[:])
        last.then_inc(self.s_tr, 1)

    def scalar_hT(self, act, t):
        act.wait_ge(self.s_tr, t + 1)
        act.copy(self.hT[:, :, t * P:(t + 1) * P], self.pt[:, t % 2, :, :]).then_inc(self.s_hT, 1)


def latent_inputs(nc, io, consts, kt):
    X, ident = consts["X"], consts["ident"]
    with ExitStack() as ctx:
        sb, ps, sem = scope(nc, ctx, "li")
        norm = Norm(nc, ctx, "li", X, ident)
        wqd = sb("wqd", [P, KD, QL])
        wkv = sb("wkv", [P, KD, P])
        cosk = sb("cosk", [P, NT, 32])
        sink = sb("sink", [P, NT, 32])
        kv = sb("kv", [P, NT, P])
        tmp = sb("tmp", [P, 4, NT, 32])
        maskf = sb("maskf", [P, P])
        pkv = ps("pkv", [P, 2, 512])
        pcq = ps("pcq", [P, 2, 512])
        pk = ps("pk", [P, 2, 4, P])

        x_loaded = [sem(f"x_loaded{c}") for c in range(4)]
        const_loaded = sem("const_loaded")
        w_loaded = sem("w_loaded")
        table_loaded = sem("table_loaded")
        consts_cast = sem("consts_cast")
        kv_ready, kv_read = sem("kv_ready"), sem("kv_read")
        cq_ready, cq_read = sem("cq_ready"), sem("cq_read")
        prod_ready, rope_ready, lat_ready, dup_ready = (
            sem("prod_ready"), sem("rope_ready"), sem("lat_ready"), sem("dup_ready"))
        kT_ready, kT_read = sem("kT_ready"), [sem("kT_read_act"), sem("kT_read_dve")]

        x_in = io["x"].rearrange("b (t p) d -> p (b t) d", p=P)
        ktok = kt["ktok"]
        block = ctx.enter_context(nc.Block())

        @block.sync
        def _(sp):
            for c in range(4):
                sp.dma_start(X[:, 4 * c:4 * c + 4, :], x_in[:, 4 * c:4 * c + 4, :]).then_inc(x_loaded[c], 16)
            sp.dma_start(cosk[:], io["cos_tok"]).then_inc(table_loaded, 16)
            sp.dma_start(sink[:], io["sin_tok"]).then_inc(table_loaded, 16)

        @block.gpsimd
        def _(pool):
            pool.dma_start(ident[:], io["identity"]).then_inc(const_loaded, 16)
            pool.dma_start(maskf[:], io["causal"]).then_inc(const_loaded, 16)
            pool.dma_start(wqd[:], io["w_q_down"].rearrange("(k p) n -> p k n", p=P)).then_inc(w_loaded, 16)
            pool.dma_start(wkv[:, :, 0:DR], io["w_k_rope"].rearrange("(k p) n -> p k n", p=P)).then_inc(w_loaded, 16)
            pool.dma_start(wkv[:, :, DR:P], io["w_kv_down"].rearrange("(k p) n -> p k n", p=P)).then_inc(w_loaded, 16)
            pool.wait_ge(const_loaded, 32)
            pool.tensor_copy(consts["ident_b"][:], ident[:]).then_inc(consts_cast, 1)
            pool.tensor_copy(consts["causal_b"][:], maskf[:]).then_inc(consts_cast, 1)

        @block.vector
        def _(dve):
            norm.vector_stats(dve, x_loaded)

            def read_kv(t):
                dve.wait_ge(kv_ready, t + 1)
                dve.tensor_copy(kv[:, t, :], pkv[:, t % 2, 0:P]).then_inc(kv_read, 1)

            for t in range(NT):
                norm.vector_h(dve, t)
                if t >= 2:
                    read_kv(t - 2)
            read_kv(NT - 2)
            read_kv(NT - 1)
            dve.wait_ge(kv_read, NT)
            dve.wait_ge(table_loaded, 32)
            x1, x2 = kv[:, :, 0:32], kv[:, :, 32:64]
            for n, (a, b) in enumerate(((x1, cosk), (x2, sink), (x1, sink), (x2, cosk))):
                dve.tensor_tensor(tmp[:, n], a, b[:], ALU.mult).then_inc(prod_ready, 1)
            for half, op in ((0, ALU.subtract), (1, ALU.add)):
                dve.wait_ge(prod_ready, 2 + 2 * half)
                to = ktok[:, :, 0:DR].rearrange("p t (q h i) -> p t q h i", q=2, h=2)[:, :, :, half, :]
                a, b = (tmp[:, 2 * half + n].rearrange("p t (q i) -> p t q i", q=2) for n in range(2))
                for q in range(2):
                    last = dve.tensor_tensor(to[:, :, q, :], a[:, :, q, :], b[:, :, q, :], op)
                    last.then_inc(rope_ready, 1)
            for n in range(8):
                if n % 2:
                    dve.wait_ge(kT_ready, n + 1)
                    dst = kt["k_rl"] if n < 4 else kt["k_lr"]
                    c = n % 4
                    dve.tensor_copy(dst[:, c * 512:(c + 1) * 512], pk[:, n % 2]).then_inc(kT_read[1], 1)

        @block.scalar
        def _(act):
            norm.scalar_sqrt(act)

            def read_cq(n):
                c, m = n // 2, n % 2
                act.wait_ge(cq_ready, n + 1)
                act.copy(kt["cq"][:, m, c * 512:(c + 1) * 512], pcq[0:QC, n % 2, :]).then_inc(cq_read, 1)

            for t in range(NT):
                norm.scalar_hT(act, t)
                if t % 4 == 2 and t > 4:
                    read_cq(2 * (t // 4) - 2)
                    read_cq(2 * (t // 4) - 1)
            read_cq(6)
            read_cq(7)
            act.wait_ge(kv_read, NT)
            act.copy(ktok[:, :, DR:P], kv[:, :, DR:P]).then_inc(lat_ready, 1)
            act.wait_ge(rope_ready, 4)
            act.copy(ktok[:, :, P:192], ktok[:, :, 0:DR]).then_inc(dup_ready, 1)
            for n in range(0, 8, 2):
                act.wait_ge(kT_ready, n + 1)
                dst = kt["k_rl"] if n < 4 else kt["k_lr"]
                c = n % 4
                act.copy(dst[:, c * 512:(c + 1) * 512], pk[:, n % 2]).then_inc(kT_read[0], 1)

        @block.tensor
        def _(pe):
            def keys(t):
                pe.wait_ge(norm.s_hT, t + 1)
                if t >= 2:
                    pe.wait_ge(kv_read, t - 1)
                for k in range(KD):
                    last = pe.matmul(pkv[:, t % 2, 0:P], norm.hT[:, k, t * P:(t + 1) * P], wkv[:, k, :],
                                     start=(k == 0), stop=(k == KD - 1))
                last.then_inc(kv_ready, 1)

            def queries(c):
                for m in range(2):
                    n = 2 * c + m
                    if n >= 2:
                        pe.wait_ge(cq_read, n - 1)
                    for k in range(KD):
                        last = pe.matmul(pcq[0:QC, n % 2, :], wqd[:, k, m * QC:(m + 1) * QC],
                                         norm.hT[:, k, c * 512:(c + 1) * 512], start=(k == 0), stop=(k == KD - 1))
                    last.then_inc(cq_ready, 1)

            pe.wait_ge(const_loaded, 32)
            pe.wait_ge(w_loaded, 48)
            for t in range(NT):
                norm.tensor_transpose(pe, t)
                if t >= 1:
                    keys(t - 1)
                if t % 4 == 1 and t > 4:
                    queries(t // 4 - 1)
            keys(NT - 1)
            queries(3)
            pe.wait_ge(lat_ready, 1)
            for n in range(8):
                if n == 0:
                    pe.wait_ge(rope_ready, 4)
                if n == 4:
                    pe.wait_ge(dup_ready, 1)
                if n >= 2:
                    pe.wait_ge(kT_read[n % 2], n // 2)
                off = 0 if n < 4 else DR
                for j in range(4):
                    t = 4 * (n % 4) + j
                    last = pe.transpose(pk[:, n % 2, j, :], ktok[:, t, off:off + P], ident[:])
                last.then_inc(kT_ready, 1)


def attention_loop(nc, consts, shape, tag, turns, side):
    X, ident = consts["X"], consts["ident"]
    sh = shape
    NU, NGR, NK = sh.nu, len(sh.groups), sh.nchunk
    CW = sh.tpc * P
    M = P // sh.heads

    with ExitStack() as ctx:
        sb, ps, sem = scope(nc, ctx, tag)
        prob = sb("prob", [P, RING_P, S])
        probT = sb("probT", [P, 2, sh.heads, TB, CW])
        negmax = sb("negmax", [P, RING_P])
        rowsum = sb("rowsum", [P, RING_P])
        rinv = sb("rinv", [P, RING_P])
        head_out = sb("head_out", [P, 2, CW])
        score = ps("score", [P, 2, S])
        turned = ps("turned", [P, 2, 4, P])
        misc = ps("misc", [P, 2, 512])

        scores_ready = sem("scores_ready")
        negmax_ready = sem("negmax_ready")
        exp_done = sem("exp_done")
        rinv_ready = sem("rinv_ready")
        units_begun = sem("units_begun")
        prob_ready = sem("prob_ready")
        turned_ready = sem("turned_ready")
        read_dve = sem("read_dve")
        read_act = sem("read_act")
        pv_ready = sem("pv_ready")
        head_out_ready = sem("head_out_ready")
        proj_ready = sem("proj_ready")
        x_added = sem("x_added")

        side.allocate(sb, sem, misc, scores_ready, pv_ready, proj_ready)

        items = list(side.items)
        for k in range(NK):
            at = sh.last_unit(k) + LAG + 1
            items.append((at % NU, "pv", k if at < NU else k - NK))
            for n in range(sh.tpc):
                at = sh.last_unit(k) + LAG + 2 + n
                items.append((at % NU, "proj", k * sh.tpc + n if at < NU else (k - NK) * sh.tpc + n))
        items.sort(key=lambda x: x[0])
        assert len(items) % 2 == 0

        def skipped(item, first, last):
            return (first and item[2] < 0) or (last and item[1] in side.for_next)

        def place(item):
            return items.index(item)

        prologue = [it for it in items if it[1] in side.for_next]
        wrapped = [it for it in items if it[2] < 0]

        def last_in_bank(item, first, last, draining=False):
            at = len(items) if draining else place(item)
            seq = [(1, it) for it in (prologue if first else items)]
            if draining:
                seq = [(1, it) for it in items if not skipped(it, False, True)]
                seq += [(0, it) for it in wrapped[:wrapped.index(item)]]
            else:
                seq += [(0, it) for it in items[:at] if not skipped(it, first, last)]
            return next((x for x in reversed(seq) if place(x[1]) % 2 == place(item) % 2), None)

        def wait_bank(pe, i, before):
            if before is None:
                return
            back, (_, what, arg) = before
            if what == "pv":
                pe.wait_ge(head_out_ready, (i - back) * NK + arg + 1)
            elif what == "proj":
                pe.wait_ge(x_added, (i - back) * NT + arg + 1)
            else:
                pe.wait_ge(*side.read_out(i - back, what, arg))

        def run(engine, step, drain):
            for s in range(NU):
                step(0, s, True, False)
            with engine.Fori(1, turns - 1) as i:
                for s in range(NU):
                    step(i, s, False, False)
            for s in range(NU):
                step(turns - 1, s, False, True)
            drain(turns)

        block = ctx.enter_context(nc.Block())

        @block.tensor
        def _(pe):
            side.tensor_setup(pe)

            def scores(i, s, first):
                b, t, h = sh.units[s]
                side.tensor_scores_wait(pe, i, s)
                if not (first and s < 2):
                    pe.wait_ge(exp_done, i * NU + s - 1)
                n = (t + 1) * P
                for c0 in range(0, n, 512):
                    c1 = min(c0 + 512, n)
                    lhsT, rhs = side.score_operands(b, t, h, c0, c1)
                    pe.matmul(score[:, s % 2, c0:c1], lhsT, rhs, start=True, stop=(c1 < n))
                pe.matmul(score[:, s % 2, n - P:n], consts["ident_b"][:], consts["causal_b"][:],
                          start=False, stop=True).then_inc(scores_ready, 1)

            def transposes(i, u):
                uu = u % NU
                pe.wait_ge(prob_ready, i * NU + u + 1)
                for g in range(sh.first_group[uu], sh.first_group[uu + 1]):
                    _, j0, j1, _ = sh.groups[g]
                    gg = g if u >= 0 else g - NGR
                    by_act = sh.groups[g - 2][3]
                    if not (isinstance(i, int) and i == 0 and gg < 2):
                        pe.wait_ge(read_act if by_act else read_dve,
                                   i * sh.evacuated(NGR, by_act) + sh.evacuated(gg - 1, by_act))
                    for j in range(j0, j1):
                        last = pe.transpose(turned[:, g % 2, j - j0, :], prob[:, uu % RING_P, j * P:(j + 1) * P],
                                            ident[:])
                    last.then_inc(turned_ready, 1)

            def pv(i, k, bank):
                kk = k % NK
                b, c = divmod(kk, sh.chunks_per_batch)
                end = sh.first_group[sh.last_unit(kk) + 1] - (0 if k >= 0 else NGR)
                pe.wait_ge(read_act, i * sh.evacuated(NGR, True) + sh.evacuated(end, True))
                pe.wait_ge(read_dve, i * sh.evacuated(NGR, False) + sh.evacuated(end, False))
                side.tensor_pv_wait(pe, i, k)
                jn = (c + 1) * sh.tpc
                for j in range(jn):
                    q0 = max(0, j - c * sh.tpc) * P
                    for h in range(sh.heads):
                        last = pe.matmul(misc[h * M:(h + 1) * M, bank, q0:CW], side.value_operand(b, j, h),
                                         probT[:, kk % 2, h, j, q0:CW], start=(j == 0), stop=(j == jn - 1),
                                         skip_group_check=True)
                last.then_inc(pv_ready, 1)

            def proj(i, n, bank):
                k, tt = divmod(n, sh.tpc)
                pe.wait_ge(head_out_ready, i * NK + k + 1)
                side.tensor_proj_wait(pe, i, n)
                pe.matmul(misc[:, bank, :], head_out[:, k % 2, tt * P:(tt + 1) * P], side.out_w[:],
                          start=True, stop=True).then_inc(proj_ready, 1)

            def do(item, i, first, last):
                wait_bank(pe, i, last_in_bank(item, first, last))
                bank = place(item) % 2
                if item[1] == "pv":
                    pv(i, item[2], bank)
                elif item[1] == "proj":
                    proj(i, item[2], bank)
                else:
                    side.tensor_item(pe, i, item[1], item[2], bank)

            def step(i, s, first, last):
                scores(i, s, first)
                if s >= LAG or not first:
                    transposes(i, s - LAG)
                for item in items:
                    if item[0] == s and not skipped(item, first, last):
                        do(item, i, first, last)

            for n, item in enumerate(prologue):
                same = [(0, it) for it in prologue[:n] if place(it) % 2 == place(item) % 2]
                wait_bank(pe, -1, same[-1] if same else None)
                side.tensor_item(pe, -1, item[1], item[2], place(item) % 2)

            def drain(end):
                for s in range(LAG + 2 + sh.tpc):
                    if s < LAG:
                        transposes(end, s - LAG)
                    for item in wrapped:
                        if item[0] == s:
                            wait_bank(pe, end, last_in_bank(item, False, False, draining=True))
                            (pv if item[1] == "pv" else proj)(end, item[2], place(item) % 2)

            run(pe, step, drain)

        def read_out(eng, copy, i, u, by_act):
            uu = u % NU
            k = sh.chunk_of(uu)
            _, t, h = sh.units[uu]
            for g in range(sh.first_group[uu], sh.first_group[uu + 1]):
                _, j0, j1, act_has = sh.groups[g]
                if act_has != by_act:
                    continue
                gg = g if u >= 0 else g - NGR
                kk = k if u >= 0 else k - NK
                eng.wait_ge(turned_ready, i * NGR + gg + 1)
                if not (isinstance(i, int) and i == 0 and kk < 2):
                    eng.wait_ge(pv_ready, i * NK + kk - 1)
                q0 = (t % sh.tpc) * P
                copy(probT[:, k % 2, h, j0:j1, q0:q0 + P],
                     turned[:, g % 2, 0:j1 - j0, :]).then_inc(read_act if by_act else read_dve, 1)

        @block.vector
        def _(dve):
            side.vector_setup(dve)

            def evacuate(i, u):
                read_out(dve, dve.tensor_copy, i, u, False)

            def step(i, s, first, last):
                b, t, h = sh.units[s]
                n = (t + 1) * P
                dve.wait_ge(scores_ready, i * NU + s + 1)
                dve.reduce_max(negmax[:, s % RING_P:s % RING_P + 1], score[:, s % 2, 0:n], AX,
                               negate=True).then_inc(negmax_ready, 1)
                if s >= 1 or not first:
                    recip(i, s - 1)
                if s >= LAG or not first:
                    evacuate(i, s - LAG)
                for item in items:
                    if item[0] == s and not skipped(item, first, last):
                        if item[1] == "proj":
                            add(i, item)
                        else:
                            side.vector_item(dve, i, item[1], item[2], place(item) % 2)

            def recip(i, u):
                dve.wait_ge(exp_done, i * NU + u + 1)
                r = u % RING_P
                dve.reciprocal(rinv[:, r:r + 1], rowsum[:, r:r + 1]).then_inc(rinv_ready, 1)

            def add(i, item):
                n = item[2]
                tile = X[:, n % NT, :]
                dve.wait_ge(proj_ready, i * NT + n + 1)
                if not (isinstance(i, int) and i * NT + n == 0):
                    dve.wait_ge(x_added, i * NT + n)
                bank = place(item) % 2
                dve.tensor_tensor(tile, tile, misc[:, bank, :], ALU.add).then_inc(x_added, 1)

            for item in prologue:
                side.vector_item(dve, -1, item[1], item[2], place(item) % 2)

            def drain(end):
                for s in range(LAG + 2 + sh.tpc):
                    if s == 0:
                        recip(end, -1)
                    if s < LAG:
                        evacuate(end, s - LAG)
                    for item in wrapped:
                        if item[0] == s and item[1] == "proj":
                            add(end, item)

            run(dve, step, drain)

        @block.scalar
        def _(act):
            side.scalar_setup(act)

            def head_copy(i, item):
                k = item[2]
                bank = place(item) % 2
                act.wait_ge(pv_ready, i * NK + k + 1)
                if not (isinstance(i, int) and i == 0 and k < 2):
                    act.wait_ge(proj_ready, i * NT + (k - 1) * sh.tpc)
                act.copy(head_out[:, k % 2, :], misc[:, bank, 0:CW]).then_inc(head_out_ready, 1)

            def step(i, s, first, last):
                b, t, h = sh.units[s]
                n = (t + 1) * P
                r = s % RING_P
                act.wait_ge(negmax_ready, i * NU + s + 1)
                if not (first and s < RING_P):
                    act.wait_ge(turned_ready, i * NGR + turned_by(s - RING_P))
                act.activation(prob[:, r, 0:n], score[:, s % 2, 0:n], ACT.Exp, bias=negmax[:, r:r + 1],
                               accum_out=rowsum[:, r:r + 1]).then_inc(exp_done, 1)
                if s >= LAG or not first:
                    read_out(act, act.copy, i, s - LAG, True)
                for item in items:
                    if item[0] == s and not skipped(item, first, last):
                        if item[1] == "pv":
                            head_copy(i, item)
                        else:
                            side.scalar_item(act, i, item[1], item[2], place(item) % 2)

            def turned_by(u):
                return sh.first_group[u % NU + 1] - (0 if u >= 0 else NGR)

            for item in prologue:
                side.scalar_item(act, -1, item[1], item[2], place(item) % 2)

            def drain(end):
                for s in range(LAG + 2 + sh.tpc):
                    if s < LAG:
                        read_out(act, act.copy, end, s - LAG, True)
                    for item in wrapped:
                        if item[0] == s and item[1] == "pv":
                            head_copy(end, item)

            run(act, step, drain)

        @block.gpsimd
        def _(pool):
            side.gpsimd_setup(pool)

            def normalise(i, u):
                uu = u % NU
                n = (sh.units[uu][1] + 1) * P
                r = uu % RING_P
                pool.wait_ge(rinv_ready, i * NU + u + 1)
                pool.sem_inc(units_begun, 1)
                pool.tensor_scalar(prob[:, r, 0:n], prob[:, r, 0:n], rinv[:, r:r + 1], 1.0,
                                   ALU.mult, ALU.mult).then_inc(prob_ready, 1)

            def step(i, s, first, last):
                if s >= 1 or not first:
                    normalise(i, s - 1)
                for item in items:
                    if item[0] == s and not skipped(item, first, last):
                        side.gpsimd_item(pool, i, item[1], item[2])
                side.gpsimd_step(pool, i, s, first, last)

            for item in prologue:
                side.gpsimd_item(pool, -1, item[1], item[2])

            run(pool, step, lambda end: normalise(end, -1))

        @block.sync
        def _(sp):
            side.loads(sp, turns)


class LatentSide:

    for_next = ("nopeT", "fold_q", "rope0", "lat0")
    items = [(1, "rope", 2), (2, "lat", 2), (3, "rope", 3), (4, "lat", 3), (9, "fold_v", 0),
             (9, "nopeT", 0), (10, "nopeT", 1), (16, "fold_q", 0),
             (18, "rope0", 0), (20, "lat0", 0), (22, "rope0", 1), (24, "lat0", 1)]

    def __init__(self, nc, io, consts, kt):
        self.nc, self.io, self.consts, self.kt = nc, io, consts, kt

    def allocate(self, sb, sem, misc, scores_ready, pv_ready, proj_ready):
        self.misc, self.scores_ready = misc, scores_ready
        self.proj_ready = proj_ready
        self.q = sb("q", [P, 2, T])
        self.w_nope = sb("w_nope", [QC, 2, 2 * DN])
        self.w_rope = sb("w_rope", [QC, 2, P])
        self.wuk = sb("wuk", [P, 2, KVL])
        self.wuv = sb("wuv", [P, 2, KVL])
        self.wo = sb("wo", [P, 2, D])
        self.nopeT = sb("nopeT", [P, 2, 2, QC])
        self.w_lat = sb("w_lat", [QC, 2, P])
        self.out_w = sb("out_w", [P, D])
        self.cosq = sb("cosq", [P, S])
        self.sinq = sb("sinq", [P, S])
        self.partner = sb("partner", [P, 512])
        self.cosine = sb("cosine", [P, 512])
        self.tables = sem("tables")
        self.n_loaded, self.r_loaded, self.v_loaded = sem("n_loaded"), sem("r_loaded"), sem("v_loaded")
        self.nopeT_ready, self.nopeT_read = sem("nopeT_ready"), sem("nopeT_read")
        self.fold_q_ready, self.w_lat_ready = sem("fold_q_ready"), sem("w_lat_ready")
        self.fold_v_ready, self.out_w_ready = sem("fold_v_ready"), sem("out_w_ready")
        self.rope_ready, self.lat_ready = sem("rope_ready"), sem("lat_ready")
        self.partner_ready, self.cosine_ready = sem("partner_ready"), sem("cosine_ready")
        self.sine_done, self.q_rope_done, self.q_lat_done = sem("sine_done"), sem("q_rope_done"), sem("q_lat_done")

    @staticmethod
    def chunk(i, what, c):
        return (i + 1, c) if what.endswith("0") else (i, c)

    def read_out(self, i, what, c):
        if what == "nopeT":
            return self.nopeT_read, 2 * (i + 1) + c + 1
        if what == "fold_q":
            return self.w_lat_ready, i + 2
        if what == "fold_v":
            return self.out_w_ready, i + 1
        pair, c = self.chunk(i, what, c)
        if what.startswith("rope"):
            return self.partner_ready, 4 * pair + c + 1
        return self.q_lat_done, 8 * pair + 2 * c + 2

    def loads(self, sp, turns):
        io = self.io

        def load_n(pair):
            sp.dma_start(self.w_nope[:], io["w_q_up_nope"].rearrange("(k p) n -> p k n", p=QC)
                         [:, :, bass.ds(pair * 2 * DN, 2 * DN)]).then_inc(self.n_loaded, 16)
            sp.dma_start(self.wuk[:], io["w_uk"][bass.ds(pair * 2 * DN, 2 * DN), :]
                         .rearrange("(h p) r -> p h r", p=P)).then_inc(self.n_loaded, 16)

        def load_r(pair):
            src = io["w_q_up_rope"].rearrange("(k p) n -> p k n", p=QC)[:, :, bass.ds(pair * P, P)]
            src = src.rearrange("p k (h f q i) -> p k h f q i", h=2, f=2, q=2)
            dst = self.w_rope[:].rearrange("p k (h q f i) -> p k h q f i", h=2, f=2, q=2)
            for h in range(2):
                for f in range(2):
                    for q in range(2):
                        sp.dma_start(dst[:, :, h, q, f, :], src[:, :, h, f, q, :]).then_inc(self.r_loaded, 16)

        def load_v(pair):
            sp.dma_start(self.wuv[:], io["w_uv"][bass.ds(pair * 2 * DV, 2 * DV), :]
                         .rearrange("(h p) r -> p h r", p=P)).then_inc(self.v_loaded, 16)
            sp.dma_start(self.wo[:], io["w_out"][bass.ds(pair * 2 * DV, 2 * DV), :]
                         .rearrange("(h p) r -> p h r", p=P)).then_inc(self.v_loaded, 16)

        load_n(0)
        load_r(0)
        sp.dma_start(self.cosq[:], io["cos_rows"]).then_inc(self.tables, 16)
        sp.dma_start(self.sinq[:], io["sin_rows"]).then_inc(self.tables, 16)
        load_v(0)
        with sp.Fori(0, turns - 1) as i:
            sp.wait_ge(self.fold_q_ready, i + 1)
            load_n(i + 1)
            sp.wait_ge(self.rope_ready, 4 * i + 4)
            load_r(i + 1)
            sp.wait_ge(self.fold_v_ready, i + 1)
            load_v(i + 1)

    def tensor_setup(self, pe):
        pass

    def vector_setup(self, dve):
        pass

    def scalar_setup(self, act):
        pass

    def gpsimd_setup(self, pool):
        pass

    def gpsimd_step(self, pool, i, s, first, last):
        pass

    def tensor_scores_wait(self, pe, i, s):
        if s % 8 == 0:
            pe.wait_ge(self.q_rope_done, 8 * i + 2 * (s // 8) + 2)
            pe.wait_ge(self.q_lat_done, 8 * i + 2 * (s // 8) + 2)

    def score_operands(self, b, t, h, c0, c1):
        keys = self.kt["k_rl"] if h == 0 else self.kt["k_lr"]
        return self.q[:, h, b * S + t * P:b * S + (t + 1) * P], keys[:, b * S + c0:b * S + c1]

    def tensor_pv_wait(self, pe, i, k):
        pass

    def value_operand(self, b, j, h):
        return self.kt["ktok"][:, b * TB + j, DR:P]

    def tensor_proj_wait(self, pe, i, n):
        if n == 0:
            pe.wait_ge(self.out_w_ready, i + 1)

    def tensor_item(self, pe, i, what, c, bank):
        misc = self.misc
        if what == "nopeT":
            pe.wait_ge(self.n_loaded, 32 * (i + 1) + 32)
            for k in range(2):
                last = pe.transpose(misc[:, bank, k * QC:(k + 1) * QC], self.w_nope[:, k, c * DN:(c + 1) * DN],
                                    self.consts["ident"][0:QC, 0:QC])
            last.then_inc(self.nopeT_ready, 1)
        elif what == "fold_q":
            pe.wait_ge(self.nopeT_read, 2 * (i + 1) + 2)
            for k in range(2):
                for h in range(2):
                    at = k * P + (1 - h) * KVL
                    last = pe.matmul(misc[0:QC, bank, at:at + KVL], self.nopeT[:, h, k, :], self.wuk[:, h, :],
                                     start=True, stop=True)
            last.then_inc(self.fold_q_ready, 1)
        elif what == "fold_v":
            pe.wait_ge(self.v_loaded, 32 * i + 32)
            for h in range(2):
                last = pe.matmul(misc[h * KVL:(h + 1) * KVL, bank, :], self.wuv[:, h, :], self.wo[:, h, :],
                                 start=True, stop=True, skip_group_check=True)
            last.then_inc(self.fold_v_ready, 1)
        else:
            pair, c = self.chunk(i, what, c)
            rope = what.startswith("rope")
            if rope:
                pe.wait_ge(self.r_loaded, 128 * pair + 128)
            else:
                pe.wait_ge(self.w_lat_ready, pair + 1)
            w = self.w_rope if rope else self.w_lat
            for k in range(2):
                last = pe.matmul(misc[:, bank, :], w[:, k, :], self.kt["cq"][:, k, c * 512:(c + 1) * 512],
                                 start=(k == 0), stop=(k == 1))
            last.then_inc(self.rope_ready if rope else self.lat_ready, 1)

    def vector_item(self, dve, i, what, c, bank):
        if not what.startswith("rope"):
            return
        pair, c = self.chunk(i, what, c)
        n = pair * 4 + c
        first = isinstance(n, int) and n == 0
        if first:
            dve.wait_ge(self.tables, 32)
        else:
            dve.wait_ge(self.q_rope_done, 2 * n)
        dve.wait_ge(self.rope_ready, n + 1)
        cc = c % 2
        dve.tensor_tensor(self.cosine[:], self.misc[:, bank, :], self.cosq[:, cc * 512:(cc + 1) * 512], ALU.mult)\
           .then_inc(self.cosine_ready, 1)
        dve.stream_shuffle(self.partner[:], self.misc[:, bank, :], [(r + 16) % 32 for r in range(32)])\
           .then_inc(self.partner_ready, 1)

    def gpsimd_item(self, pool, i, what, c):
        if not what.startswith("rope"):
            return
        pair, c = self.chunk(i, what, c)
        n = pair * 4 + c
        cc = c % 2
        pool.wait_ge(self.partner_ready, n + 1)
        if isinstance(n, int) and n == 0:
            pool.wait_ge(self.tables, 32)
        pool.tensor_tensor(self.partner[:], self.partner[:], self.sinq[:, cc * 512:(cc + 1) * 512], ALU.mult)\
            .then_inc(self.sine_done, 1)
        pool.wait_ge(self.sine_done, n + 1)
        pool.wait_ge(self.cosine_ready, n + 1)
        self.wait_q_free(pool, pair, c)
        for h in range(2):
            rows = slice(h * DR, (h + 1) * DR)
            pool.tensor_tensor(self.q[rows, h, c * 512:(c + 1) * 512], self.cosine[rows, :], self.partner[rows, :],
                               ALU.add).then_inc(self.q_rope_done, 1)
        pool.wait_ge(self.q_rope_done, 2 * n + 2)

    def wait_q_free(self, eng, pair, c):
        if not (isinstance(pair, int) and pair == 0):
            eng.wait_ge(self.scores_ready, pair * 32 - 32 + 16 * (c // 2) + 16)

    def scalar_item(self, act, i, what, c, bank):
        misc = self.misc
        if what == "nopeT":
            n = (i + 1) * 2 + c
            act.wait_ge(self.nopeT_ready, n + 1)
            if not (isinstance(i, int) and i == -1):
                act.wait_ge(self.fold_q_ready, i + 1)
            act.copy(self.nopeT[:, c].rearrange("p k n -> p (k n)"), misc[:, bank, 0:2 * QC]).then_inc(
                self.nopeT_read, 1)
        elif what == "fold_q":
            act.wait_ge(self.fold_q_ready, i + 2)
            if not (isinstance(i, int) and i == -1):
                act.wait_ge(self.lat_ready, 4 * i + 4)
            act.copy(self.w_lat[:], misc[0:QC, bank, 0:2 * P].rearrange("p (k n) -> p k n", k=2)).then_inc(
                self.w_lat_ready, 1)
        elif what == "fold_v":
            act.wait_ge(self.fold_v_ready, i + 1)
            if not (isinstance(i, int) and i == 0):
                act.wait_ge(self.proj_ready, i * NT)
            act.copy(self.out_w[:], misc[:, bank, :]).then_inc(self.out_w_ready, 1)
        elif what.startswith("lat"):
            pair, c = self.chunk(i, what, c)
            n = pair * 4 + c
            act.wait_ge(self.lat_ready, n + 1)
            self.wait_q_free(act, pair, c)
            for h in range(2):
                rows = slice((1 - h) * KVL, (2 - h) * KVL)
                act.mul(self.q[rows, h, c * 512:(c + 1) * 512], misc[rows, bank, :], SCALE_A)\
                    .then_inc(self.q_lat_done, 1)


def latent_attention(nc, io, consts, kt):
    shape = Shape(2, 4, lambda n, u, j0, j1: n % 2 == 1)
    attention_loop(nc, consts, shape, "la", PAIRS, LatentSide(nc, io, consts, kt))


class GroupedSide:

    for_next = ()
    items = []

    def __init__(self, nc, io, consts, vtok, scratch):
        self.nc, self.io, self.consts, self.vtok, self.scratch = nc, io, consts, vtok, scratch

    def allocate(self, sb, sem, misc, scores_ready, pv_ready, proj_ready):
        self.scores_ready, self.pv_ready, self.proj_ready = scores_ready, pv_ready, proj_ready
        self.q = sb("q", [96, NB, REP, S], BF16)
        self.k = sb("k", [96, NB, S], BF16)
        self.v = sb("v", [P, NT, 32])
        self.out_w = sb("out_w", [P, D])
        self.qk_loaded = [sem("qk_loaded0"), sem("qk_loaded1")]
        self.w_loaded, self.zeroed, self.v_ready = sem("w_loaded"), sem("zeroed"), sem("v_ready")

    def loads(self, sp, turns):
        q3, k3 = self.scratch

        def load_qk(g, b):
            for n, (qp, kp) in enumerate(((0, 0), (0, 1), (0, 2), (1, 0), (1, 1), (2, 0))):
                rows = slice(n * HD, (n + 1) * HD)
                cols = slice(b * S, (b + 1) * S)
                sp.dma_start(self.q[rows, b], q3[qp, bass.ds(g * REP * HD, REP * HD), cols]
                             .rearrange("(h d) t -> d h t", d=HD)).then_inc(self.qk_loaded[b], 16)
                sp.dma_start(self.k[rows, b], k3[kp, bass.ds(b * G + g, 1)].rearrange("a d t -> (a d) t"))\
                    .then_inc(self.qk_loaded[b], 16)

        def load_w(g):
            for h in range(REP):
                sp.dma_start(self.out_w[32 * h:32 * h + HD, :],
                             self.io["b_Wo"][bass.ds(g * REP * HD + h * HD, HD), :]).then_inc(self.w_loaded, 16)

        load_qk(0, 0)
        load_qk(0, 1)
        sp.wait_ge(self.zeroed, 2)
        load_w(0)
        with sp.Fori(1, turns) as i:
            sp.wait_ge(self.scores_ready, (i - 1) * 64 + 32)
            load_qk(i, 0)
            sp.wait_ge(self.scores_ready, i * 64)
            load_qk(i, 1)
            sp.wait_ge(self.proj_ready, i * NT)
            load_w(i)

    def tensor_setup(self, pe):
        pass

    def vector_setup(self, dve):
        pass

    def scalar_setup(self, act):
        pass

    def copy_values(self, pool, g, b):
        pool.tensor_copy(self.v[:, b * TB:(b + 1) * TB, 0:HD],
                         self.vtok[:, bass.ds(b * G + g, 1)].rearrange("p a t d -> p (a t) d")).then_inc(self.v_ready, 1)

    def gpsimd_setup(self, pool):
        pool.memset(self.out_w[:], 0.0).then_inc(self.zeroed, 1)
        pool.memset(self.v[:], 0.0).then_inc(self.zeroed, 1)
        pool.wait_ge(self.zeroed, 2)
        self.copy_values(pool, 0, 0)

    def gpsimd_step(self, pool, i, s, first, last):
        if s == 8:
            if not first:
                pool.wait_ge(self.pv_ready, i * 8)
            self.copy_values(pool, i, 1)
        if s == 40 and not last:
            pool.wait_ge(self.pv_ready, i * 8 + 4)
            self.copy_values(pool, i + 1, 0)

    def tensor_scores_wait(self, pe, i, s):
        if s % 32 == 0:
            pe.wait_ge(self.qk_loaded[s // 32], 192 * i + 192)

    def score_operands(self, b, t, h, c0, c1):
        return self.q[:, b, h, t * P:(t + 1) * P], self.k[:, b, c0:c1]

    def tensor_pv_wait(self, pe, i, k):
        if k in (0, 4):
            pe.wait_ge(self.v_ready, 2 * i + 1 + k // 4)

    def value_operand(self, b, j, h):
        return self.v[:, b * TB + j, :]

    def tensor_proj_wait(self, pe, i, n):
        if n == 0:
            pe.wait_ge(self.w_loaded, 64 * i + 64)

    def vector_item(self, dve, i, what, c, bank):
        pass

    def gpsimd_item(self, pool, i, what, c):
        pass

    def scalar_item(self, act, i, what, c, bank):
        pass


def grouped_attention(nc, io, consts, vtok, scratch):
    shape = Shape(REP, 2, lambda n, u, j0, j1: n % 4 != 0)
    attention_loop(nc, consts, shape, "ga", G, GroupedSide(nc, io, consts, vtok, scratch))


def grouped_inputs(nc, io, consts, vtok, scratch):
    q3, k3 = scratch
    with ExitStack() as ctx:
        sb, ps, sem = scope(nc, ctx, "gi")
        norm = Norm(nc, ctx, "gi", consts["X"], consts["ident"])
        wq = sb("wq", [P, KD, D])
        wk = sb("wk", [P, KD, P])
        wv = sb("wv", [P, KD, P])
        bo = sb("bo", [P, D])
        parts = sb("parts", [P, 2, 3, 512], BF16)
        rest = sb("rest", [P, 2, 512])
        pv = ps("pv", [P, 2, 512])
        pq = ps("pq", [P, 4, 512])
        w_loaded, v_ready, v_read = sem("w_loaded"), sem("v_ready"), sem("v_read")
        q_ready, high_ready, rest_ready, mid_ready, low_ready = (
            sem("q_ready"), sem("high_ready"), sem("rest_ready"), sem("mid_ready"), sem("low_ready"))
        stored = [sem("stored_even"), sem("stored_odd")]
        bias_added = sem("bias_added")
        NQ = 5 * 4
        block = ctx.enter_context(nc.Block())

        @block.sync
        def _(sp):
            sp.dma_start(wq[:], io["b_Wq"].rearrange("(k p) n -> p k n", p=P)).then_inc(w_loaded, 16)
            wkv = io["b_Wkv"].rearrange("(k p) (g two d) -> p k g two d", p=P, two=2, d=HD)
            for k in range(KD):
                for n, w in enumerate((wk, wv)):
                    sp.dma_start(w[:, k, :].rearrange("p (g d) -> p g d", d=HD), wkv[:, k, :, n, :])\
                        .then_inc(w_loaded, 16)
            sp.dma_start(bo[:], io["b_bo"].partition_broadcast(P)).then_inc(w_loaded, 16)
            for n in range(NQ):
                c, m = divmod(n, 5)
                sp.wait_ge(low_ready, n + 1)
                cols = slice(c * 512, (c + 1) * 512)
                b, part = divmod(c, 2)
                for s in range(3):
                    dst = q3[s, m * P:(m + 1) * P, cols] if m < 4 else (
                        k3[s].rearrange("(g b) d t -> b g d t", b=NB)[b, :, :, part * 512:(part + 1) * 512])
                    sp.dma_start(dst, parts[:, n % 2, s]).then_inc(stored[n % 2], 16)
            for s in stored:
                sp.wait_ge(s, 48 * (NQ // 2))

        @block.vector
        def _(dve):
            norm.vector_stats(dve)

            def split(n):
                dve.wait_ge(high_ready, n + 1)
                if n >= 2:
                    dve.wait_ge(low_ready, n - 1)
                dve.scalar_tensor_tensor(rest[:, n % 2], pq[:, n % 4], 0.25 if n % 5 < 4 else 1.0,
                                         parts[:, n % 2, 0], ALU.mult, ALU.subtract).then_inc(rest_ready, 1)

            def values(t):
                dve.wait_ge(v_ready, t + 1)
                to = vtok[:].rearrange("p (g b) t d -> p b t g d", b=NB)[:, t // TB, t % TB]
                dve.tensor_copy(to, pv[:, t % 2, 0:P].rearrange("p (g d) -> p g d", d=HD)).then_inc(v_read, 1)

            dve.wait_ge(w_loaded, 160)
            for t in range(NT):
                norm.vector_h(dve, t)
                if t >= 2:
                    values(t - 2)
                if t % 4 == 1 and t > 4:
                    for m in range(5):
                        split((t // 4 - 1) * 5 + m)
            values(NT - 2)
            values(NT - 1)
            for m in range(5):
                split(15 + m)
            for t in range(NT):
                dve.wait_ge(norm.s_h, NT)
                dve.tensor_tensor(consts["X"][:, t, :], consts["X"][:, t, :], bo[:], ALU.add).then_inc(bias_added, 1)

        @block.scalar
        def _(act):
            norm.scalar_sqrt(act)

            def high(n):
                act.wait_ge(q_ready, n + 1)
                if n >= 2:
                    act.wait_ge(stored[n % 2], 48 * (n // 2))
                act.mul(parts[:, n % 2, 0], pq[:, n % 4], 0.25 if n % 5 < 4 else 1.0).then_inc(high_ready, 1)

            def mid(n):
                act.wait_ge(rest_ready, n + 1)
                act.copy(parts[:, n % 2, 1], rest[:, n % 2]).then_inc(mid_ready, 1)

            for t in range(NT):
                norm.scalar_hT(act, t)
                if t % 4 == 1 and t > 4:
                    for m in range(5):
                        n = (t // 4 - 1) * 5 + m
                        high(n)
                        mid(n)
            for n in range(15, 20):
                high(n)
                mid(n)

        @block.gpsimd
        def _(pool):
            for n in range(NQ):
                pool.wait_ge(mid_ready, n + 1)
                pool.tensor_tensor(parts[:, n % 2, 2], rest[:, n % 2], parts[:, n % 2, 1],
                                   ALU.subtract).then_inc(low_ready, 1)

        @block.tensor
        def _(pe):
            def values(t):
                pe.wait_ge(norm.s_hT, t + 1)
                if t >= 2:
                    pe.wait_ge(v_read, t - 1)
                for k in range(KD):
                    last = pe.matmul(pv[:, t % 2, 0:P], norm.hT[:, k, t * P:(t + 1) * P], wv[:, k, :],
                                     start=(k == 0), stop=(k == KD - 1))
                last.then_inc(v_ready, 1)

            def project(c):
                for m in range(5):
                    n = 5 * c + m
                    if n >= 4:
                        pe.wait_ge(rest_ready, n - 3)
                    for k in range(KD):
                        w = wq[:, k, m * P:(m + 1) * P] if m < 4 else wk[:, k, :]
                        last = pe.matmul(pq[:, n % 4, :], w, norm.hT[:, k, c * 512:(c + 1) * 512],
                                         start=(k == 0), stop=(k == KD - 1))
                    last.then_inc(q_ready, 1)

            pe.wait_ge(w_loaded, 160)
            for t in range(NT):
                norm.tensor_transpose(pe, t)
                if t >= 1:
                    values(t - 1)
                if t % 4 == 1 and t > 4:
                    project(t // 4 - 1)
            values(NT - 1)
            project(3)


def memory_weights(nc, io, consts, mem):
    ident = consts["ident"]
    with ExitStack() as ctx:
        sb, ps, sem = scope(nc, ctx, "mw")
        raw = {n: sb(n, s) for n, s in (("Wq", [BOT, D]), ("Wr", [RDIM, BOT]), ("keys", [P, BOT]), ("vals", [P, D]),
                                        ("Wvd", [VB, D]), ("Wvu", [P, KD, VB]), ("Wu1", [P, D]))}
        rhs = sb("rhs", [BOT, 2 * P])
        keysT = sb("keysT", [BOT, P])
        WrT = sb("WrT", [BOT, RDIM])
        rkT = sb("rkT", [RDIM, P])
        valsT = sb("valsT", [P, KD, P])
        WvdT = sb("WvdT", [P, KD, VB])
        WvuT = sb("WvuT", [VB, D])
        lowT = sb("lowT", [VB, P])
        bank = ps("bank", [P, 2, 512])
        loaded, made, read = sem("loaded"), sem("made"), sem("read")
        block = ctx.enter_context(nc.Block())
        NLOAD = 14

        @block.sync
        def _(sp):
            for to, of in ((raw["Wq"][:], io["f_Wq"]), (raw["Wr"][:], io["f_Wr"]), (raw["keys"][:], io["f_aux_keys"]),
                           (raw["vals"][:], io["f_aux_values"]), (raw["Wvd"][:], io["f_Wvd"]),
                           (raw["Wvu"][:], io["f_Wvu"].rearrange("(k p) v -> p k v", p=P)), (raw["Wu1"][:], io["f_Wu1"]),
                           (mem["logit_bias"][:, 0:P], io["f_log_rel"].partition_broadcast(P)),
                           (mem["logit_bias"][:, P:2 * P], io["f_log_rel"].partition_broadcast(P)),
                           (mem["logit_bias"][:, 2 * P:], io["f_bu1"].partition_broadcast(P)),
                           (mem["u2"][:], io["f_Wu2"].rearrange("a n -> (a n)").partition_broadcast(P)),
                           (mem["bu2"][:], io["f_bu2"].partition_broadcast(P)),
                           (mem["gw1"][:], io["f_gate_w1"].partition_broadcast(P)),
                           (mem["gbias"][:], io["f_gate_bias"].partition_broadcast(P))):
                sp.dma_start(to, of).then_inc(loaded, 16)

        def turned(dst, of, rows):
            return lambda pe, b: pe.transpose(bank[0:of.shape[-1], b, dst:dst + rows], of, ident[0:rows, 0:rows])

        def product(out, lhsT, rhs_, start=True, stop=True):
            return lambda pe, b: pe.matmul(out(b), lhsT, rhs_, start=start, stop=stop)

        stages = [
            ([turned(0, raw["keys"][:], P), turned(P, raw["Wr"][:], RDIM)],
             [(keysT[:], lambda b: bank[0:BOT, b, 0:P], 1.0), (WrT[:], lambda b: bank[0:BOT, b, P:P + RDIM], 1.0),
              (rhs[:, P:], lambda b: bank[0:BOT, b, 0:P], float(1.0 / np.sqrt(BOT)))]),
            ([turned(k * P, raw["vals"][:, k * P:(k + 1) * P], P) for k in range(KD)],
             [(valsT[:], lambda b: bank[:, b, :].rearrange("p (k n) -> p k n", k=KD), 1.0)]),
            ([turned(k * VB, raw["Wvd"][:, k * P:(k + 1) * P], VB) for k in range(KD)],
             [(WvdT[:], lambda b: bank[:, b, 0:KD * VB].rearrange("p (k n) -> p k n", k=KD), 1.0)]),
            ([turned(k * P, raw["Wvu"][:, k, :], P) for k in range(KD)],
             [(WvuT[:], lambda b: bank[0:VB, b, :], 1.0)]),
            ([turned(k * P, raw["Wu1"][:, k * P:(k + 1) * P], P) for k in range(KD)],
             [(mem["logit_w"][:, :, 2 * P:], lambda b: bank[:, b, :].rearrange("p (k n) -> p k n", k=KD), 1.0)]),
            ([product(lambda b: bank[0:RDIM, b, 0:P], WrT[:], keysT[:])],
             [(rkT[:], lambda b: bank[0:RDIM, b, 0:P], 1.0)]),
            ([product(lambda b: bank[0:VB, b, 0:P], WvdT[:, k, :], valsT[:, k, :], k == 0, k == KD - 1)
              for k in range(KD)],
             [(lowT[:], lambda b: bank[0:VB, b, 0:P], 1.0)]),
            ([product(lambda b: bank[0:BOT, b, 0:P], raw["Wr"][:], rkT[:])],
             [(rhs[:, 0:P], lambda b: bank[0:BOT, b, 0:P], float(1.0 / np.sqrt(RDIM)))]),
            ([product(lambda b: bank[:, b, :], lowT[:], WvuT[:])],
             [(mem["value_w"][:], lambda b: bank[:, b, :], 1.0)]),
        ] + [
            ([product(lambda b, o=o: bank[:, b, o * 256:o * 256 + 256], raw["Wq"][:, k * P:(k + 1) * P], rhs[:])
              for o, k in enumerate((kk, kk + 1))],
             [(mem["logit_w"][:, kk:kk + 2, 0:2 * P],
               lambda b: bank[:, b, :].rearrange("p (k n) -> p k n", k=2), 1.0)])
            for kk in (0, 2)
        ]
        reads = [sum(len(st[1]) for st in stages[:n + 1]) for n in range(len(stages))]
        needs = {5: 0, 6: 2, 7: 5, 8: 6, 9: 7, 10: 7}

        @block.tensor
        def _(pe):
            pe.wait_ge(loaded, 16 * NLOAD)
            for n, (mms, _) in enumerate(stages):
                before = max(needs.get(n, 0), n - 2)
                if n >= 2:
                    pe.wait_ge(read, reads[before])
                for mm in mms:
                    last = mm(pe, n % 2)
                last.then_inc(made, 1)

        @block.vector
        def _(dve):
            for n, (_, outs) in enumerate(stages):
                dve.wait_ge(made, n + 1)
                for dst, src, scale in outs:
                    dve.tensor_scalar(dst, src(n % 2), scale, None, ALU.mult).then_inc(read, 1)


def memory_block(nc, io, consts, mem, tag, out):
    X, ident = consts["X"], consts["ident"]
    with ExitStack() as ctx:
        sb, ps, sem = scope(nc, ctx, tag)
        norm = Norm(nc, ctx, tag, X, ident)
        logits = sb("logits", [P, NT, 3 * P])
        top = sb("top", [P, NT, 8])
        rest = sb("rest", [P, 2, 4, P])
        chosen = sb("chosen", [P, 2, 4, P])
        negmax = sb("negmax", [P, NT])
        weight = sb("weight", [P, 2, 4, P])
        wsum = sb("wsum", [P, NT])
        weightT = sb("weightT", [P, T])
        small = sb("small", [P, 24, NT])
        gel = sb("gel", [P, 3, NT, UH])
        ones = sb("ones", [P, P])
        mean = sb("mean", [P, 2])
        gain = sb("gain", [P, NT])
        plog = ps("plog", [P, 2, 512])
        pturn = ps("pturn", [P, 512])
        pmean = ps("pmean", [P, 512])
        pout = ps("pout", [P, 2, 512])
        lg_ready, lg_read = sem("lg_ready"), sem("lg_read")
        top_ready, rest_ready, same_ready, chosen_ready, nm_ready = (
            sem("top_ready"), sem("rest_ready"), sem("same_ready"), sem("chosen_ready"), sem("nm_ready"))
        w_ready, wT_ready, wT_read = sem("w_ready"), sem("wT_ready"), sem("wT_read")
        ln_in, ln_done = sem("ln_in"), sem("ln_done")
        mean_in, mean_done, ones_ready = sem("mean_in"), sem("mean_done"), sem("ones_ready")
        tanh_in, tanh_done = sem("tanh_in"), sem("tanh_done")
        out_ready, x_ready, stored = sem("out_ready"), sem("x_ready"), sem("stored")
        gain_ready, normed_added = sem("gain_ready"), sem("normed_added")
        chain = sem("chain")
        block = ctx.enter_context(nc.Block())

        @block.vector
        def _(dve):
            linked = [0]

            def link(instruction):
                linked[0] += 1
                instruction.then_inc(chain, 1)
                dve.wait_ge(chain, linked[0])

            norm.vector_stats(dve)
            (v2, v3, u, ln, less, zero, num, den, rden, lv, me, nv, lsum, lrn, lt, un, un2, gz, gt, gate, ok, rs,
             sc, shift) = (small[:, n, :] for n in range(24))
            link(dve.tensor_tensor(v2, norm.mv[:, :, 1], norm.rstd[:], ALU.mult))
            link(dve.tensor_tensor(v3, v2, norm.rstd[:], ALU.mult))
            dve.tensor_scalar(u, v3, 1.0, None, ALU.add).then_inc(ln_in, 1)
            link(dve.tensor_tensor(shift, norm.mv[:, :, 0], norm.rstd[:], ALU.mult))
            link(dve.tensor_scalar(shift, shift, -1.0, None, ALU.mult))
            dve.tensor_scalar(gain[:], norm.rstd[:], 1.0, None, ALU.add).then_inc(gain_ready, 1)
            for t in range(2):
                norm.vector_h(dve, t)
            dve.wait_ge(ln_in, 1)
            link(dve.tensor_scalar(less, u, 1.0, None, ALU.subtract))
            link(dve.tensor_scalar(zero, less, 0.0, None, ALU.is_equal))
            link(dve.tensor_tensor(den, less, zero, ALU.add))
            link(dve.reciprocal(rden, den))
            dve.wait_ge(ln_done, 1)
            link(dve.tensor_tensor(num, ln, zero, ALU.add))
            link(dve.tensor_tensor(num, num, v3, ALU.mult))
            link(dve.tensor_tensor(lv, num, rden, ALU.mult))
            dve.reduce_sum(mean[:, 0:1], lv, AX).then_inc(mean_in, 1)

            def read_logits(t):
                dve.wait_ge(lg_ready, t + 1)
                dve.tensor_tensor(logits[:, t, :], plog[:, t % 2, 0:3 * P], mem["logit_bias"][:],
                                  ALU.add).then_inc(lg_read, 1)

            def choose(c):
                tiles = range(4 * c, 4 * c + 4)
                par = c % 2
                for t in tiles:
                    dve.wait_ge(lg_read, t + 1)
                    dve.max(top[:, t, :], logits[:, t, 0:P]).then_inc(top_ready, 1)
                for t in tiles:
                    dve.wait_ge(top_ready, t + 1)
                    dve.match_replace(rest[:, par, t % 4, :], top[:, t, :], logits[:, t, 0:P], -3.4e38)\
                        .then_inc(rest_ready, 1)
                dve.wait_ge(rest_ready, 4 * c + 4)
                if c >= 2:
                    dve.wait_ge(w_ready, 4 * c - 4)
                four = slice(4 * c, 4 * c + 4)
                dve.tensor_tensor(chosen[:, par], rest[:, par], logits[:, four, 0:P], ALU.is_equal)\
                    .then_inc(same_ready, 1)
                dve.wait_ge(same_ready, c + 1)
                dve.scalar_tensor_tensor(chosen[:, par], chosen[:, par], NEG, logits[:, four, P:2 * P],
                                         ALU.mult, ALU.add).then_inc(chosen_ready, 1)
                dve.wait_ge(chosen_ready, c + 1)
                dve.reduce_max(negmax[:, four], chosen[:, par], AX, negate=True).then_inc(nm_ready, 1)

            for t in range(2, NT):
                norm.vector_h(dve, t)
                read_logits(t - 2)
                if t % 4 == 2 and t > 2:
                    choose(t // 4 - 1)
            read_logits(NT - 2)
            read_logits(NT - 1)
            choose(3)

            hid = logits[:, :, 2 * P:3 * P]
            sq, z, th = gel[:, 0], gel[:, 1], gel[:, 2]
            link(dve.tensor_tensor(sq, hid, hid, ALU.mult))
            link(dve.tensor_scalar(sq, sq, 0.044715, 1.0, ALU.mult, ALU.add))
            dve.tensor_tensor(z, sq, hid, ALU.mult).then_inc(tanh_in, 1)
            dve.wait_ge(mean_done, 1)
            link(dve.tensor_scalar(me[:, 0:1], pmean[:, 0:1], 1e-6, None, ALU.add))
            link(dve.reciprocal(mean[:, 1:2], me[:, 0:1]))
            link(dve.tensor_scalar(nv, lv, mean[:, 1:2], 0.5, ALU.mult, ALU.mult))
            dve.wait_ge(tanh_done, 1)
            link(dve.scalar_tensor_tensor(sq, th, 1.0, hid, ALU.add, ALU.mult))
            link(dve.tensor_tensor(z, sq, mem["u2"][:].unsqueeze(1).broadcast_to([P, NT, UH]), ALU.mult))
            link(dve.reduce_sum(lsum, z, AX))
            dve.tensor_scalar(lrn, lsum, 0.5, mem["bu2"][:, 0:1], ALU.mult, ALU.add).then_inc(tanh_in, 1)
            dve.wait_ge(tanh_done, 2)
            link(dve.tensor_scalar(un, lt, 1.25, 1.25, ALU.mult, ALU.add))
            link(dve.tensor_tensor(un, un, nv, ALU.add))
            link(dve.tensor_scalar(un, un, 0.0, 5.0, ALU.max, ALU.min))
            link(dve.tensor_scalar(un, un, 0.5, 1.0 / 1.5, ALU.subtract, ALU.mult))
            link(dve.tensor_scalar(un2, un, 0.0, 1.0, ALU.max, ALU.min))
            dve.tensor_scalar(gz, un2, mem["gw1"][:, 0:1], mem["gbias"][:, 0:1], ALU.mult, ALU.add)\
                .then_inc(tanh_in, 1)
            dve.wait_ge(tanh_done, 3)
            link(dve.tensor_scalar(gate, gt, 0.5, 0.5, ALU.mult, ALU.add))
            link(dve.tensor_scalar(ok, gate, 0.05, None, ALU.is_ge))
            link(dve.tensor_tensor(gate, gate, ok, ALU.mult))
            dve.wait_ge(w_ready, NT)
            link(dve.reciprocal(rs, wsum[:]))
            link(dve.tensor_tensor(sc, gate, rs, ALU.mult))
            for t in range(NT):
                dve.wait_ge(out_ready, t + 1)
                dve.wait_ge(normed_added, t + 1)
                dve.scalar_tensor_tensor(X[:, t, :], pout[:, t % 2, :], sc[:, t:t + 1], X[:, t, :],
                                         ALU.mult, ALU.add).then_inc(x_ready, 1)

        @block.scalar
        def _(act):
            norm.scalar_sqrt(act)
            act.wait_ge(ln_in, 1)
            act.activation(small[:, 3, :], small[:, 2, :], ACT.Ln).then_inc(ln_done, 1)

            def weights(c):
                for t in range(4 * c, 4 * c + 4):
                    act.wait_ge(nm_ready, c + 1)
                    if c >= 2:
                        act.wait_ge(wT_ready, c - 1)
                    act.activation(weight[:, c % 2, t % 4, :], chosen[:, c % 2, t % 4, :], ACT.Exp,
                                   bias=negmax[:, t:t + 1], accum_out=wsum[:, t:t + 1]).then_inc(w_ready, 1)

            def read_turned(c):
                act.wait_ge(wT_ready, c + 1)
                act.copy(weightT[:, c * 512:(c + 1) * 512], pturn[:]).then_inc(wT_read, 1)

            for t in range(NT):
                norm.scalar_hT(act, t)
                if t % 4 == 3 and t > 4:
                    weights(t // 4 - 1)
                if t % 4 == 1 and t > 8:
                    read_turned(t // 4 - 2)
            read_turned(2)
            weights(3)
            read_turned(3)
            act.wait_ge(tanh_in, 1)
            act.activation(gel[:, 2], gel[:, 1], ACT.Tanh, scale=float(np.sqrt(2.0 / np.pi))).then_inc(tanh_done, 1)
            act.wait_ge(tanh_in, 2)
            act.activation(small[:, 14, :], small[:, 13, :], ACT.Tanh, scale=0.5).then_inc(tanh_done, 1)
            act.wait_ge(tanh_in, 3)
            act.activation(small[:, 18, :], small[:, 17, :], ACT.Tanh, scale=0.5).then_inc(tanh_done, 1)

        @block.gpsimd
        def _(pool):
            pool.memset(ones[:], 1.0 / T).then_inc(ones_ready, 1)
            pool.wait_ge(gain_ready, 1)
            for t in range(NT):
                pool.wait_ge(norm.s_h, t + 1)
                pool.tensor_scalar(X[:, t, :], X[:, t, :], gain[:, t:t + 1], small[:, 23, t:t + 1],
                                   ALU.mult, ALU.add).then_inc(normed_added, 1)

        @block.tensor
        def _(pe):
            def logit(t):
                pe.wait_ge(norm.s_hT, t + 1)
                if t >= 2:
                    pe.wait_ge(lg_read, t - 1)
                for k in range(KD):
                    last = pe.matmul(plog[:, t % 2, 0:3 * P], norm.hT[:, k, t * P:(t + 1) * P],
                                     mem["logit_w"][:, k, :], start=(k == 0), stop=(k == KD - 1))
                last.then_inc(lg_ready, 1)

            def turn(c):
                pe.wait_ge(w_ready, 4 * c + 4)
                if c >= 1:
                    pe.wait_ge(wT_read, c)
                for j in range(4):
                    last = pe.transpose(pturn[:, j * P:(j + 1) * P], weight[:, c % 2, j, :], ident[:])
                last.then_inc(wT_ready, 1)

            for t in range(NT):
                norm.tensor_transpose(pe, t)
                if t >= 1:
                    logit(t - 1)
                if t % 4 == 0 and t >= 8:
                    turn(t // 4 - 2)
            logit(NT - 1)
            pe.wait_ge(ones_ready, 1)
            pe.wait_ge(mean_in, 1)
            pe.matmul(pmean[:, 0:1], ones[:], mean[:, 0:1], start=True, stop=True).then_inc(mean_done, 1)
            turn(2)
            turn(3)
            for t in range(NT):
                pe.wait_ge(wT_read, t // 4 + 1)
                if t >= 2:
                    pe.wait_ge(x_ready, t - 1)
                pe.matmul(pout[:, t % 2, :], weightT[:, t * P:(t + 1) * P], mem["value_w"][:],
                          start=True, stop=True).then_inc(out_ready, 1)

        @block.sync
        def _(sp):
            if out is not None:
                o = out.rearrange("b (t p) d -> p (b t) d", p=P)
                for c in range(4):
                    sp.wait_ge(x_ready, 4 * c + 4)
                    sp.dma_start(o[:, 4 * c:4 * c + 4, :], X[:, 4 * c:4 * c + 4, :]).then_inc(stored, 16)
                sp.wait_ge(stored, 64)


_NAMES = {"L0_attn_a_hidden_states": "x", "L0_attn_a_w_q_down": "w_q_down", "L0_attn_a_w_q_up_nope": "w_q_up_nope",
          "L0_attn_a_w_q_up_rope": "w_q_up_rope", "L0_attn_a_w_kv_down": "w_kv_down",
          "L0_attn_a_w_k_rope": "w_k_rope", "L0_attn_a_w_uk": "w_uk", "L0_attn_a_w_uv": "w_uv",
          "L0_attn_a_w_out": "w_out", "L0_attn_b_Wq": "b_Wq", "L0_attn_b_Wkv": "b_Wkv", "L0_attn_b_Wo": "b_Wo",
          "L0_attn_b_bo": "b_bo", "L0_ffn_Wq": "f_Wq", "L0_ffn_Wr": "f_Wr", "L0_ffn_aux_keys": "f_aux_keys",
          "L0_ffn_aux_values": "f_aux_values", "L0_ffn_Wvd": "f_Wvd", "L0_ffn_Wvu": "f_Wvu", "L0_ffn_Wu1": "f_Wu1",
          "L0_ffn_bu1": "f_bu1", "L0_ffn_Wu2": "f_Wu2", "L0_ffn_bu2": "f_bu2", "L0_ffn_gate_w1": "f_gate_w1",
          "L0_ffn_gate_bias": "f_gate_bias", "L0_ffn_log_rel": "f_log_rel"}


def _tables():
    f = np.float32
    freqs = f(1.0) / np.power(f(10000.0), np.arange(0, DR, 2, dtype=f) / f(DR))
    wavelengths = f(2.0 * np.pi) / freqs
    ramp = np.clip((wavelengths / f(4096.0) - f(1.0)) / f(31.0), f(0), f(1)).astype(f)
    inv_freq = (freqs / (f(1.0) - ramp + ramp * f(40.0))).astype(f)
    angle = (np.arange(S, dtype=f)[:, None] * inv_freq[None, :]).astype(f)
    cos, sin = np.cos(angle).astype(f), np.sin(angle).astype(f)
    tok = lambda a: np.ascontiguousarray(np.tile(a.reshape(TB, P, 32).transpose(1, 0, 2), (1, NB, 1)))
    scaled = f(SCALE_A)

    def rows(low, high):
        quads = [part[:, 16 * q:16 * q + 16].T for q in range(2) for part in (low, high)]
        return np.ascontiguousarray(np.concatenate(quads * 2, axis=0) * scaled)

    i = np.arange(P)
    return {"identity": np.eye(P, dtype=f), "causal": np.where(i[None, :] > i[:, None], f(NEG), f(0)).astype(f),
            "cos_tok": tok(cos), "sin_tok": tok(sin), "cos_rows": rows(cos, cos), "sin_rows": rows(-sin, sin)}


def kernel(**inputs):
    import numpy as _np
    import concourse.bacc as _bacc
    from concourse import mybir as _mybir
    from concourse.bass_utils import run_bass_kernel_spmd as _run

    nc = _bacc.Bacc("TRN2", target_bir_lowering=False, num_devices=1)
    arrays, io = {}, {}
    given = {short: _np.atleast_1d(_np.ascontiguousarray(inputs[name])) for name, short in _NAMES.items()}
    for short, a in {**given, **_tables()}.items():
        arrays[f"in_{short}"] = a
        io[short] = nc.dram_tensor(f"in_{short}", a.shape, _mybir.dt.from_np(a.dtype), kind="ExternalInput").ap()
    io["out"] = nc.dram_tensor("out_dram", (NB, S, D), _mybir.dt.float32, kind="ExternalOutput").ap()
    build(nc, io)
    r = _run(nc, [arrays], core_ids=[0])
    return r.results[0]["out_dram"]
```

```python
from contextlib import ExitStack

import numpy as np

import concourse.bass as bass
from concourse import mybir

F32 = mybir.dt.float32
BF16 = mybir.dt.bfloat16
ALU = mybir.AluOpType
ACT = mybir.ActivationFunctionType
AX = mybir.AxisListType.X

P = 128
D = 512
KD = D // P
NB = 2
S = 1024
T = NB * S
NT = T // P
TB = S // P
EPS = 1e-5
NEG = -1e30

H = 32
QL = 192
QC = QL // 2
KVL = 64
DN = 128
DR = 64
DV = 128
PAIRS = H // 2
SCALE_A = float(1.0 / np.sqrt(np.float32(DN + DR)))
G = 8
HD = 16
REP = H // G
BOT, RDIM, NSLOT, VB = 64, 48, 128, 32
UH = D // 4

RING_P = 4
LAG = 3


def groups_of(t):
    return [(0, t + 1)] if t < 4 else [(0, 4), (4, t + 1)]


class Shape:

    def __init__(self, heads, tiles_per_chunk, on_act):
        self.heads, self.tpc = heads, tiles_per_chunk
        self.units = [(b, t, h) for b in range(NB) for t in range(TB) for h in range(heads)]
        self.nu = len(self.units)
        self.chunks_per_batch = TB // tiles_per_chunk
        self.nchunk = NB * self.chunks_per_batch
        self.groups = []
        for u, (b, t, h) in enumerate(self.units):
            for j0, j1 in groups_of(t):
                self.groups.append((u, j0, j1, on_act(len(self.groups), u, j0, j1)))
        self.first_group = [next(n for n, g in enumerate(self.groups) if g[0] == u) for u in range(self.nu)]
        self.first_group.append(len(self.groups))
        assert len(self.groups) % 2 == 0

    def chunk_of(self, u):
        b, t, _ = self.units[u]
        return b * self.chunks_per_batch + t // self.tpc

    def last_unit(self, k):
        return (k + 1) * self.tpc * self.heads - 1

    def evacuated(self, n_groups, by_act):
        turn = sum(g[3] == by_act for g in self.groups)
        if n_groups < 0:
            return self.evacuated(n_groups + len(self.groups), by_act) - turn
        return sum(g[3] == by_act for g in self.groups[:n_groups])


def build(nc, io):
    top = ExitStack()
    with top:
        def keep(name, shape, dt=F32):
            return top.enter_context(nc.sbuf_tensor(name, shape, dt))

        X = keep("X", [P, NT, D])
        ident = keep("ident", [P, P])
        ident_b = keep("ident_b", [P, P], BF16)
        causal_b = keep("causal_b", [P, P], BF16)
        consts = dict(X=X, ident=ident, ident_b=ident_b, causal_b=causal_b)
        with ExitStack() as latent:
            kt = {n: latent.enter_context(nc.sbuf_tensor(n, s, F32)) for n, s in (
                ("cq", [QC, 2, T]), ("k_rl", [P, T]), ("k_lr", [P, T]), ("ktok", [P, NT, 192]))}
            latent_inputs(nc, io, consts, kt)
            latent_attention(nc, io, consts, kt)
        mem = {n: keep(n, s) for n, s in (
            ("logit_w", [P, KD, 3 * P]), ("value_w", [P, D]), ("logit_bias", [P, 3 * P]),
            ("u2", [P, UH]), ("bu2", [P, 1]), ("gw1", [P, 1]), ("gbias", [P, 1]))}
        memory_weights(nc, io, consts, mem)
        memory_block(nc, io, consts, mem, "f1", None)
        with ExitStack() as grouped:
            vtok = grouped.enter_context(nc.sbuf_tensor("vtok", [P, NB * G, TB, HD], F32))
            scratch = (nc.dram_tensor("query_parts", (3, D, T), BF16).ap(),
                       nc.dram_tensor("key_parts", (3, NB * G, HD, S), BF16).ap(),
                       nc.dram_tensor("heads_out", (D, T), F32).ap())
            grouped_inputs(nc, io, consts, vtok, scratch)
            grouped_attention(nc, io, consts, vtok, scratch)
        memory_block(nc, io, consts, mem, "f2", io["out"])


def scope(nc, ctx, tag):
    def sb(name, shape, dt=F32):
        return ctx.enter_context(nc.sbuf_tensor(f"{tag}_{name}", shape, dt))

    def ps(name, shape, dt=F32):
        return ctx.enter_context(nc.psum_tensor(f"{tag}_{name}", shape, dt))

    held = []

    def clear():
        nc.clear_and_free_semaphores(held)
        nc.all_engine_barrier()

    ctx.callback(clear)

    def sem(name):
        held.append(nc.alloc_semaphore(f"{tag}_{name}"))
        return held[-1]

    return sb, ps, sem


class Norm:

    def __init__(self, nc, ctx, tag, X, ident):
        sb, ps, sem = scope(nc, ctx, tag)
        self.X, self.ident = X, ident
        self.stats = sb("ln_stats", [P, NT, 6])
        self.mv = sb("ln_mv", [P, NT, 2])
        self.ve = sb("ln_ve", [P, NT])
        self.sd = sb("ln_sd", [P, NT])
        self.rstd = sb("ln_rstd", [P, NT])
        self.h = sb("ln_h", [P, 2, D])
        self.hT = sb("hT", [P, KD, T])
        self.pt = ps("ln_pt", [P, 2, KD, P])
        self.s_stats = sem("ln_stats_ready")
        self.s_mv = sem("ln_mv_ready")
        self.s_ve = sem("ln_ve_ready")
        self.s_sd = sem("ln_sd_ready")
        self.s_rstd = sem("ln_rstd_ready")
        self.s_h = sem("ln_h_ready")
        self.s_tr = sem("ln_transposed")
        self.s_hT = sem("ln_hT_ready")

    def vector_stats(self, dve, x_loaded=None):
        for t in range(NT):
            if x_loaded is not None:
                dve.wait_ge(x_loaded[t // 4], 16)
            dve.bn_stats(self.stats[:, t, :], self.X[:, t, :]).then_inc(self.s_stats, 1)
        for t in range(NT):
            dve.wait_ge(self.s_stats, t + 1)
            dve.bn_aggr(self.mv[:, t, :], self.stats[:, t, :]).then_inc(self.s_mv, 1)
        dve.wait_ge(self.s_mv, NT)
        dve.tensor_scalar(self.ve[:], self.mv[:, :, 1], EPS, None, ALU.add).then_inc(self.s_ve, 1)
        dve.wait_ge(self.s_sd, 1)
        dve.reciprocal(self.rstd[:], self.sd[:]).then_inc(self.s_rstd, 1)
        dve.wait_ge(self.s_rstd, 1)

    def scalar_sqrt(self, act):
        act.wait_ge(self.s_ve, 1)
        act.activation(self.sd[:], self.ve[:], ACT.Sqrt).then_inc(self.s_sd, 1)

    def vector_h(self, dve, t):
        if t >= 2:
            dve.wait_ge(self.s_tr, t - 1)
        dve.tensor_scalar(self.h[:, t % 2, :], self.X[:, t, :], self.mv[:, t, 0:1], self.rstd[:, t:t + 1],
                          ALU.subtract, ALU.mult).then_inc(self.s_h, 1)

    def tensor_transpose(self, pe, t):
        pe.wait_ge(self.s_h, t + 1)
        if t >= 2:
            pe.wait_ge(self.s_hT, t - 1)
        for k in range(KD):
            last = pe.transpose(self.pt[:, t % 2, k, :], self.h[:, t % 2, k * P:(k + 1) * P], self.ident[:])
        last.then_inc(self.s_tr, 1)

    def scalar_hT(self, act, t):
        act.wait_ge(self.s_tr, t + 1)
        act.copy(self.hT[:, :, t * P:(t + 1) * P], self.pt[:, t % 2, :, :]).then_inc(self.s_hT, 1)


def latent_inputs(nc, io, consts, kt):
    X, ident = consts["X"], consts["ident"]
    with ExitStack() as ctx:
        sb, ps, sem = scope(nc, ctx, "li")
        norm = Norm(nc, ctx, "li", X, ident)
        wqd = sb("wqd", [P, KD, QL])
        wkv = sb("wkv", [P, KD, P])
        cosk = sb("cosk", [P, NT, 32])
        sink = sb("sink", [P, NT, 32])
        kv = sb("kv", [P, NT, P])
        tmp = sb("tmp", [P, 4, NT, 32])
        maskf = sb("maskf", [P, P])
        pkv = ps("pkv", [P, 2, 512])
        pcq = ps("pcq", [P, 2, 512])
        pk = ps("pk", [P, 2, 4, P])

        x_loaded = [sem(f"x_loaded{c}") for c in range(4)]
        const_loaded = sem("const_loaded")
        w_loaded = sem("w_loaded")
        table_loaded = sem("table_loaded")
        consts_cast = sem("consts_cast")
        kv_ready, kv_read = sem("kv_ready"), sem("kv_read")
        cq_ready, cq_read = sem("cq_ready"), sem("cq_read")
        prod_ready, rope_ready, lat_ready, dup_ready = (
            sem("prod_ready"), sem("rope_ready"), sem("lat_ready"), sem("dup_ready"))
        kT_ready, kT_read = sem("kT_ready"), [sem("kT_read_act"), sem("kT_read_dve")]

        x_in = io["x"].rearrange("b (t p) d -> p (b t) d", p=P)
        ktok = kt["ktok"]
        block = ctx.enter_context(nc.Block())

        @block.sync
        def _(sp):
            for c in range(4):
                sp.dma_start(X[:, 4 * c:4 * c + 4, :], x_in[:, 4 * c:4 * c + 4, :]).then_inc(x_loaded[c], 16)
            sp.dma_start(cosk[:], io["cos_tok"]).then_inc(table_loaded, 16)
            sp.dma_start(sink[:], io["sin_tok"]).then_inc(table_loaded, 16)

        @block.gpsimd
        def _(pool):
            pool.dma_start(ident[:], io["identity"]).then_inc(const_loaded, 16)
            pool.dma_start(maskf[:], io["causal"]).then_inc(const_loaded, 16)
            pool.dma_start(wqd[:], io["w_q_down"].rearrange("(k p) n -> p k n", p=P)).then_inc(w_loaded, 16)
            pool.dma_start(wkv[:, :, 0:DR], io["w_k_rope"].rearrange("(k p) n -> p k n", p=P)).then_inc(w_loaded, 16)
            pool.dma_start(wkv[:, :, DR:P], io["w_kv_down"].rearrange("(k p) n -> p k n", p=P)).then_inc(w_loaded, 16)
            pool.wait_ge(const_loaded, 32)
            pool.tensor_copy(consts["ident_b"][:], ident[:]).then_inc(consts_cast, 1)
            pool.tensor_copy(consts["causal_b"][:], maskf[:]).then_inc(consts_cast, 1)

        @block.vector
        def _(dve):
            norm.vector_stats(dve, x_loaded)

            def read_kv(t):
                dve.wait_ge(kv_ready, t + 1)
                dve.tensor_copy(kv[:, t, :], pkv[:, t % 2, 0:P]).then_inc(kv_read, 1)

            for t in range(NT):
                norm.vector_h(dve, t)
                if t >= 2:
                    read_kv(t - 2)
            read_kv(NT - 2)
            read_kv(NT - 1)
            dve.wait_ge(kv_read, NT)
            dve.wait_ge(table_loaded, 32)
            x1, x2 = kv[:, :, 0:32], kv[:, :, 32:64]
            for n, (a, b) in enumerate(((x1, cosk), (x2, sink), (x1, sink), (x2, cosk))):
                dve.tensor_tensor(tmp[:, n], a, b[:], ALU.mult).then_inc(prod_ready, 1)
            for half, op in ((0, ALU.subtract), (1, ALU.add)):
                dve.wait_ge(prod_ready, 2 + 2 * half)
                to = ktok[:, :, 0:DR].rearrange("p t (q h i) -> p t q h i", q=2, h=2)[:, :, :, half, :]
                a, b = (tmp[:, 2 * half + n].rearrange("p t (q i) -> p t q i", q=2) for n in range(2))
                for q in range(2):
                    last = dve.tensor_tensor(to[:, :, q, :], a[:, :, q, :], b[:, :, q, :], op)
                    last.then_inc(rope_ready, 1)
            for n in range(8):
                if n % 2:
                    dve.wait_ge(kT_ready, n + 1)
                    dst = kt["k_rl"] if n < 4 else kt["k_lr"]
                    c = n % 4
                    dve.tensor_copy(dst[:, c * 512:(c + 1) * 512], pk[:, n % 2]).then_inc(kT_read[1], 1)

        @block.scalar
        def _(act):
            norm.scalar_sqrt(act)

            def read_cq(n):
                c, m = n // 2, n % 2
                act.wait_ge(cq_ready, n + 1)
                act.copy(kt["cq"][:, m, c * 512:(c + 1) * 512], pcq[0:QC, n % 2, :]).then_inc(cq_read, 1)

            for t in range(NT):
                norm.scalar_hT(act, t)
                if t % 4 == 2 and t > 4:
                    read_cq(2 * (t // 4) - 2)
                    read_cq(2 * (t // 4) - 1)
            read_cq(6)
            read_cq(7)
            act.wait_ge(kv_read, NT)
            act.copy(ktok[:, :, DR:P], kv[:, :, DR:P]).then_inc(lat_ready, 1)
            act.wait_ge(rope_ready, 4)
            act.copy(ktok[:, :, P:192], ktok[:, :, 0:DR]).then_inc(dup_ready, 1)
            for n in range(0, 8, 2):
                act.wait_ge(kT_ready, n + 1)
                dst = kt["k_rl"] if n < 4 else kt["k_lr"]
                c = n % 4
                act.copy(dst[:, c * 512:(c + 1) * 512], pk[:, n % 2]).then_inc(kT_read[0], 1)

        @block.tensor
        def _(pe):
            def keys(t):
                pe.wait_ge(norm.s_hT, t + 1)
                if t >= 2:
                    pe.wait_ge(kv_read, t - 1)
                for k in range(KD):
                    last = pe.matmul(pkv[:, t % 2, 0:P], norm.hT[:, k, t * P:(t + 1) * P], wkv[:, k, :],
                                     start=(k == 0), stop=(k == KD - 1))
                last.then_inc(kv_ready, 1)

            def queries(c):
                for m in range(2):
                    n = 2 * c + m
                    if n >= 2:
                        pe.wait_ge(cq_read, n - 1)
                    for k in range(KD):
                        last = pe.matmul(pcq[0:QC, n % 2, :], wqd[:, k, m * QC:(m + 1) * QC],
                                         norm.hT[:, k, c * 512:(c + 1) * 512], start=(k == 0), stop=(k == KD - 1))
                    last.then_inc(cq_ready, 1)

            pe.wait_ge(const_loaded, 32)
            pe.wait_ge(w_loaded, 48)
            for t in range(NT):
                norm.tensor_transpose(pe, t)
                if t >= 1:
                    keys(t - 1)
                if t % 4 == 1 and t > 4:
                    queries(t // 4 - 1)
            keys(NT - 1)
            queries(3)
            pe.wait_ge(lat_ready, 1)
            for n in range(8):
                if n == 0:
                    pe.wait_ge(rope_ready, 4)
                if n == 4:
                    pe.wait_ge(dup_ready, 1)
                if n >= 2:
                    pe.wait_ge(kT_read[n % 2], n // 2)
                off = 0 if n < 4 else DR
                for j in range(4):
                    t = 4 * (n % 4) + j
                    last = pe.transpose(pk[:, n % 2, j, :], ktok[:, t, off:off + P], ident[:])
                last.then_inc(kT_ready, 1)


def attention_loop(nc, consts, shape, tag, turns, side):
    X, ident = consts["X"], consts["ident"]
    sh = shape
    NU, NGR, NK = sh.nu, len(sh.groups), sh.nchunk
    CW = sh.tpc * P
    M = P // sh.heads

    with ExitStack() as ctx:
        sb, ps, sem = scope(nc, ctx, tag)
        prob = sb("prob", [P, RING_P, S])
        probT = sb("probT", [P, 2, sh.heads, TB, CW])
        negmax = sb("negmax", [P, RING_P])
        rowsum = sb("rowsum", [P, RING_P])
        rinv = sb("rinv", [P, RING_P])
        head_out = sb("head_out", [P, 2, CW])
        score = ps("score", [P, 2, S])
        turned = ps("turned", [P, 2, 4, P])
        misc = ps("misc", [P, 2, 512])

        scores_ready = sem("scores_ready")
        negmax_ready = sem("negmax_ready")
        exp_done = sem("exp_done")
        rinv_ready = sem("rinv_ready")
        units_begun = sem("units_begun")
        prob_ready = sem("prob_ready")
        turned_ready = sem("turned_ready")
        read_dve = sem("read_dve")
        read_act = sem("read_act")
        pv_ready = sem("pv_ready")
        head_out_ready = sem("head_out_ready")
        proj_ready = sem("proj_ready")
        x_added = sem("x_added")

        side.allocate(sb, sem, misc, scores_ready, pv_ready, proj_ready)

        items = list(side.items)
        for k in range(NK):
            at = sh.last_unit(k) + LAG + 1
            items.append((at % NU, "pv", k if at < NU else k - NK))
            for n in range(sh.tpc):
                at = sh.last_unit(k) + LAG + 2 + n
                items.append((at % NU, "proj", k * sh.tpc + n if at < NU else (k - NK) * sh.tpc + n))
        items.sort(key=lambda x: x[0])
        assert len(items) % 2 == 0

        def skipped(item, first, last):
            return (first and item[2] < 0) or (last and item[1] in side.for_next)

        def place(item):
            return items.index(item)

        prologue = [it for it in items if it[1] in side.for_next]
        wrapped = [it for it in items if it[2] < 0]

        def last_in_bank(item, first, last, draining=False):
            at = len(items) if draining else place(item)
            seq = [(1, it) for it in (prologue if first else items)]
            if draining:
                seq = [(1, it) for it in items if not skipped(it, False, True)]
                seq += [(0, it) for it in wrapped[:wrapped.index(item)]]
            else:
                seq += [(0, it) for it in items[:at] if not skipped(it, first, last)]
            return next((x for x in reversed(seq) if place(x[1]) % 2 == place(item) % 2), None)

        def wait_bank(pe, i, before):
            if before is None:
                return
            back, (_, what, arg) = before
            if what == "pv":
                pe.wait_ge(head_out_ready, (i - back) * NK + arg + 1)
            elif what == "proj":
                pe.wait_ge(x_added, (i - back) * NT + arg + 1)
            else:
                pe.wait_ge(*side.read_out(i - back, what, arg))

        def run(engine, step, drain):
            for s in range(NU):
                step(0, s, True, False)
            with engine.Fori(1, turns - 1) as i:
                for s in range(NU):
                    step(i, s, False, False)
            for s in range(NU):
                step(turns - 1, s, False, True)
            drain(turns)

        block = ctx.enter_context(nc.Block())

        @block.tensor
        def _(pe):
            side.tensor_setup(pe)

            def scores(i, s, first):
                b, t, h = sh.units[s]
                side.tensor_scores_wait(pe, i, s)
                if not (first and s < 2):
                    pe.wait_ge(exp_done, i * NU + s - 1)
                n = (t + 1) * P
                for c0 in range(0, n, 512):
                    c1 = min(c0 + 512, n)
                    lhsT, rhs = side.score_operands(b, t, h, c0, c1)
                    pe.matmul(score[:, s % 2, c0:c1], lhsT, rhs, start=True, stop=(c1 < n))
                pe.matmul(score[:, s % 2, n - P:n], consts["ident_b"][:], consts["causal_b"][:],
                          start=False, stop=True).then_inc(scores_ready, 1)

            def transposes(i, u):
                uu = u % NU
                pe.wait_ge(prob_ready, i * NU + u + 1)
                for g in range(sh.first_group[uu], sh.first_group[uu + 1]):
                    _, j0, j1, _ = sh.groups[g]
                    gg = g if u >= 0 else g - NGR
                    by_act = sh.groups[g - 2][3]
                    if not (isinstance(i, int) and i == 0 and gg < 2):
                        pe.wait_ge(read_act if by_act else read_dve,
                                   i * sh.evacuated(NGR, by_act) + sh.evacuated(gg - 1, by_act))
                    for j in range(j0, j1):
                        last = pe.transpose(turned[:, g % 2, j - j0, :], prob[:, uu % RING_P, j * P:(j + 1) * P],
                                            ident[:])
                    last.then_inc(turned_ready, 1)

            def pv(i, k, bank):
                kk = k % NK
                b, c = divmod(kk, sh.chunks_per_batch)
                end = sh.first_group[sh.last_unit(kk) + 1] - (0 if k >= 0 else NGR)
                pe.wait_ge(read_act, i * sh.evacuated(NGR, True) + sh.evacuated(end, True))
                pe.wait_ge(read_dve, i * sh.evacuated(NGR, False) + sh.evacuated(end, False))
                side.tensor_pv_wait(pe, i, k)
                jn = (c + 1) * sh.tpc
                for j in range(jn):
                    q0 = max(0, j - c * sh.tpc) * P
                    for h in range(sh.heads):
                        last = pe.matmul(misc[h * M:(h + 1) * M, bank, q0:CW], side.value_operand(b, j, h),
                                         probT[:, kk % 2, h, j, q0:CW], start=(j == 0), stop=(j == jn - 1),
                                         skip_group_check=True)
                last.then_inc(pv_ready, 1)

            def proj(i, n, bank):
                k, tt = divmod(n, sh.tpc)
                pe.wait_ge(head_out_ready, i * NK + k + 1)
                side.tensor_proj_wait(pe, i, n)
                pe.matmul(misc[:, bank, :], head_out[:, k % 2, tt * P:(tt + 1) * P], side.out_w[:],
                          start=True, stop=True).then_inc(proj_ready, 1)

            def do(item, i, first, last):
                wait_bank(pe, i, last_in_bank(item, first, last))
                bank = place(item) % 2
                if item[1] == "pv":
                    pv(i, item[2], bank)
                elif item[1] == "proj":
                    proj(i, item[2], bank)
                else:
                    side.tensor_item(pe, i, item[1], item[2], bank)

            def step(i, s, first, last):
                scores(i, s, first)
                if s >= LAG or not first:
                    transposes(i, s - LAG)
                for item in items:
                    if item[0] == s and not skipped(item, first, last):
                        do(item, i, first, last)

            for n, item in enumerate(prologue):
                same = [(0, it) for it in prologue[:n] if place(it) % 2 == place(item) % 2]
                wait_bank(pe, -1, same[-1] if same else None)
                side.tensor_item(pe, -1, item[1], item[2], place(item) % 2)

            def drain(end):
                for s in range(LAG + 2 + sh.tpc):
                    if s < LAG:
                        transposes(end, s - LAG)
                    for item in wrapped:
                        if item[0] == s:
                            wait_bank(pe, end, last_in_bank(item, False, False, draining=True))
                            (pv if item[1] == "pv" else proj)(end, item[2], place(item) % 2)

            run(pe, step, drain)

        def read_out(eng, copy, i, u, by_act):
            uu = u % NU
            k = sh.chunk_of(uu)
            _, t, h = sh.units[uu]
            for g in range(sh.first_group[uu], sh.first_group[uu + 1]):
                _, j0, j1, act_has = sh.groups[g]
                if act_has != by_act:
                    continue
                gg = g if u >= 0 else g - NGR
                kk = k if u >= 0 else k - NK
                eng.wait_ge(turned_ready, i * NGR + gg + 1)
                if not (isinstance(i, int) and i == 0 and kk < 2):
                    eng.wait_ge(pv_ready, i * NK + kk - 1)
                q0 = (t % sh.tpc) * P
                copy(probT[:, k % 2, h, j0:j1, q0:q0 + P],
                     turned[:, g % 2, 0:j1 - j0, :]).then_inc(read_act if by_act else read_dve, 1)

        @block.vector
        def _(dve):
            side.vector_setup(dve)

            def evacuate(i, u):
                read_out(dve, dve.tensor_copy, i, u, False)

            def step(i, s, first, last):
                b, t, h = sh.units[s]
                n = (t + 1) * P
                dve.wait_ge(scores_ready, i * NU + s + 1)
                dve.reduce_max(negmax[:, s % RING_P:s % RING_P + 1], score[:, s % 2, 0:n], AX,
                               negate=True).then_inc(negmax_ready, 1)
                if s >= 1 or not first:
                    recip(i, s - 1)
                if s >= LAG or not first:
                    evacuate(i, s - LAG)
                for item in items:
                    if item[0] == s and not skipped(item, first, last):
                        if item[1] == "proj":
                            add(i, item)
                        else:
                            side.vector_item(dve, i, item[1], item[2], place(item) % 2)

            def recip(i, u):
                dve.wait_ge(exp_done, i * NU + u + 1)
                r = u % RING_P
                dve.reciprocal(rinv[:, r:r + 1], rowsum[:, r:r + 1]).then_inc(rinv_ready, 1)

            def add(i, item):
                n = item[2]
                tile = X[:, n % NT, :]
                dve.wait_ge(proj_ready, i * NT + n + 1)
                if not (isinstance(i, int) and i * NT + n == 0):
                    dve.wait_ge(x_added, i * NT + n)
                bank = place(item) % 2
                dve.tensor_tensor(tile, tile, misc[:, bank, :], ALU.add).then_inc(x_added, 1)

            for item in prologue:
                side.vector_item(dve, -1, item[1], item[2], place(item) % 2)

            def drain(end):
                for s in range(LAG + 2 + sh.tpc):
                    if s == 0:
                        recip(end, -1)
                    if s < LAG:
                        evacuate(end, s - LAG)
                    for item in wrapped:
                        if item[0] == s and item[1] == "proj":
                            add(end, item)

            run(dve, step, drain)

        @block.scalar
        def _(act):
            side.scalar_setup(act)

            def head_copy(i, item):
                k = item[2]
                bank = place(item) % 2
                act.wait_ge(pv_ready, i * NK + k + 1)
                if not (isinstance(i, int) and i == 0 and k < 2):
                    act.wait_ge(proj_ready, i * NT + (k - 1) * sh.tpc)
                act.copy(head_out[:, k % 2, :], misc[:, bank, 0:CW]).then_inc(head_out_ready, 1)

            def step(i, s, first, last):
                b, t, h = sh.units[s]
                n = (t + 1) * P
                r = s % RING_P
                act.wait_ge(negmax_ready, i * NU + s + 1)
                if not (first and s < RING_P):
                    act.wait_ge(turned_ready, i * NGR + turned_by(s - RING_P))
                act.activation(prob[:, r, 0:n], score[:, s % 2, 0:n], ACT.Exp, bias=negmax[:, r:r + 1],
                               accum_out=rowsum[:, r:r + 1]).then_inc(exp_done, 1)
                if s >= LAG or not first:
                    read_out(act, act.copy, i, s - LAG, True)
                for item in items:
                    if item[0] == s and not skipped(item, first, last):
                        if item[1] == "pv":
                            head_copy(i, item)
                        else:
                            side.scalar_item(act, i, item[1], item[2], place(item) % 2)

            def turned_by(u):
                return sh.first_group[u % NU + 1] - (0 if u >= 0 else NGR)

            for item in prologue:
                side.scalar_item(act, -1, item[1], item[2], place(item) % 2)

            def drain(end):
                for s in range(LAG + 2 + sh.tpc):
                    if s < LAG:
                        read_out(act, act.copy, end, s - LAG, True)
                    for item in wrapped:
                        if item[0] == s and item[1] == "pv":
                            head_copy(end, item)

            run(act, step, drain)

        @block.gpsimd
        def _(pool):
            side.gpsimd_setup(pool)

            def normalise(i, u):
                uu = u % NU
                n = (sh.units[uu][1] + 1) * P
                r = uu % RING_P
                pool.wait_ge(rinv_ready, i * NU + u + 1)
                pool.sem_inc(units_begun, 1)
                pool.tensor_scalar(prob[:, r, 0:n], prob[:, r, 0:n], rinv[:, r:r + 1], 1.0,
                                   ALU.mult, ALU.mult).then_inc(prob_ready, 1)

            def step(i, s, first, last):
                if s >= 1 or not first:
                    normalise(i, s - 1)
                for item in items:
                    if item[0] == s and not skipped(item, first, last):
                        side.gpsimd_item(pool, i, item[1], item[2])
                side.gpsimd_step(pool, i, s, first, last)

            for item in prologue:
                side.gpsimd_item(pool, -1, item[1], item[2])

            run(pool, step, lambda end: normalise(end, -1))

        @block.sync
        def _(sp):
            side.loads(sp, turns)


class LatentSide:

    for_next = ("nopeT", "fold_q", "rope0", "lat0")
    items = [(1, "rope", 2), (2, "lat", 2), (3, "rope", 3), (4, "lat", 3), (9, "fold_v", 0),
             (9, "nopeT", 0), (10, "nopeT", 1), (16, "fold_q", 0),
             (18, "rope0", 0), (20, "lat0", 0), (22, "rope0", 1), (24, "lat0", 1)]

    def __init__(self, nc, io, consts, kt):
        self.nc, self.io, self.consts, self.kt = nc, io, consts, kt

    def allocate(self, sb, sem, misc, scores_ready, pv_ready, proj_ready):
        self.misc, self.scores_ready = misc, scores_ready
        self.proj_ready = proj_ready
        self.q = sb("q", [P, 2, T])
        self.w_nope = sb("w_nope", [QC, 2, 2 * DN])
        self.w_rope = sb("w_rope", [QC, 2, P])
        self.wuk = sb("wuk", [P, 2, KVL])
        self.wuv = sb("wuv", [P, 2, KVL])
        self.wo = sb("wo", [P, 2, D])
        self.nopeT = sb("nopeT", [P, 2, 2, QC])
        self.w_lat = sb("w_lat", [QC, 2, P])
        self.out_w = sb("out_w", [P, D])
        self.cosq = sb("cosq", [P, S])
        self.sinq = sb("sinq", [P, S])
        self.partner = sb("partner", [P, 512])
        self.cosine = sb("cosine", [P, 512])
        self.tables = sem("tables")
        self.n_loaded, self.r_loaded, self.v_loaded = sem("n_loaded"), sem("r_loaded"), sem("v_loaded")
        self.nopeT_ready, self.nopeT_read = sem("nopeT_ready"), sem("nopeT_read")
        self.fold_q_ready, self.w_lat_ready = sem("fold_q_ready"), sem("w_lat_ready")
        self.fold_v_ready, self.out_w_ready = sem("fold_v_ready"), sem("out_w_ready")
        self.rope_ready, self.lat_ready = sem("rope_ready"), sem("lat_ready")
        self.partner_ready, self.cosine_ready = sem("partner_ready"), sem("cosine_ready")
        self.sine_done, self.q_rope_done, self.q_lat_done = sem("sine_done"), sem("q_rope_done"), sem("q_lat_done")

    @staticmethod
    def chunk(i, what, c):
        return (i + 1, c) if what.endswith("0") else (i, c)

    def read_out(self, i, what, c):
        if what == "nopeT":
            return self.nopeT_read, 2 * (i + 1) + c + 1
        if what == "fold_q":
            return self.w_lat_ready, i + 2
        if what == "fold_v":
            return self.out_w_ready, i + 1
        pair, c = self.chunk(i, what, c)
        if what.startswith("rope"):
            return self.partner_ready, 4 * pair + c + 1
        return self.q_lat_done, 8 * pair + 2 * c + 2

    def loads(self, sp, turns):
        io = self.io

        def load_n(pair):
            sp.dma_start(self.w_nope[:], io["w_q_up_nope"].rearrange("(k p) n -> p k n", p=QC)
                         [:, :, bass.ds(pair * 2 * DN, 2 * DN)]).then_inc(self.n_loaded, 16)
            sp.dma_start(self.wuk[:], io["w_uk"][bass.ds(pair * 2 * DN, 2 * DN), :]
                         .rearrange("(h p) r -> p h r", p=P)).then_inc(self.n_loaded, 16)

        def load_r(pair):
            src = io["w_q_up_rope"].rearrange("(k p) n -> p k n", p=QC)[:, :, bass.ds(pair * P, P)]
            src = src.rearrange("p k (h f q i) -> p k h f q i", h=2, f=2, q=2)
            dst = self.w_rope[:].rearrange("p k (h q f i) -> p k h q f i", h=2, f=2, q=2)
            for h in range(2):
                for f in range(2):
                    for q in range(2):
                        sp.dma_start(dst[:, :, h, q, f, :], src[:, :, h, f, q, :]).then_inc(self.r_loaded, 16)

        def load_v(pair):
            sp.dma_start(self.wuv[:], io["w_uv"][bass.ds(pair * 2 * DV, 2 * DV), :]
                         .rearrange("(h p) r -> p h r", p=P)).then_inc(self.v_loaded, 16)
            sp.dma_start(self.wo[:], io["w_out"][bass.ds(pair * 2 * DV, 2 * DV), :]
                         .rearrange("(h p) r -> p h r", p=P)).then_inc(self.v_loaded, 16)

        load_n(0)
        load_r(0)
        sp.dma_start(self.cosq[:], io["cos_rows"]).then_inc(self.tables, 16)
        sp.dma_start(self.sinq[:], io["sin_rows"]).then_inc(self.tables, 16)
        load_v(0)
        with sp.Fori(0, turns - 1) as i:
            sp.wait_ge(self.fold_q_ready, i + 1)
            load_n(i + 1)
            sp.wait_ge(self.rope_ready, 4 * i + 4)
            load_r(i + 1)
            sp.wait_ge(self.fold_v_ready, i + 1)
            load_v(i + 1)

    def tensor_setup(self, pe):
        pass

    def vector_setup(self, dve):
        pass

    def scalar_setup(self, act):
        pass

    def gpsimd_setup(self, pool):
        pass

    def gpsimd_step(self, pool, i, s, first, last):
        pass

    def tensor_scores_wait(self, pe, i, s):
        if s % 8 == 0:
            pe.wait_ge(self.q_rope_done, 8 * i + 2 * (s // 8) + 2)
            pe.wait_ge(self.q_lat_done, 8 * i + 2 * (s // 8) + 2)

    def score_operands(self, b, t, h, c0, c1):
        keys = self.kt["k_rl"] if h == 0 else self.kt["k_lr"]
        return self.q[:, h, b * S + t * P:b * S + (t + 1) * P], keys[:, b * S + c0:b * S + c1]

    def tensor_pv_wait(self, pe, i, k):
        pass

    def value_operand(self, b, j, h):
        return self.kt["ktok"][:, b * TB + j, DR:P]

    def tensor_proj_wait(self, pe, i, n):
        if n == 0:
            pe.wait_ge(self.out_w_ready, i + 1)

    def tensor_item(self, pe, i, what, c, bank):
        misc = self.misc
        if what == "nopeT":
            pe.wait_ge(self.n_loaded, 32 * (i + 1) + 32)
            for k in range(2):
                last = pe.transpose(misc[:, bank, k * QC:(k + 1) * QC], self.w_nope[:, k, c * DN:(c + 1) * DN],
                                    self.consts["ident"][0:QC, 0:QC])
            last.then_inc(self.nopeT_ready, 1)
        elif what == "fold_q":
            pe.wait_ge(self.nopeT_read, 2 * (i + 1) + 2)
            for k in range(2):
                for h in range(2):
                    at = k * P + (1 - h) * KVL
                    last = pe.matmul(misc[0:QC, bank, at:at + KVL], self.nopeT[:, h, k, :], self.wuk[:, h, :],
                                     start=True, stop=True)
            last.then_inc(self.fold_q_ready, 1)
        elif what == "fold_v":
            pe.wait_ge(self.v_loaded, 32 * i + 32)
            for h in range(2):
                last = pe.matmul(misc[h * KVL:(h + 1) * KVL, bank, :], self.wuv[:, h, :], self.wo[:, h, :],
                                 start=True, stop=True, skip_group_check=True)
            last.then_inc(self.fold_v_ready, 1)
        else:
            pair, c = self.chunk(i, what, c)
            rope = what.startswith("rope")
            if rope:
                pe.wait_ge(self.r_loaded, 128 * pair + 128)
            else:
                pe.wait_ge(self.w_lat_ready, pair + 1)
            w = self.w_rope if rope else self.w_lat
            for k in range(2):
                last = pe.matmul(misc[:, bank, :], w[:, k, :], self.kt["cq"][:, k, c * 512:(c + 1) * 512],
                                 start=(k == 0), stop=(k == 1))
            last.then_inc(self.rope_ready if rope else self.lat_ready, 1)

    def vector_item(self, dve, i, what, c, bank):
        if not what.startswith("rope"):
            return
        pair, c = self.chunk(i, what, c)
        n = pair * 4 + c
        first = isinstance(n, int) and n == 0
        if first:
            dve.wait_ge(self.tables, 32)
        else:
            dve.wait_ge(self.q_rope_done, 2 * n)
        dve.wait_ge(self.rope_ready, n + 1)
        cc = c % 2
        dve.tensor_tensor(self.cosine[:], self.misc[:, bank, :], self.cosq[:, cc * 512:(cc + 1) * 512], ALU.mult)\
           .then_inc(self.cosine_ready, 1)
        dve.stream_shuffle(self.partner[:], self.misc[:, bank, :], [(r + 16) % 32 for r in range(32)])\
           .then_inc(self.partner_ready, 1)

    def gpsimd_item(self, pool, i, what, c):
        if not what.startswith("rope"):
            return
        pair, c = self.chunk(i, what, c)
        n = pair * 4 + c
        cc = c % 2
        pool.wait_ge(self.partner_ready, n + 1)
        if isinstance(n, int) and n == 0:
            pool.wait_ge(self.tables, 32)
        pool.tensor_tensor(self.partner[:], self.partner[:], self.sinq[:, cc * 512:(cc + 1) * 512], ALU.mult)\
            .then_inc(self.sine_done, 1)
        pool.wait_ge(self.sine_done, n + 1)
        pool.wait_ge(self.cosine_ready, n + 1)
        self.wait_q_free(pool, pair, c)
        for h in range(2):
            rows = slice(h * DR, (h + 1) * DR)
            pool.tensor_tensor(self.q[rows, h, c * 512:(c + 1) * 512], self.cosine[rows, :], self.partner[rows, :],
                               ALU.add).then_inc(self.q_rope_done, 1)
        pool.wait_ge(self.q_rope_done, 2 * n + 2)

    def wait_q_free(self, eng, pair, c):
        if not (isinstance(pair, int) and pair == 0):
            eng.wait_ge(self.scores_ready, pair * 32 - 32 + 16 * (c // 2) + 16)

    def scalar_item(self, act, i, what, c, bank):
        misc = self.misc
        if what == "nopeT":
            n = (i + 1) * 2 + c
            act.wait_ge(self.nopeT_ready, n + 1)
            if not (isinstance(i, int) and i == -1):
                act.wait_ge(self.fold_q_ready, i + 1)
            act.copy(self.nopeT[:, c].rearrange("p k n -> p (k n)"), misc[:, bank, 0:2 * QC]).then_inc(
                self.nopeT_read, 1)
        elif what == "fold_q":
            act.wait_ge(self.fold_q_ready, i + 2)
            if not (isinstance(i, int) and i == -1):
                act.wait_ge(self.lat_ready, 4 * i + 4)
            act.copy(self.w_lat[:], misc[0:QC, bank, 0:2 * P].rearrange("p (k n) -> p k n", k=2)).then_inc(
                self.w_lat_ready, 1)
        elif what == "fold_v":
            act.wait_ge(self.fold_v_ready, i + 1)
            if not (isinstance(i, int) and i == 0):
                act.wait_ge(self.proj_ready, i * NT)
            act.copy(self.out_w[:], misc[:, bank, :]).then_inc(self.out_w_ready, 1)
        elif what.startswith("lat"):
            pair, c = self.chunk(i, what, c)
            n = pair * 4 + c
            act.wait_ge(self.lat_ready, n + 1)
            self.wait_q_free(act, pair, c)
            for h in range(2):
                rows = slice((1 - h) * KVL, (2 - h) * KVL)
                act.mul(self.q[rows, h, c * 512:(c + 1) * 512], misc[rows, bank, :], SCALE_A)\
                    .then_inc(self.q_lat_done, 1)


def latent_attention(nc, io, consts, kt):
    shape = Shape(2, 4, lambda n, u, j0, j1: n % 2 == 1)
    attention_loop(nc, consts, shape, "la", PAIRS, LatentSide(nc, io, consts, kt))


class Grouped:

    CW = 512
    CT = CW // P
    LAGQ = 3
    ZT = 8
    QUAD_COST, PIECE_COST = 1400, 64
    RING_Q = 4


MAXIMA = [(t, h, half) for t in (0, 7, 1, 6, 2, 5, 3, 4) for h in range(REP) for half in range(1 if t < 4 else 2)]
QUADS = [(c, j) for c in range(S // Grouped.CW) for j in range(Grouped.CT * (c + 1))]


def spread_maxima():
    n, zt = len(QUADS), Grouped.ZT
    window = list(range(zt + 1, n)) + list(range(zt))
    room = {z: Grouped.QUAD_COST + min(Grouped.CW, (QUADS[z][0] + 1) * Grouped.CW - QUADS[z][1] * P) for z in window}
    cost = [min(512, (t - 3) * P if half else (t + 1) * P) + Grouped.PIECE_COST for t, _, half in MAXIMA]
    at, p = {}, 0
    for x, z in enumerate(window):
        end = sum(cost) * sum(room[y] for y in window[:x + 1]) / sum(room.values())
        q = p
        while q < len(MAXIMA) and (x == len(window) - 1 or sum(cost[:q + 1]) <= end):
            q += 1
        at[z] = range(p, q)
        p = q
    return at


def grouped_attention(nc, io, consts, vtok, scratch):
    X, ident_b, causal_b = consts["X"], consts["ident_b"], consts["causal_b"]
    q3, k3, heads_d = scratch
    g = Grouped
    NQ, NM, CT, CW = len(QUADS), len(MAXIMA), g.CT, g.CW
    NP2 = NQ * REP
    RB = 3
    maxima_at, ZT = spread_maxima(), g.ZT
    assert NM % RB == 0 and NP2 % RB == 0 and NQ % g.RING_Q == 0

    with ExitStack() as ctx:
        sb, ps, sem = scope(nc, ctx, "ga")
        q1, q2 = (sb(f"q{n}", [99, NB, REP, S], BF16) for n in (1, 2))
        k1, k2 = (sb(f"k{n}", [99, NB, S], BF16) for n in (1, 2))
        v = sb("v", [P, NB, TB, 32])
        out_w = sb("out_w", [P, KD, D])
        heads_all = sb("heads_all", [P, KD, T])
        prob = sb("prob", [P, g.RING_Q, REP, CW])
        mx = sb("mx", [P, REP, TB])
        mx_far = sb("mx_far", [P, REP, TB // 2])
        neg_rest = sb("neg_rest", [P, REP * TB])
        neg_parts = sb("neg_parts", [P, 3, REP * TB], BF16)
        neg_rows = sb("neg_rows", [3 * REP * TB, P], BF16)
        turned = sb("turned", [P, CW // 32, 32])
        inverse = sb("inverse", [P, CW // 32])
        heads = sb("heads", [P, 2, CW])
        s1 = ps("s1", [P, RB, 512])
        s2 = ps("s2", [P, RB, 512])
        ov = ps("ov", [P, 2, 512])

        loaded1, loaded2, stored, heads_loaded = (
            [sem(f"{n}{b}") for b in range(NB)] for n in ("loaded1_", "loaded2_", "stored", "heads_loaded"))
        w_loaded, late_loaded = sem("w_loaded"), [sem("late_loaded0"), sem("late_loaded1")]
        zeroed, v_ready = sem("zeroed"), sem("v_ready")
        s1_ready, s1_read, mx_step = sem("s1_ready"), sem("s1_read"), sem("mx_step")
        neg_turned, neg_copied, neg_placed = sem("neg_turned"), sem("neg_copied"), sem("neg_placed")
        s2_ready, prob_ready, pv_done = sem("s2_ready"), sem("prob_ready"), sem("pv_done")
        turned_ready, inverse_ready, divided, heads_ready = (
            sem("turned_ready"), sem("inverse_ready"), sem("divided"), sem("heads_ready"))
        proj_ready, x_added = sem("proj_ready"), sem("x_added")

        def run(engine, body):
            body(0, True, False)
            with engine.Fori(1, G - 1) as i:
                body(i, False, False)
            body(G - 1, False, True)

        def ahead(i, b, z, first, last):
            if z == ZT or (last and (b == 1 or z > ZT)):
                return []
            step = 2 if z > ZT else 1
            return [(2 * i + b + step, i + (b + step) // 2, (b + step) % 2, p) for p in maxima_at[z]]

        ahead_of_all = [(0, 0, 0, p) for p in range(NM)], [(1, 0, 1, p) for z in range(ZT + 1, NQ) for p in maxima_at[z]]

        block = ctx.enter_context(nc.Block())

        @block.sync
        def _(sp):
            def load(q, k, i, b, landed):
                cols = slice(b * S, (b + 1) * S)
                for n, (qp, kp) in enumerate(((0, 0), (0, 1), (0, 2), (1, 0), (1, 1), (2, 0))):
                    rows = slice(n * HD, (n + 1) * HD)
                    sp.dma_start(q[rows, b], q3[qp, bass.ds(i * REP * HD, REP * HD), cols]
                                 .rearrange("(h d) t -> d h t", d=HD)).then_inc(landed, 16)
                    sp.dma_start(k[rows, b], k3[kp, bass.ds(b * G + i, 1)].rearrange("a d t -> (a d) t"))\
                        .then_inc(landed, 16)

            def store(i, b, back):
                ii, bb, c = (i, b, 0) if back == 0 else (i, 0, 1) if b else (i - 1, 1, 1)
                sp.wait_ge(heads_ready, 4 * i + 2 * b - back + 1)
                for h in range(REP):
                    sp.dma_start(heads_d[bass.ds((ii * REP + h) * HD, HD), bb * S + c * CW:bb * S + (c + 1) * CW],
                                 heads[32 * h:32 * h + HD, c, :]).then_inc(stored[c], 16)

            def load_last_rows(cols, landed):
                sp.dma_start(heads_all[P // 2:, KD - 1, cols], heads_d[D - P // 2:, cols]).then_inc(landed, 16)

            def load_earlier_rows():
                sp.wait_ge(stored[0], 64 * (2 * G - 1))
                sp.wait_ge(stored[1], 64 * (2 * G - 2))
                for b in range(NB):
                    cols = slice(b * S, (b + 1) * S)
                    sp.dma_start(heads_all[:, 0:KD - 1, cols],
                                 heads_d[0:D - P, cols].rearrange("(k p) t -> p k t", p=P))\
                        .then_inc(heads_loaded[b], 16)
                    sp.dma_start(heads_all[0:P // 2, KD - 1, cols], heads_d[D - P:D - P // 2, cols])\
                        .then_inc(heads_loaded[b], 16)

            load(q1, k1, 0, 0, loaded1[0])
            load(q1, k1, 0, 1, loaded1[1])
            load(q2, k2, 0, 0, loaded2[0])
            load(q2, k2, 0, 1, loaded2[1])
            sp.dma_start(out_w[:], io["b_Wo"].rearrange("(k p) n -> p k n", p=P)).then_inc(w_loaded, 16)

            def body(i, first, last):
                for b in range(NB):
                    if not (first and b == 0):
                        store(i, b, 1)
                    if last and b == 1:
                        sp.wait_ge(stored[1], 64 * (2 * G - 1))
                        load_last_rows(slice(0, S), heads_loaded[0])
                    if not last:
                        sp.wait_ge(s1_ready, 2 * NM * i + NM * (b + 1))
                        load(q1, k1, i + 1, b, loaded1[b])
                    store(i, b, 0)
                    if not last:
                        sp.wait_ge(s2_ready, 2 * NP2 * i + NP2 * (b + 1))
                        load(q2, k2, i + 1, b, loaded2[b])
                    if last and b == 0:
                        load_earlier_rows()

            run(sp, body)
            sp.wait_ge(stored[0], 64 * 2 * G)
            load_last_rows(slice(S, S + CW), late_loaded[0])
            store(G, 0, 1)
            sp.wait_ge(stored[1], 64 * 2 * G)
            load_last_rows(slice(S + CW, T), late_loaded[1])

        @block.gpsimd
        def _(pool):
            def values(i, b):
                pool.tensor_copy(v[:, b, :, 0:HD], vtok[:, bass.ds(b * G + i, 1)]
                                 .rearrange("p a t d -> p (a t) d")).then_inc(v_ready, 1)

            pool.memset(v[:], 1.0).then_inc(zeroed, 1)
            pool.wait_ge(zeroed, 1)
            pool.memset(k2[96:99], 1.0).then_inc(zeroed, 1)
            pool.wait_ge(zeroed, 2)
            values(0, 0)

            def divide(i, b, back):
                k = 4 * i + 2 * b - back
                pool.wait_ge(inverse_ready, k + 1)
                pool.tensor_tensor(turned[:], turned[:], inverse[:, :, None].to_broadcast([P, CW // 32, 32]),
                                   ALU.mult).then_inc(divided, 1)

            def body(i, first, last):
                for b in range(NB):
                    if not (first and b == 0):
                        divide(i, b, 1)
                    if not (last and b == 1):
                        if not (first and b == 0):
                            pool.wait_ge(pv_done, (2 * i + b) * NQ)
                        values(i + b, 1 - b)
                    divide(i, b, 0)

            run(pool, body)
            divide(G, 0, 1)

        @block.vector
        def _(dve):
            def maximum(n, i, b, p):
                t, h, half = MAXIMA[p]
                if p == 0 and not (isinstance(n, int) and n == 0):
                    dve.wait_ge(mx_step, 4 * n)
                to = mx_far[:, h, t - 4:t - 3] if half else mx[:, h, t:t + 1]
                cols = min(512, (t + 1) * P) if not half else (t - 3) * P
                dve.wait_ge(s1_ready, n * NM + p + 1)
                dve.reduce_max(to, s1[:, p % RB, 0:cols], AX).then_inc(s1_read, 1)

            def negate(n):
                flat = mx[:].rearrange("p h t -> p (h t)")
                if not (isinstance(n, int) and n == 0):
                    dve.wait_ge(neg_turned, n)
                dve.wait_ge(s1_read, n * (NM + 1) + NM)
                dve.tensor_tensor(mx[:, :, 4:8], mx[:, :, 4:8], mx_far[:], ALU.max).then_inc(s1_read, 1)
                dve.wait_ge(s1_read, (n + 1) * (NM + 1))
                dve.tensor_scalar(neg_parts[:, 0], flat, -1.0, None, ALU.mult).then_inc(mx_step, 1)
                dve.wait_ge(mx_step, 4 * n + 1)
                dve.scalar_tensor_tensor(neg_rest[:], flat, -1.0, neg_parts[:, 0], ALU.mult, ALU.subtract)\
                   .then_inc(mx_step, 1)
                dve.wait_ge(mx_step, 4 * n + 2)
                dve.tensor_copy(neg_parts[:, 1], neg_rest[:]).then_inc(mx_step, 1)
                dve.wait_ge(mx_step, 4 * n + 3)
                dve.tensor_tensor(neg_parts[:, 2], neg_rest[:], neg_parts[:, 1], ALU.subtract).then_inc(mx_step, 1)

            def turn_heads(i, b, back):
                k = 4 * i + 2 * b - back
                dve.wait_ge(pv_done, (2 * i + b) * NQ + (CT if back == 0 else 0))
                dve.transpose(turned[:].rearrange("p a c -> p (a c)"), ov[:, back, :]).then_inc(turned_ready, 1)
                dve.wait_ge(turned_ready, k + 1)
                dve.reciprocal(inverse[:], turned[:, :, HD]).then_inc(inverse_ready, 1)

            def turn_back(i, b, back):
                k = 4 * i + 2 * b - back
                if not (isinstance(k, int) and k < 2):
                    dve.wait_ge(stored[back], 64 * (2 * i + b - back))
                dve.wait_ge(divided, k + 1)
                dve.transpose(heads[:, back, :], turned[:].rearrange("p a c -> p (a c)")).then_inc(heads_ready, 1)

            def add_projection(tile):
                dve.wait_ge(proj_ready, tile + 1)
                dve.tensor_tensor(X[:, tile, :], X[:, tile, :], s1[:, tile % RB, :], ALU.add).then_inc(x_added, 1)

            for piece in ahead_of_all[0]:
                maximum(*piece)
            negate(0)
            for piece in ahead_of_all[1]:
                maximum(*piece)

            def body(i, first, last):
                for b in range(NB):
                    n = 2 * i + b
                    for z in range(NQ):
                        for piece in ahead(i, b, z, first, last):
                            maximum(*piece)
                        if z == ZT and not (last and b == 1):
                            negate(n + 1)
                        if z == 2 and not (first and b == 0):
                            turn_heads(i, b, 1)
                        if z == 3 and not (first and b == 0):
                            turn_back(i, b, 1)
                        if z == 6:
                            turn_heads(i, b, 0)
                        if z == 7:
                            turn_back(i, b, 0)
                        if last and b == 1 and z >= NQ - TB:
                            add_projection(z - (NQ - TB))

            run(dve, body)
            turn_heads(G, 0, 1)
            turn_back(G, 0, 1)
            for tile in range(TB, NT):
                add_projection(tile)

        @block.scalar
        def _(act):
            def weights(i, b, z):
                c, j = QUADS[z]
                q0 = max(0, j - CT * c) * P
                n = 2 * i + b
                if not (isinstance(n, int) and n == 0 and z < g.RING_Q):
                    act.wait_ge(pv_done, n * NQ + z - g.RING_Q + 1)
                for h in range(REP):
                    p = z * REP + h
                    act.wait_ge(s2_ready, n * NP2 + p + 1)
                    act.activation(prob[:, z % g.RING_Q, h, q0:CW], s2[:, p % RB, q0:CW], ACT.Exp)\
                       .then_inc(prob_ready, 1)

            def place_maxima(n, b):
                act.wait_ge(neg_turned, n + 1)
                if not (isinstance(n, int) and n == 0):
                    act.wait_ge(neg_placed, 48 * n)
                act.copy(neg_rows[:], s1[0:3 * REP * TB, 0, 0:P // 2].bitcast(BF16)).then_inc(neg_copied, 1)
                act.wait_ge(neg_copied, n + 1)
                if not (isinstance(n, int) and n < 2):
                    act.wait_ge(s2_ready, (n - 1) * NP2)
                for s in range(3):
                    act.dma_start(q2[96 + s:97 + s, b].rearrange("a h (t n) -> a (h t) n", n=P),
                                  neg_rows[s * REP * TB:(s + 1) * REP * TB, :]).then_inc(neg_placed, 16)

            place_maxima(0, 0)

            def body(i, first, last):
                for b in range(NB):
                    for z in range(NQ):
                        weights(i, b, z)
                        if z == ZT and not (last and b == 1):
                            place_maxima(2 * i + b + 1, 1 - b)

            run(act, body)

        @block.tensor
        def _(pe):
            def scores_for_maximum(n, i, b, p):
                t, h, half = MAXIMA[p]
                if p == 0:
                    pe.wait_ge(loaded1[b], 192 * (i + 1))
                if not (isinstance(n, int) and n == 0 and p < RB):
                    pe.wait_ge(s1_read, n * (NM + 1) + p - RB + 1)
                if p == 0 and not (isinstance(n, int) and n == 0):
                    pe.wait_ge(neg_copied, n)
                c0, c1 = (512, (t + 1) * P) if half else (0, min(512, (t + 1) * P))
                diagonal = c1 == (t + 1) * P
                last = pe.matmul(s1[:, p % RB, 0:c1 - c0], q1[0:96, b, h, t * P:(t + 1) * P], k1[0:96, b, c0:c1],
                                 start=True, stop=not diagonal)
                if diagonal:
                    last = pe.matmul(s1[:, p % RB, c1 - c0 - P:c1 - c0], ident_b[:], causal_b[:],
                                     start=False, stop=True)
                last.then_inc(s1_ready, 1)

            def turn_maxima(n):
                pe.wait_ge(mx_step, 4 * n + 4)
                pe.transpose(s1[0:3 * REP * TB, 0, 0:P // 2].bitcast(BF16),
                             neg_parts[:].rearrange("p s x -> p (s x)"), ident_b[:]).then_inc(neg_turned, 1)

            def scores(i, b, z, h):
                c, j = QUADS[z]
                q0 = max(0, j - CT * c) * P
                n, p = 2 * i + b, z * REP + h
                if p == 0:
                    pe.wait_ge(loaded2[b], 192 * (i + 1))
                    pe.wait_ge(neg_placed, 48 * (n + 1))
                if not (isinstance(n, int) and n == 0 and p < RB):
                    pe.wait_ge(prob_ready, n * NP2 + p - RB + 1)
                diagonal = j >= CT * c
                last = pe.matmul(s2[:, p % RB, q0:CW], k2[:, b, j * P:(j + 1) * P],
                                 q2[:, b, h, c * CW + q0:(c + 1) * CW], start=True, stop=not diagonal)
                if diagonal:
                    last = pe.matmul(s2[:, p % RB, q0:q0 + P], causal_b[:], ident_b[:], start=False, stop=True)
                last.then_inc(s2_ready, 1)

            def product(i, b, z):
                c, j = QUADS[z]
                q0 = max(0, j - CT * c) * P
                n = 2 * i + b
                pe.wait_ge(prob_ready, n * NP2 + (z + 1) * REP)
                if z == 0:
                    pe.wait_ge(v_ready, n + 1)
                if j == 0 and not (isinstance(n, int) and n == 0):
                    pe.wait_ge(turned_ready, 2 * n + c - 1)
                for h in range(REP):
                    last = pe.matmul(ov[32 * h:32 * h + 32, c, q0:CW], v[:, b, j, :],
                                     prob[:, z % g.RING_Q, h, q0:CW], start=(j == 0), stop=(j == CT * (c + 1) - 1),
                                     skip_group_check=True)
                last.then_inc(pv_done, 1)

            def project(tile):
                if tile == 0:
                    pe.wait_ge(w_loaded, 16)
                    pe.wait_ge(heads_loaded[0], 48)
                if tile == TB:
                    pe.wait_ge(heads_loaded[1], 32)
                if tile >= TB and tile % CT == 0:
                    pe.wait_ge(late_loaded[(tile - TB) // CT], 16)
                if tile >= RB:
                    pe.wait_ge(x_added, tile - RB + 1)
                for k in range(KD):
                    last = pe.matmul(s1[:, tile % RB, :], heads_all[:, k, tile * P:(tile + 1) * P], out_w[:, k, :],
                                     start=(k == 0), stop=(k == KD - 1))
                last.then_inc(proj_ready, 1)

            pe.wait_ge(zeroed, 2)
            for piece in ahead_of_all[0]:
                scores_for_maximum(*piece)
            turn_maxima(0)
            for piece in ahead_of_all[1]:
                scores_for_maximum(*piece)

            def body(i, first, last):
                for b in range(NB):
                    n = 2 * i + b
                    for z in range(NQ):
                        pieces = ahead(i, b, z, first, last)
                        for h in range(REP):
                            scores(i, b, z, h)
                            for piece in pieces[len(pieces) * h // REP:len(pieces) * (h + 1) // REP]:
                                scores_for_maximum(*piece)
                            if h == 1:
                                if z >= g.LAGQ:
                                    product(i, b, z - g.LAGQ)
                                elif not (first and b == 0):
                                    product(i if b else i - 1, 1 - b, z - g.LAGQ + NQ)
                        if z == ZT and not (last and b == 1):
                            turn_maxima(n + 1)
                        if last and b == 1 and z >= NQ - TB:
                            project(z - (NQ - TB))

            run(pe, body)
            for z in range(g.LAGQ):
                product(G - 1, 1, z - g.LAGQ + NQ)
            for tile in range(TB, NT):
                project(tile)


def grouped_inputs(nc, io, consts, vtok, scratch):
    q3, k3, _ = scratch
    with ExitStack() as ctx:
        sb, ps, sem = scope(nc, ctx, "gi")
        norm = Norm(nc, ctx, "gi", consts["X"], consts["ident"])
        wq = sb("wq", [P, KD, D])
        wk = sb("wk", [P, KD, P])
        wv = sb("wv", [P, KD, P])
        bo = sb("bo", [P, D])
        parts = sb("parts", [P, 2, 3, 512], BF16)
        rest = sb("rest", [P, 2, 512])
        pv = ps("pv", [P, 2, 512])
        pq = ps("pq", [P, 4, 512])
        w_loaded, v_ready, v_read = sem("w_loaded"), sem("v_ready"), sem("v_read")
        q_ready, high_ready, rest_ready, mid_ready, low_ready = (
            sem("q_ready"), sem("high_ready"), sem("rest_ready"), sem("mid_ready"), sem("low_ready"))
        stored = [sem("stored_even"), sem("stored_odd")]
        bias_added = sem("bias_added")
        NQ = 5 * 4
        block = ctx.enter_context(nc.Block())

        @block.sync
        def _(sp):
            sp.dma_start(wq[:], io["b_Wq"].rearrange("(k p) n -> p k n", p=P)).then_inc(w_loaded, 16)
            wkv = io["b_Wkv"].rearrange("(k p) (g two d) -> p k g two d", p=P, two=2, d=HD)
            for k in range(KD):
                for n, w in enumerate((wk, wv)):
                    sp.dma_start(w[:, k, :].rearrange("p (g d) -> p g d", d=HD), wkv[:, k, :, n, :])\
                        .then_inc(w_loaded, 16)
            sp.dma_start(bo[:], io["b_bo"].partition_broadcast(P)).then_inc(w_loaded, 16)
            for n in range(NQ):
                c, m = divmod(n, 5)
                sp.wait_ge(low_ready, n + 1)
                cols = slice(c * 512, (c + 1) * 512)
                b, part = divmod(c, 2)
                for s in range(3):
                    dst = q3[s, m * P:(m + 1) * P, cols] if m < 4 else (
                        k3[s].rearrange("(g b) d t -> b g d t", b=NB)[b, :, :, part * 512:(part + 1) * 512])
                    sp.dma_start(dst, parts[:, n % 2, s]).then_inc(stored[n % 2], 16)
            for s in stored:
                sp.wait_ge(s, 48 * (NQ // 2))

        @block.vector
        def _(dve):
            norm.vector_stats(dve)

            def split(n):
                dve.wait_ge(high_ready, n + 1)
                if n >= 2:
                    dve.wait_ge(low_ready, n - 1)
                dve.scalar_tensor_tensor(rest[:, n % 2], pq[:, n % 4], 0.25 if n % 5 < 4 else 1.0,
                                         parts[:, n % 2, 0], ALU.mult, ALU.subtract).then_inc(rest_ready, 1)

            def values(t):
                dve.wait_ge(v_ready, t + 1)
                to = vtok[:].rearrange("p (g b) t d -> p b t g d", b=NB)[:, t // TB, t % TB]
                dve.tensor_copy(to, pv[:, t % 2, 0:P].rearrange("p (g d) -> p g d", d=HD)).then_inc(v_read, 1)

            dve.wait_ge(w_loaded, 160)
            for t in range(NT):
                norm.vector_h(dve, t)
                if t >= 2:
                    values(t - 2)
                if t % 4 == 1 and t > 4:
                    for m in range(5):
                        split((t // 4 - 1) * 5 + m)
            values(NT - 2)
            values(NT - 1)
            for m in range(5):
                split(15 + m)
            for t in range(NT):
                dve.wait_ge(norm.s_h, NT)
                dve.tensor_tensor(consts["X"][:, t, :], consts["X"][:, t, :], bo[:], ALU.add).then_inc(bias_added, 1)

        @block.scalar
        def _(act):
            norm.scalar_sqrt(act)

            def high(n):
                act.wait_ge(q_ready, n + 1)
                if n >= 2:
                    act.wait_ge(stored[n % 2], 48 * (n // 2))
                act.mul(parts[:, n % 2, 0], pq[:, n % 4], 0.25 if n % 5 < 4 else 1.0).then_inc(high_ready, 1)

            def mid(n):
                act.wait_ge(rest_ready, n + 1)
                act.copy(parts[:, n % 2, 1], rest[:, n % 2]).then_inc(mid_ready, 1)

            for t in range(NT):
                norm.scalar_hT(act, t)
                if t % 4 == 1 and t > 4:
                    for m in range(5):
                        n = (t // 4 - 1) * 5 + m
                        high(n)
                        mid(n)
            for n in range(15, 20):
                high(n)
                mid(n)

        @block.gpsimd
        def _(pool):
            for n in range(NQ):
                pool.wait_ge(mid_ready, n + 1)
                pool.tensor_tensor(parts[:, n % 2, 2], rest[:, n % 2], parts[:, n % 2, 1],
                                   ALU.subtract).then_inc(low_ready, 1)

        @block.tensor
        def _(pe):
            def values(t):
                pe.wait_ge(norm.s_hT, t + 1)
                if t >= 2:
                    pe.wait_ge(v_read, t - 1)
                for k in range(KD):
                    last = pe.matmul(pv[:, t % 2, 0:P], norm.hT[:, k, t * P:(t + 1) * P], wv[:, k, :],
                                     start=(k == 0), stop=(k == KD - 1))
                last.then_inc(v_ready, 1)

            def project(c):
                for m in range(5):
                    n = 5 * c + m
                    if n >= 4:
                        pe.wait_ge(rest_ready, n - 3)
                    for k in range(KD):
                        w = wq[:, k, m * P:(m + 1) * P] if m < 4 else wk[:, k, :]
                        last = pe.matmul(pq[:, n % 4, :], w, norm.hT[:, k, c * 512:(c + 1) * 512],
                                         start=(k == 0), stop=(k == KD - 1))
                    last.then_inc(q_ready, 1)

            pe.wait_ge(w_loaded, 160)
            for t in range(NT):
                norm.tensor_transpose(pe, t)
                if t >= 1:
                    values(t - 1)
                if t % 4 == 1 and t > 4:
                    project(t // 4 - 1)
            values(NT - 1)
            project(3)


def memory_weights(nc, io, consts, mem):
    ident = consts["ident"]
    with ExitStack() as ctx:
        sb, ps, sem = scope(nc, ctx, "mw")
        raw = {n: sb(n, s) for n, s in (("Wq", [BOT, D]), ("Wr", [RDIM, BOT]), ("keys", [P, BOT]), ("vals", [P, D]),
                                        ("Wvd", [VB, D]), ("Wvu", [P, KD, VB]), ("Wu1", [P, D]))}
        rhs = sb("rhs", [BOT, 2 * P])
        keysT = sb("keysT", [BOT, P])
        WrT = sb("WrT", [BOT, RDIM])
        rkT = sb("rkT", [RDIM, P])
        valsT = sb("valsT", [P, KD, P])
        WvdT = sb("WvdT", [P, KD, VB])
        WvuT = sb("WvuT", [VB, D])
        lowT = sb("lowT", [VB, P])
        bank = ps("bank", [P, 2, 512])
        loaded, made, read = sem("loaded"), sem("made"), sem("read")
        block = ctx.enter_context(nc.Block())
        NLOAD = 14

        @block.sync
        def _(sp):
            for to, of in ((raw["Wq"][:], io["f_Wq"]), (raw["Wr"][:], io["f_Wr"]), (raw["keys"][:], io["f_aux_keys"]),
                           (raw["vals"][:], io["f_aux_values"]), (raw["Wvd"][:], io["f_Wvd"]),
                           (raw["Wvu"][:], io["f_Wvu"].rearrange("(k p) v -> p k v", p=P)), (raw["Wu1"][:], io["f_Wu1"]),
                           (mem["logit_bias"][:, 0:P], io["f_log_rel"].partition_broadcast(P)),
                           (mem["logit_bias"][:, P:2 * P], io["f_log_rel"].partition_broadcast(P)),
                           (mem["logit_bias"][:, 2 * P:], io["f_bu1"].partition_broadcast(P)),
                           (mem["u2"][:], io["f_Wu2"].rearrange("a n -> (a n)").partition_broadcast(P)),
                           (mem["bu2"][:], io["f_bu2"].partition_broadcast(P)),
                           (mem["gw1"][:], io["f_gate_w1"].partition_broadcast(P)),
                           (mem["gbias"][:], io["f_gate_bias"].partition_broadcast(P))):
                sp.dma_start(to, of).then_inc(loaded, 16)

        def turned(dst, of, rows):
            return lambda pe, b: pe.transpose(bank[0:of.shape[-1], b, dst:dst + rows], of, ident[0:rows, 0:rows])

        def product(out, lhsT, rhs_, start=True, stop=True):
            return lambda pe, b: pe.matmul(out(b), lhsT, rhs_, start=start, stop=stop)

        stages = [
            ([turned(0, raw["keys"][:], P), turned(P, raw["Wr"][:], RDIM)],
             [(keysT[:], lambda b: bank[0:BOT, b, 0:P], 1.0), (WrT[:], lambda b: bank[0:BOT, b, P:P + RDIM], 1.0),
              (rhs[:, P:], lambda b: bank[0:BOT, b, 0:P], float(1.0 / np.sqrt(BOT)))]),
            ([turned(k * P, raw["vals"][:, k * P:(k + 1) * P], P) for k in range(KD)],
             [(valsT[:], lambda b: bank[:, b, :].rearrange("p (k n) -> p k n", k=KD), 1.0)]),
            ([turned(k * VB, raw["Wvd"][:, k * P:(k + 1) * P], VB) for k in range(KD)],
             [(WvdT[:], lambda b: bank[:, b, 0:KD * VB].rearrange("p (k n) -> p k n", k=KD), 1.0)]),
            ([turned(k * P, raw["Wvu"][:, k, :], P) for k in range(KD)],
             [(WvuT[:], lambda b: bank[0:VB, b, :], 1.0)]),
            ([turned(k * P, raw["Wu1"][:, k * P:(k + 1) * P], P) for k in range(KD)],
             [(mem["logit_w"][:, :, 2 * P:], lambda b: bank[:, b, :].rearrange("p (k n) -> p k n", k=KD), 1.0)]),
            ([product(lambda b: bank[0:RDIM, b, 0:P], WrT[:], keysT[:])],
             [(rkT[:], lambda b: bank[0:RDIM, b, 0:P], 1.0)]),
            ([product(lambda b: bank[0:VB, b, 0:P], WvdT[:, k, :], valsT[:, k, :], k == 0, k == KD - 1)
              for k in range(KD)],
             [(lowT[:], lambda b: bank[0:VB, b, 0:P], 1.0)]),
            ([product(lambda b: bank[0:BOT, b, 0:P], raw["Wr"][:], rkT[:])],
             [(rhs[:, 0:P], lambda b: bank[0:BOT, b, 0:P], float(1.0 / np.sqrt(RDIM)))]),
            ([product(lambda b: bank[:, b, :], lowT[:], WvuT[:])],
             [(mem["value_w"][:], lambda b: bank[:, b, :], 1.0)]),
        ] + [
            ([product(lambda b, o=o: bank[:, b, o * 256:o * 256 + 256], raw["Wq"][:, k * P:(k + 1) * P], rhs[:])
              for o, k in enumerate((kk, kk + 1))],
             [(mem["logit_w"][:, kk:kk + 2, 0:2 * P],
               lambda b: bank[:, b, :].rearrange("p (k n) -> p k n", k=2), 1.0)])
            for kk in (0, 2)
        ]
        reads = [sum(len(st[1]) for st in stages[:n + 1]) for n in range(len(stages))]
        needs = {5: 0, 6: 2, 7: 5, 8: 6, 9: 7, 10: 7}

        @block.tensor
        def _(pe):
            pe.wait_ge(loaded, 16 * NLOAD)
            for n, (mms, _) in enumerate(stages):
                before = max(needs.get(n, 0), n - 2)
                if n >= 2:
                    pe.wait_ge(read, reads[before])
                for mm in mms:
                    last = mm(pe, n % 2)
                last.then_inc(made, 1)

        @block.vector
        def _(dve):
            for n, (_, outs) in enumerate(stages):
                dve.wait_ge(made, n + 1)
                for dst, src, scale in outs:
                    dve.tensor_scalar(dst, src(n % 2), scale, None, ALU.mult).then_inc(read, 1)


def memory_block(nc, io, consts, mem, tag, out):
    X, ident = consts["X"], consts["ident"]
    with ExitStack() as ctx:
        sb, ps, sem = scope(nc, ctx, tag)
        norm = Norm(nc, ctx, tag, X, ident)
        logits = sb("logits", [P, NT, 3 * P])
        top = sb("top", [P, NT, 8])
        rest = sb("rest", [P, 2, 4, P])
        chosen = sb("chosen", [P, 2, 4, P])
        negmax = sb("negmax", [P, NT])
        weight = sb("weight", [P, 2, 4, P])
        wsum = sb("wsum", [P, NT])
        weightT = sb("weightT", [P, T])
        small = sb("small", [P, 24, NT])
        gel = sb("gel", [P, 3, NT, UH])
        ones = sb("ones", [P, P])
        mean = sb("mean", [P, 2])
        gain = sb("gain", [P, NT])
        plog = ps("plog", [P, 2, 512])
        pturn = ps("pturn", [P, 512])
        pmean = ps("pmean", [P, 512])
        pout = ps("pout", [P, 2, 512])
        lg_ready, lg_read = sem("lg_ready"), sem("lg_read")
        top_ready, rest_ready, same_ready, chosen_ready, nm_ready = (
            sem("top_ready"), sem("rest_ready"), sem("same_ready"), sem("chosen_ready"), sem("nm_ready"))
        w_ready, wT_ready, wT_read = sem("w_ready"), sem("wT_ready"), sem("wT_read")
        ln_in, ln_done = sem("ln_in"), sem("ln_done")
        mean_in, mean_done, ones_ready = sem("mean_in"), sem("mean_done"), sem("ones_ready")
        tanh_in, tanh_done = sem("tanh_in"), sem("tanh_done")
        out_ready, x_ready, stored = sem("out_ready"), sem("x_ready"), sem("stored")
        gain_ready, normed_added = sem("gain_ready"), sem("normed_added")
        chain = sem("chain")
        block = ctx.enter_context(nc.Block())

        @block.vector
        def _(dve):
            linked = [0]

            def link(instruction):
                linked[0] += 1
                instruction.then_inc(chain, 1)
                dve.wait_ge(chain, linked[0])

            norm.vector_stats(dve)
            (v2, v3, u, ln, less, zero, num, den, rden, lv, me, nv, lsum, lrn, lt, un, un2, gz, gt, gate, ok, rs,
             sc, shift) = (small[:, n, :] for n in range(24))
            link(dve.tensor_tensor(v2, norm.mv[:, :, 1], norm.rstd[:], ALU.mult))
            link(dve.tensor_tensor(v3, v2, norm.rstd[:], ALU.mult))
            dve.tensor_scalar(u, v3, 1.0, None, ALU.add).then_inc(ln_in, 1)
            link(dve.tensor_tensor(shift, norm.mv[:, :, 0], norm.rstd[:], ALU.mult))
            link(dve.tensor_scalar(shift, shift, -1.0, None, ALU.mult))
            dve.tensor_scalar(gain[:], norm.rstd[:], 1.0, None, ALU.add).then_inc(gain_ready, 1)
            for t in range(2):
                norm.vector_h(dve, t)
            dve.wait_ge(ln_in, 1)
            link(dve.tensor_scalar(less, u, 1.0, None, ALU.subtract))
            link(dve.tensor_scalar(zero, less, 0.0, None, ALU.is_equal))
            link(dve.tensor_tensor(den, less, zero, ALU.add))
            link(dve.reciprocal(rden, den))
            dve.wait_ge(ln_done, 1)
            link(dve.tensor_tensor(num, ln, zero, ALU.add))
            link(dve.tensor_tensor(num, num, v3, ALU.mult))
            link(dve.tensor_tensor(lv, num, rden, ALU.mult))
            dve.reduce_sum(mean[:, 0:1], lv, AX).then_inc(mean_in, 1)

            def read_logits(t):
                dve.wait_ge(lg_ready, t + 1)
                dve.tensor_tensor(logits[:, t, :], plog[:, t % 2, 0:3 * P], mem["logit_bias"][:],
                                  ALU.add).then_inc(lg_read, 1)

            def choose(c):
                tiles = range(4 * c, 4 * c + 4)
                par = c % 2
                for t in tiles:
                    dve.wait_ge(lg_read, t + 1)
                    dve.max(top[:, t, :], logits[:, t, 0:P]).then_inc(top_ready, 1)
                for t in tiles:
                    dve.wait_ge(top_ready, t + 1)
                    dve.match_replace(rest[:, par, t % 4, :], top[:, t, :], logits[:, t, 0:P], -3.4e38)\
                        .then_inc(rest_ready, 1)
                dve.wait_ge(rest_ready, 4 * c + 4)
                if c >= 2:
                    dve.wait_ge(w_ready, 4 * c - 4)
                four = slice(4 * c, 4 * c + 4)
                dve.tensor_tensor(chosen[:, par], rest[:, par], logits[:, four, 0:P], ALU.is_equal)\
                    .then_inc(same_ready, 1)
                dve.wait_ge(same_ready, c + 1)
                dve.scalar_tensor_tensor(chosen[:, par], chosen[:, par], NEG, logits[:, four, P:2 * P],
                                         ALU.mult, ALU.add).then_inc(chosen_ready, 1)
                dve.wait_ge(chosen_ready, c + 1)
                dve.reduce_max(negmax[:, four], chosen[:, par], AX, negate=True).then_inc(nm_ready, 1)

            for t in range(2, NT):
                norm.vector_h(dve, t)
                read_logits(t - 2)
                if t % 4 == 2 and t > 2:
                    choose(t // 4 - 1)
            read_logits(NT - 2)
            read_logits(NT - 1)
            choose(3)

            hid = logits[:, :, 2 * P:3 * P]
            sq, z, th = gel[:, 0], gel[:, 1], gel[:, 2]
            link(dve.tensor_tensor(sq, hid, hid, ALU.mult))
            link(dve.tensor_scalar(sq, sq, 0.044715, 1.0, ALU.mult, ALU.add))
            dve.tensor_tensor(z, sq, hid, ALU.mult).then_inc(tanh_in, 1)
            dve.wait_ge(mean_done, 1)
            link(dve.tensor_scalar(me[:, 0:1], pmean[:, 0:1], 1e-6, None, ALU.add))
            link(dve.reciprocal(mean[:, 1:2], me[:, 0:1]))
            link(dve.tensor_scalar(nv, lv, mean[:, 1:2], 0.5, ALU.mult, ALU.mult))
            dve.wait_ge(tanh_done, 1)
            link(dve.scalar_tensor_tensor(sq, th, 1.0, hid, ALU.add, ALU.mult))
            link(dve.tensor_tensor(z, sq, mem["u2"][:].unsqueeze(1).broadcast_to([P, NT, UH]), ALU.mult))
            link(dve.reduce_sum(lsum, z, AX))
            dve.tensor_scalar(lrn, lsum, 0.5, mem["bu2"][:, 0:1], ALU.mult, ALU.add).then_inc(tanh_in, 1)
            dve.wait_ge(tanh_done, 2)
            link(dve.tensor_scalar(un, lt, 1.25, 1.25, ALU.mult, ALU.add))
            link(dve.tensor_tensor(un, un, nv, ALU.add))
            link(dve.tensor_scalar(un, un, 0.0, 5.0, ALU.max, ALU.min))
            link(dve.tensor_scalar(un, un, 0.5, 1.0 / 1.5, ALU.subtract, ALU.mult))
            link(dve.tensor_scalar(un2, un, 0.0, 1.0, ALU.max, ALU.min))
            dve.tensor_scalar(gz, un2, mem["gw1"][:, 0:1], mem["gbias"][:, 0:1], ALU.mult, ALU.add)\
                .then_inc(tanh_in, 1)
            dve.wait_ge(tanh_done, 3)
            link(dve.tensor_scalar(gate, gt, 0.5, 0.5, ALU.mult, ALU.add))
            link(dve.tensor_scalar(ok, gate, 0.05, None, ALU.is_ge))
            link(dve.tensor_tensor(gate, gate, ok, ALU.mult))
            dve.wait_ge(w_ready, NT)
            link(dve.reciprocal(rs, wsum[:]))
            link(dve.tensor_tensor(sc, gate, rs, ALU.mult))
            for t in range(NT):
                dve.wait_ge(out_ready, t + 1)
                dve.wait_ge(normed_added, t + 1)
                dve.scalar_tensor_tensor(X[:, t, :], pout[:, t % 2, :], sc[:, t:t + 1], X[:, t, :],
                                         ALU.mult, ALU.add).then_inc(x_ready, 1)

        @block.scalar
        def _(act):
            norm.scalar_sqrt(act)
            act.wait_ge(ln_in, 1)
            act.activation(small[:, 3, :], small[:, 2, :], ACT.Ln).then_inc(ln_done, 1)

            def weights(c):
                for t in range(4 * c, 4 * c + 4):
                    act.wait_ge(nm_ready, c + 1)
                    if c >= 2:
                        act.wait_ge(wT_ready, c - 1)
                    act.activation(weight[:, c % 2, t % 4, :], chosen[:, c % 2, t % 4, :], ACT.Exp,
                                   bias=negmax[:, t:t + 1], accum_out=wsum[:, t:t + 1]).then_inc(w_ready, 1)

            def read_turned(c):
                act.wait_ge(wT_ready, c + 1)
                act.copy(weightT[:, c * 512:(c + 1) * 512], pturn[:]).then_inc(wT_read, 1)

            for t in range(NT):
                norm.scalar_hT(act, t)
                if t % 4 == 3 and t > 4:
                    weights(t // 4 - 1)
                if t % 4 == 1 and t > 8:
                    read_turned(t // 4 - 2)
            read_turned(2)
            weights(3)
            read_turned(3)
            act.wait_ge(tanh_in, 1)
            act.activation(gel[:, 2], gel[:, 1], ACT.Tanh, scale=float(np.sqrt(2.0 / np.pi))).then_inc(tanh_done, 1)
            act.wait_ge(tanh_in, 2)
            act.activation(small[:, 14, :], small[:, 13, :], ACT.Tanh, scale=0.5).then_inc(tanh_done, 1)
            act.wait_ge(tanh_in, 3)
            act.activation(small[:, 18, :], small[:, 17, :], ACT.Tanh, scale=0.5).then_inc(tanh_done, 1)

        @block.gpsimd
        def _(pool):
            pool.memset(ones[:], 1.0 / T).then_inc(ones_ready, 1)
            pool.wait_ge(gain_ready, 1)
            for t in range(NT):
                pool.wait_ge(norm.s_h, t + 1)
                pool.tensor_scalar(X[:, t, :], X[:, t, :], gain[:, t:t + 1], small[:, 23, t:t + 1],
                                   ALU.mult, ALU.add).then_inc(normed_added, 1)

        @block.tensor
        def _(pe):
            def logit(t):
                pe.wait_ge(norm.s_hT, t + 1)
                if t >= 2:
                    pe.wait_ge(lg_read, t - 1)
                for k in range(KD):
                    last = pe.matmul(plog[:, t % 2, 0:3 * P], norm.hT[:, k, t * P:(t + 1) * P],
                                     mem["logit_w"][:, k, :], start=(k == 0), stop=(k == KD - 1))
                last.then_inc(lg_ready, 1)

            def turn(c):
                pe.wait_ge(w_ready, 4 * c + 4)
                if c >= 1:
                    pe.wait_ge(wT_read, c)
                for j in range(4):
                    last = pe.transpose(pturn[:, j * P:(j + 1) * P], weight[:, c % 2, j, :], ident[:])
                last.then_inc(wT_ready, 1)

            for t in range(NT):
                norm.tensor_transpose(pe, t)
                if t >= 1:
                    logit(t - 1)
                if t % 4 == 0 and t >= 8:
                    turn(t // 4 - 2)
            logit(NT - 1)
            pe.wait_ge(ones_ready, 1)
            pe.wait_ge(mean_in, 1)
            pe.matmul(pmean[:, 0:1], ones[:], mean[:, 0:1], start=True, stop=True).then_inc(mean_done, 1)
            turn(2)
            turn(3)
            for t in range(NT):
                pe.wait_ge(wT_read, t // 4 + 1)
                if t >= 2:
                    pe.wait_ge(x_ready, t - 1)
                pe.matmul(pout[:, t % 2, :], weightT[:, t * P:(t + 1) * P], mem["value_w"][:],
                          start=True, stop=True).then_inc(out_ready, 1)

        @block.sync
        def _(sp):
            if out is not None:
                o = out.rearrange("b (t p) d -> p (b t) d", p=P)
                for c in range(4):
                    sp.wait_ge(x_ready, 4 * c + 4)
                    sp.dma_start(o[:, 4 * c:4 * c + 4, :], X[:, 4 * c:4 * c + 4, :]).then_inc(stored, 16)
                sp.wait_ge(stored, 64)


_NAMES = {"L0_attn_a_hidden_states": "x", "L0_attn_a_w_q_down": "w_q_down", "L0_attn_a_w_q_up_nope": "w_q_up_nope",
          "L0_attn_a_w_q_up_rope": "w_q_up_rope", "L0_attn_a_w_kv_down": "w_kv_down",
          "L0_attn_a_w_k_rope": "w_k_rope", "L0_attn_a_w_uk": "w_uk", "L0_attn_a_w_uv": "w_uv",
          "L0_attn_a_w_out": "w_out", "L0_attn_b_Wq": "b_Wq", "L0_attn_b_Wkv": "b_Wkv", "L0_attn_b_Wo": "b_Wo",
          "L0_attn_b_bo": "b_bo", "L0_ffn_Wq": "f_Wq", "L0_ffn_Wr": "f_Wr", "L0_ffn_aux_keys": "f_aux_keys",
          "L0_ffn_aux_values": "f_aux_values", "L0_ffn_Wvd": "f_Wvd", "L0_ffn_Wvu": "f_Wvu", "L0_ffn_Wu1": "f_Wu1",
          "L0_ffn_bu1": "f_bu1", "L0_ffn_Wu2": "f_Wu2", "L0_ffn_bu2": "f_bu2", "L0_ffn_gate_w1": "f_gate_w1",
          "L0_ffn_gate_bias": "f_gate_bias", "L0_ffn_log_rel": "f_log_rel"}


def _tables():
    f = np.float32
    freqs = f(1.0) / np.power(f(10000.0), np.arange(0, DR, 2, dtype=f) / f(DR))
    wavelengths = f(2.0 * np.pi) / freqs
    ramp = np.clip((wavelengths / f(4096.0) - f(1.0)) / f(31.0), f(0), f(1)).astype(f)
    inv_freq = (freqs / (f(1.0) - ramp + ramp * f(40.0))).astype(f)
    angle = (np.arange(S, dtype=f)[:, None] * inv_freq[None, :]).astype(f)
    cos, sin = np.cos(angle).astype(f), np.sin(angle).astype(f)
    tok = lambda a: np.ascontiguousarray(np.tile(a.reshape(TB, P, 32).transpose(1, 0, 2), (1, NB, 1)))
    scaled = f(SCALE_A)

    def rows(low, high):
        quads = [part[:, 16 * q:16 * q + 16].T for q in range(2) for part in (low, high)]
        return np.ascontiguousarray(np.concatenate(quads * 2, axis=0) * scaled)

    i = np.arange(P)
    return {"identity": np.eye(P, dtype=f), "causal": np.where(i[None, :] > i[:, None], f(NEG), f(0)).astype(f),
            "cos_tok": tok(cos), "sin_tok": tok(sin), "cos_rows": rows(cos, cos), "sin_rows": rows(-sin, sin)}


def kernel(**inputs):
    import numpy as _np
    import concourse.bacc as _bacc
    from concourse import mybir as _mybir
    from concourse.bass_utils import run_bass_kernel_spmd as _run

    nc = _bacc.Bacc("TRN2", target_bir_lowering=False, num_devices=1)
    arrays, io = {}, {}
    given = {short: _np.atleast_1d(_np.ascontiguousarray(inputs[name])) for name, short in _NAMES.items()}
    for short, a in {**given, **_tables()}.items():
        arrays[f"in_{short}"] = a
        io[short] = nc.dram_tensor(f"in_{short}", a.shape, _mybir.dt.from_np(a.dtype), kind="ExternalInput").ap()
    io["out"] = nc.dram_tensor("out_dram", (NB, S, D), _mybir.dt.float32, kind="ExternalOutput").ap()
    build(nc, io)
    r = _run(nc, [arrays], core_ids=[0])
    return r.results[0]["out_dram"]
```

```python
from contextlib import ExitStack

import numpy as np

import concourse.bass as bass
from concourse import mybir

F32 = mybir.dt.float32
F32R = mybir.dt.float32r
BF16 = mybir.dt.bfloat16
ALU = mybir.AluOpType
ACT = mybir.ActivationFunctionType
AX = mybir.AxisListType.X

P = 128
D = 512
KD = D // P
NB = 2
S = 1024
T = NB * S
NT = T // P
TB = S // P
EPS = 1e-5
NEG = -1e30

H = 32
QL = 192
QC = QL // 2
KVL = 64
DN = 128
DR = 64
DV = 128
PAIRS = H // 2
SCALE_A = float(1.0 / np.sqrt(np.float32(DN + DR)))
G = 8
HD = 16
REP = H // G
BOT, RDIM, NSLOT, VB = 64, 48, 128, 32
UH = D // 4

RING_P = 4
LAG = 3


def groups_of(t):
    return [(0, t + 1)] if t < 4 else [(0, 4), (4, t + 1)]


class Shape:

    def __init__(self, heads, tiles_per_chunk, on_act):
        self.heads, self.tpc = heads, tiles_per_chunk
        self.units = [(b, t, h) for b in range(NB) for t in range(TB) for h in range(heads)]
        self.nu = len(self.units)
        self.chunks_per_batch = TB // tiles_per_chunk
        self.nchunk = NB * self.chunks_per_batch
        self.groups = []
        for u, (b, t, h) in enumerate(self.units):
            for j0, j1 in groups_of(t):
                self.groups.append((u, j0, j1, on_act(len(self.groups), u, j0, j1)))
        self.first_group = [next(n for n, g in enumerate(self.groups) if g[0] == u) for u in range(self.nu)]
        self.first_group.append(len(self.groups))
        assert len(self.groups) % 2 == 0

    def chunk_of(self, u):
        b, t, _ = self.units[u]
        return b * self.chunks_per_batch + t // self.tpc

    def last_unit(self, k):
        return (k + 1) * self.tpc * self.heads - 1

    def evacuated(self, n_groups, by_act):
        turn = sum(g[3] == by_act for g in self.groups)
        if n_groups < 0:
            return self.evacuated(n_groups + len(self.groups), by_act) - turn
        return sum(g[3] == by_act for g in self.groups[:n_groups])


def build(nc, io):
    top = ExitStack()
    with top:
        def keep(name, shape, dt=F32):
            return top.enter_context(nc.sbuf_tensor(name, shape, dt))

        X = keep("X", [P, NT, D])
        ident = keep("ident", [P, P])
        ident_b = keep("ident_b", [P, P], BF16)
        causal_b = keep("causal_b", [P, P], BF16)
        consts = dict(X=X, ident=ident, ident_b=ident_b, causal_b=causal_b)
        with ExitStack() as latent:
            kt = {n: latent.enter_context(nc.sbuf_tensor(n, s, F32R)) for n, s in (
                ("cq_high", [QC, 2, T]), ("cq_low", [QC, 2, T]))}
            kt |= {n: latent.enter_context(nc.sbuf_tensor(n, s, F32)) for n, s in (
                ("k_rl", [P, T]), ("k_lr", [P, T]), ("values", [P, NT, KVL]))}
            latent_inputs(nc, io, consts, kt)
            latent_attention(nc, io, consts, kt)
        mem = {n: keep(n, s) for n, s in (
            ("logit_w", [P, KD, 3 * P]), ("value_w", [P, D]), ("logit_bias", [P, 3 * P]),
            ("u2", [P, UH]), ("bu2", [P, 1]), ("gw1", [P, 1]), ("gbias", [P, 1]))}
        memory_weights(nc, io, consts, mem)
        memory_block(nc, io, consts, mem, "f1", None)
        with ExitStack() as grouped:
            vtok = grouped.enter_context(nc.sbuf_tensor("vtok", [P, NB * G, TB, HD], F32))
            scratch = (nc.dram_tensor("query_parts", (3, D, T), BF16).ap(),
                       nc.dram_tensor("key_parts", (3, NB * G, HD, S), BF16).ap(),
                       nc.dram_tensor("heads_out", (D, T), F32).ap())
            grouped_inputs(nc, io, consts, vtok, scratch)
            grouped_attention(nc, io, consts, vtok, scratch)
        memory_block(nc, io, consts, mem, "f2", io["out"])


def scope(nc, ctx, tag):
    def sb(name, shape, dt=F32):
        return ctx.enter_context(nc.sbuf_tensor(f"{tag}_{name}", shape, dt))

    def ps(name, shape, dt=F32):
        return ctx.enter_context(nc.psum_tensor(f"{tag}_{name}", shape, dt))

    held = []

    def clear():
        nc.clear_and_free_semaphores(held)
        nc.all_engine_barrier()

    ctx.callback(clear)

    def sem(name):
        held.append(nc.alloc_semaphore(f"{tag}_{name}"))
        return held[-1]

    return sb, ps, sem


def high_part(dve, high, x):
    return dve.tensor_copy(high, x)


def low_part(engine, low, x, high):
    return engine.tensor_tensor(low, x, high.bitcast(F32), ALU.subtract)


def split_products(pe, out, pairs, start=True, stop=True):
    n = len(pairs)
    for x, ((w_high, w_low), (m_high, m_low)) in enumerate(pairs):
        pe.matmul(out, w_high, m_high, start=start and x == 0, stop=False)
        pe.matmul(out, w_high, m_low, start=False, stop=False)
        last = pe.matmul(out, w_low, m_high, start=False, stop=stop and x == n - 1)
    return last


class Norm:

    def __init__(self, nc, ctx, tag, X, ident):
        sb, ps, sem = scope(nc, ctx, tag)
        self.X, self.ident = X, ident
        self.stats = sb("ln_stats", [P, NT, 6])
        self.mv = sb("ln_mv", [P, NT, 2])
        self.ve = sb("ln_ve", [P, NT])
        self.sd = sb("ln_sd", [P, NT])
        self.rstd = sb("ln_rstd", [P, NT])
        self.h = sb("ln_h", [P, 2, D])
        self.hT = sb("hT", [P, KD, T])
        self.pt = ps("ln_pt", [P, 2, KD, P])
        self.s_stats = sem("ln_stats_ready")
        self.s_mv = sem("ln_mv_ready")
        self.s_ve = sem("ln_ve_ready")
        self.s_sd = sem("ln_sd_ready")
        self.s_rstd = sem("ln_rstd_ready")
        self.s_h = sem("ln_h_ready")
        self.s_tr = sem("ln_transposed")
        self.s_hT = sem("ln_hT_ready")

    def vector_stats(self, dve, c, x_loaded=None):
        four = slice(4 * c, 4 * c + 4)
        if x_loaded is not None:
            dve.wait_ge(x_loaded[c], 16)
        for t in range(4 * c, 4 * c + 4):
            dve.bn_stats(self.stats[:, t, :], self.X[:, t, :]).then_inc(self.s_stats, 1)
        for t in range(4 * c, 4 * c + 4):
            dve.wait_ge(self.s_stats, t + 1)
            dve.bn_aggr(self.mv[:, t, :], self.stats[:, t, :]).then_inc(self.s_mv, 1)
        dve.wait_ge(self.s_mv, 4 * c + 4)
        dve.tensor_scalar(self.ve[:, four], self.mv[:, four, 1], EPS, None, ALU.add).then_inc(self.s_ve, 1)
        dve.wait_ge(self.s_sd, c + 1)
        dve.reciprocal(self.rstd[:, four], self.sd[:, four]).then_inc(self.s_rstd, 1)
        dve.wait_ge(self.s_rstd, c + 1)

    def scalar_sqrt(self, act, c):
        four = slice(4 * c, 4 * c + 4)
        act.wait_ge(self.s_ve, c + 1)
        act.activation(self.sd[:, four], self.ve[:, four], ACT.Sqrt).then_inc(self.s_sd, 1)

    @staticmethod
    def stats_behind(t):
        return t == 1 or (t % 4 == 0 and 0 < t < NT - 4)

    def vector_h(self, dve, t):
        if t >= 2:
            dve.wait_ge(self.s_tr, t - 1)
        dve.tensor_scalar(self.h[:, t % 2, :], self.X[:, t, :], self.mv[:, t, 0:1], self.rstd[:, t:t + 1],
                          ALU.subtract, ALU.mult).then_inc(self.s_h, 1)

    def tensor_transpose(self, pe, t):
        pe.wait_ge(self.s_h, t + 1)
        if t >= 2:
            pe.wait_ge(self.s_hT, t - 1)
        for k in range(KD):
            last = pe.transpose(self.pt[:, t % 2, k, :], self.h[:, t % 2, k * P:(k + 1) * P], self.ident[:])
        last.then_inc(self.s_tr, 1)

    def scalar_hT(self, act, t):
        act.wait_ge(self.s_tr, t + 1)
        act.copy(self.hT[:, :, t * P:(t + 1) * P], self.pt[:, t % 2, :, :]).then_inc(self.s_hT, 1)


def latent_inputs(nc, io, consts, kt):
    X, ident = consts["X"], consts["ident"]
    with ExitStack() as ctx:
        sb, ps, sem = scope(nc, ctx, "li")
        norm = Norm(nc, ctx, "li", X, ident)
        wqd = sb("wqd", [P, KD, QL])
        wkv = sb("wkv", [P, KD, P])
        cosk = sb("cosk", [P, NT, 32])
        sink = sb("sink", [P, NT, 32])
        kv = sb("kv", [P, NT, P])
        ktok = sb("ktok", [P, NT, 192])
        cq = sb("cq", [QC, 2, T])
        tmp = sb("tmp", [P, 4, NT, 32])
        maskf = sb("maskf", [P, P])
        pkv = ps("pkv", [P, 2, 512])
        pcq = ps("pcq", [P, 2, 512])
        pk = ps("pk", [P, 2, 4, P])

        x_loaded = [sem(f"x_loaded{c}") for c in range(4)]
        const_loaded, mask_loaded = sem("const_loaded"), sem("mask_loaded")
        wkv_loaded, wqd_loaded = sem("wkv_loaded"), sem("wqd_loaded")
        table_loaded = sem("table_loaded")
        consts_cast = sem("consts_cast")
        kv_ready, kv_read = sem("kv_ready"), sem("kv_read")
        cq_ready, cq_read, cq_high_ready = sem("cq_ready"), sem("cq_read"), sem("cq_high_ready")
        prod_ready, rope_ready, lat_ready, dup_ready = (
            sem("prod_ready"), sem("rope_ready"), sem("lat_ready"), sem("dup_ready"))
        kT_ready, kT_read = sem("kT_ready"), [sem("kT_read_act"), sem("kT_read_dve")]

        x_in = io["x"].rearrange("b (t p) d -> p (b t) d", p=P)
        block = ctx.enter_context(nc.Block())

        @block.sync
        def _(sp):
            sp.dma_start(ident[:], io["identity"]).then_inc(const_loaded, 16)
            for c in range(4):
                sp.dma_start(X[:, 4 * c:4 * c + 4, :], x_in[:, 4 * c:4 * c + 4, :]).then_inc(x_loaded[c], 16)
                if c == 0:
                    for cols, name in ((slice(0, DR), "w_k_rope"), (slice(DR, P), "w_kv_down")):
                        sp.dma_start(wkv[:, :, cols], io[name].rearrange("(k p) n -> p k n", p=P))\
                            .then_inc(wkv_loaded, 16)
                if c == 1:
                    sp.dma_start(wqd[:], io["w_q_down"].rearrange("(k p) n -> p k n", p=P)).then_inc(wqd_loaded, 16)
            sp.dma_start(maskf[:], io["causal"]).then_inc(mask_loaded, 16)
            sp.dma_start(cosk[:], io["cos_tok"]).then_inc(table_loaded, 16)
            sp.dma_start(sink[:], io["sin_tok"]).then_inc(table_loaded, 16)

        @block.gpsimd
        def _(pool):
            pool.wait_ge(const_loaded, 16)
            pool.tensor_copy(consts["ident_b"][:], ident[:]).then_inc(consts_cast, 1)
            pool.wait_ge(mask_loaded, 16)
            pool.tensor_copy(consts["causal_b"][:], maskf[:]).then_inc(consts_cast, 1)
            for n in range(8):
                c, m = n // 2, n % 2
                cols = slice(c * 512, (c + 1) * 512)
                pool.wait_ge(cq_high_ready, n + 1)
                low_part(pool, kt["cq_low"][:, m, cols], cq[:, m, cols], kt["cq_high"][:, m, cols])

        @block.vector
        def _(dve):
            norm.vector_stats(dve, 0, x_loaded)

            def cq_high(n):
                c, m = n // 2, n % 2
                cols = slice(c * 512, (c + 1) * 512)
                dve.wait_ge(cq_read, n + 1)
                high_part(dve, kt["cq_high"][:, m, cols], cq[:, m, cols]).then_inc(cq_high_ready, 1)

            def read_kv(t):
                dve.wait_ge(kv_ready, t + 1)
                dve.tensor_copy(kv[:, t, :], pkv[:, t % 2, 0:P]).then_inc(kv_read, 1)

            for t in range(NT):
                norm.vector_h(dve, t)
                if norm.stats_behind(t):
                    norm.vector_stats(dve, t // 4 + 1, x_loaded)
                if t >= 2:
                    read_kv(t - 2)
            read_kv(NT - 2)
            read_kv(NT - 1)
            for n in range(4):
                cq_high(n)
            dve.wait_ge(kv_read, NT)
            dve.wait_ge(table_loaded, 32)
            x1, x2 = kv[:, :, 0:32], kv[:, :, 32:64]
            for n, (a, b) in enumerate(((x1, cosk), (x2, sink), (x1, sink), (x2, cosk))):
                dve.tensor_tensor(tmp[:, n], a, b[:], ALU.mult).then_inc(prod_ready, 1)
            for half, op in ((0, ALU.subtract), (1, ALU.add)):
                dve.wait_ge(prod_ready, 2 + 2 * half)
                to = ktok[:, :, 0:DR].rearrange("p t (q h i) -> p t q h i", q=2, h=2)[:, :, :, half, :]
                a, b = (tmp[:, 2 * half + n].rearrange("p t (q i) -> p t q i", q=2) for n in range(2))
                for q in range(2):
                    last = dve.tensor_tensor(to[:, :, q, :], a[:, :, q, :], b[:, :, q, :], op)
                    last.then_inc(rope_ready, 1)
            for n in range(4, 8):
                cq_high(n)
            for n in range(8):
                if n % 2:
                    dve.wait_ge(kT_ready, n + 1)
                    dst = kt["k_rl"] if n < 4 else kt["k_lr"]
                    c = n % 4
                    dve.tensor_copy(dst[:, c * 512:(c + 1) * 512], pk[:, n % 2]).then_inc(kT_read[1], 1)

        @block.scalar
        def _(act):
            norm.scalar_sqrt(act, 0)

            def read_cq(n):
                c, m = n // 2, n % 2
                act.wait_ge(cq_ready, n + 1)
                act.copy(cq[:, m, c * 512:(c + 1) * 512], pcq[0:QC, n % 2, :]).then_inc(cq_read, 1)

            for t in range(NT):
                norm.scalar_hT(act, t)
                if norm.stats_behind(t):
                    norm.scalar_sqrt(act, t // 4 + 1)
                if t % 4 == 2 and t > 4:
                    read_cq(2 * (t // 4) - 2)
                    read_cq(2 * (t // 4) - 1)
            read_cq(6)
            read_cq(7)
            act.wait_ge(kv_read, NT)
            act.copy(ktok[:, :, DR:P], kv[:, :, DR:P]).then_inc(lat_ready, 1)
            act.copy(kt["values"][:], kv[:, :, DR:P])
            act.wait_ge(rope_ready, 4)
            act.copy(ktok[:, :, P:192], ktok[:, :, 0:DR]).then_inc(dup_ready, 1)
            for n in range(0, 8, 2):
                act.wait_ge(kT_ready, n + 1)
                dst = kt["k_rl"] if n < 4 else kt["k_lr"]
                c = n % 4
                act.copy(dst[:, c * 512:(c + 1) * 512], pk[:, n % 2]).then_inc(kT_read[0], 1)

        @block.tensor
        def _(pe):
            def keys(t):
                pe.wait_ge(norm.s_hT, t + 1)
                if t == 0:
                    pe.wait_ge(wkv_loaded, 32)
                if t >= 2:
                    pe.wait_ge(kv_read, t - 1)
                for k in range(KD):
                    last = pe.matmul(pkv[:, t % 2, 0:P], norm.hT[:, k, t * P:(t + 1) * P], wkv[:, k, :],
                                     start=(k == 0), stop=(k == KD - 1))
                last.then_inc(kv_ready, 1)

            def queries(c):
                for m in range(2):
                    n = 2 * c + m
                    if n == 0:
                        pe.wait_ge(wqd_loaded, 16)
                    if n >= 2:
                        pe.wait_ge(cq_read, n - 1)
                    for k in range(KD):
                        last = pe.matmul(pcq[0:QC, n % 2, :], wqd[:, k, m * QC:(m + 1) * QC],
                                         norm.hT[:, k, c * 512:(c + 1) * 512], start=(k == 0), stop=(k == KD - 1))
                    last.then_inc(cq_ready, 1)

            pe.wait_ge(const_loaded, 16)
            for t in range(NT):
                norm.tensor_transpose(pe, t)
                if t >= 1:
                    keys(t - 1)
                if t % 4 == 1 and t > 4:
                    queries(t // 4 - 1)
            keys(NT - 1)
            queries(3)
            pe.wait_ge(lat_ready, 1)
            for n in range(8):
                if n == 0:
                    pe.wait_ge(rope_ready, 4)
                if n == 4:
                    pe.wait_ge(dup_ready, 1)
                if n >= 2:
                    pe.wait_ge(kT_read[n % 2], n // 2)
                off = 0 if n < 4 else DR
                for j in range(4):
                    t = 4 * (n % 4) + j
                    last = pe.transpose(pk[:, n % 2, j, :], ktok[:, t, off:off + P], ident[:])
                last.then_inc(kT_ready, 1)


def attention_loop(nc, consts, shape, tag, turns, side):
    X, ident = consts["X"], consts["ident"]
    sh = shape
    NU, NGR, NK = sh.nu, len(sh.groups), sh.nchunk
    CW = sh.tpc * P
    M = P // sh.heads

    with ExitStack() as ctx:
        sb, ps, sem = scope(nc, ctx, tag)
        prob = sb("prob", [P, RING_P, S])
        assert sh.chunks_per_batch == 2
        probT = [sb(f"probT{c}", [P, sh.heads, (c + 1) * sh.tpc, CW]) for c in range(2)]
        negmax = sb("negmax", [P, RING_P])
        rowsum = sb("rowsum", [P, RING_P])
        rinv = sb("rinv", [P, RING_P])
        head_out = sb("head_out", [P, CW])
        head_high, head_low = (sb(f"head_{n}", [P, 2, CW], F32R) for n in ("high", "low"))
        score = ps("score", [P, 2, S])
        turned = ps("turned", [P, 2, 4, P])
        misc = ps("misc", [P, 2, 512])

        scores_ready = sem("scores_ready")
        negmax_ready = sem("negmax_ready")
        exp_done = sem("exp_done")
        rinv_ready = sem("rinv_ready")
        units_begun = sem("units_begun")
        prob_ready = sem("prob_ready")
        turned_ready = sem("turned_ready")
        read_dve = sem("read_dve")
        read_act = sem("read_act")
        pv_ready = sem("pv_ready")
        head_out_ready, head_high_ready, head_low_ready = (
            sem("head_out_ready"), sem("head_high_ready"), sem("head_low_ready"))
        proj_ready = sem("proj_ready")
        x_added = sem("x_added")

        side.allocate(sb, sem, misc, scores_ready, pv_ready, proj_ready)

        items = list(side.items)
        for k in range(NK):
            at = sh.last_unit(k) + LAG + 1
            items.append((at % NU, "pv", k if at < NU else k - NK))
            for n in range(sh.tpc):
                at = sh.last_unit(k) + LAG + 3 + n
                items.append((at % NU, "proj", k * sh.tpc + n if at < NU else (k - NK) * sh.tpc + n))
        items.sort(key=lambda x: x[0])
        splits = [(at % NU, k if at < NU else k - NK) for k in range(NK) for at in [sh.last_unit(k) + LAG + 2]]
        assert len(items) % 2 == 0

        def skipped(item, first, last):
            return (first and item[2] < 0) or (last and item[1] in side.for_next)

        def place(item):
            return items.index(item)

        prologue = [it for it in items if it[1] in side.for_next]
        wrapped = [it for it in items if it[2] < 0]

        def last_in_bank(item, first, last, draining=False):
            at = len(items) if draining else place(item)
            seq = [(1, it) for it in (prologue if first else items)]
            if draining:
                seq = [(1, it) for it in items if not skipped(it, False, True)]
                seq += [(0, it) for it in wrapped[:wrapped.index(item)]]
            else:
                seq += [(0, it) for it in items[:at] if not skipped(it, first, last)]
            return next((x for x in reversed(seq) if place(x[1]) % 2 == place(item) % 2), None)

        def wait_bank(pe, i, before):
            if before is None:
                return
            back, (_, what, arg) = before
            if what == "pv":
                pe.wait_ge(head_out_ready, (i - back) * NK + arg + 1)
            elif what == "proj":
                pe.wait_ge(x_added, (i - back) * NT + arg + 1)
            else:
                pe.wait_ge(*side.read_out(i - back, what, arg))

        def score_of(s, c0, c1):
            bank = 512 * (s // 2 % 2) if sh.units[s][1] < 4 else 0
            return score[:, s % 2, bank + c0:bank + c1]

        def score_ring(s):
            return 4 if sh.units[s][1] < 4 and s % (TB * sh.heads) >= 2 else 2

        def run(engine, step, drain):
            for s in range(NU):
                step(0, s, True, False)
            with engine.Fori(1, turns - 1) as i:
                for s in range(NU):
                    step(i, s, False, False)
            for s in range(NU):
                step(turns - 1, s, False, True)
            drain(turns)

        block = ctx.enter_context(nc.Block())

        @block.tensor
        def _(pe):
            side.tensor_setup(pe)

            def scores(i, s, first):
                b, t, h = sh.units[s]
                side.tensor_scores_wait(pe, i, s)
                ago = score_ring(s)
                if not (first and s < ago):
                    pe.wait_ge(exp_done, i * NU + s - ago + 1)
                n = (t + 1) * P
                for c0 in range(0, n, 512):
                    c1 = min(c0 + 512, n)
                    lhsT, rhs = side.score_operands(b, t, h, c0, c1)
                    pe.matmul(score_of(s, c0, c1), lhsT, rhs, start=True, stop=(c1 < n))
                pe.matmul(score_of(s, n - P, n), consts["ident_b"][:], consts["causal_b"][:],
                          start=False, stop=True).then_inc(scores_ready, 1)

            def transposes(i, u):
                uu = u % NU
                pe.wait_ge(prob_ready, i * NU + u + 1)
                for g in range(sh.first_group[uu], sh.first_group[uu + 1]):
                    _, j0, j1, _ = sh.groups[g]
                    gg = g if u >= 0 else g - NGR
                    by_act = sh.groups[g - 2][3]
                    if not (isinstance(i, int) and i == 0 and gg < 2):
                        pe.wait_ge(read_act if by_act else read_dve,
                                   i * sh.evacuated(NGR, by_act) + sh.evacuated(gg - 1, by_act))
                    for j in range(j0, j1):
                        last = pe.transpose(turned[:, g % 2, j - j0, :], prob[:, uu % RING_P, j * P:(j + 1) * P],
                                            ident[:])
                    last.then_inc(turned_ready, 1)

            def pv(i, k, bank):
                kk = k % NK
                b, c = divmod(kk, sh.chunks_per_batch)
                end = sh.first_group[sh.last_unit(kk) + 1] - (0 if k >= 0 else NGR)
                pe.wait_ge(read_act, i * sh.evacuated(NGR, True) + sh.evacuated(end, True))
                pe.wait_ge(read_dve, i * sh.evacuated(NGR, False) + sh.evacuated(end, False))
                side.tensor_pv_wait(pe, i, k)
                jn = (c + 1) * sh.tpc
                for j in range(jn):
                    q0 = max(0, j - c * sh.tpc) * P
                    for h in range(sh.heads):
                        last = pe.matmul(misc[h * M:(h + 1) * M, bank, q0:CW], side.value_operand(b, j, h),
                                         probT[kk % 2][:, h, j, q0:CW], start=(j == 0), stop=(j == jn - 1),
                                         skip_group_check=True)
                last.then_inc(pv_ready, 1)

            def proj(i, n, bank):
                k, tt = divmod(n, sh.tpc)
                pe.wait_ge(head_low_ready, i * NK + k + 1)
                side.tensor_proj_wait(pe, i, n)
                heads = [part[:, k % 2, tt * P:(tt + 1) * P] for part in (head_high, head_low)]
                split_products(pe, misc[:, bank, :], [(heads, [part[:] for part in side.out_w_parts])])\
                    .then_inc(proj_ready, 1)

            def do(item, i, first, last):
                wait_bank(pe, i, last_in_bank(item, first, last))
                bank = place(item) % 2
                if item[1] == "pv":
                    pv(i, item[2], bank)
                elif item[1] == "proj":
                    proj(i, item[2], bank)
                else:
                    side.tensor_item(pe, i, item[1], item[2], bank)

            def step(i, s, first, last):
                scores(i, s, first)
                if s >= LAG or not first:
                    transposes(i, s - LAG)
                for item in items:
                    if item[0] == s and not skipped(item, first, last):
                        do(item, i, first, last)

            for n, item in enumerate(prologue):
                same = [(0, it) for it in prologue[:n] if place(it) % 2 == place(item) % 2]
                wait_bank(pe, -1, same[-1] if same else None)
                side.tensor_item(pe, -1, item[1], item[2], place(item) % 2)

            def drain(end):
                for s in range(LAG + 3 + sh.tpc):
                    if s < LAG:
                        transposes(end, s - LAG)
                    for item in wrapped:
                        if item[0] == s:
                            wait_bank(pe, end, last_in_bank(item, False, False, draining=True))
                            (pv if item[1] == "pv" else proj)(end, item[2], place(item) % 2)

            run(pe, step, drain)

        def read_out(eng, copy, i, u, by_act):
            uu = u % NU
            k = sh.chunk_of(uu)
            _, t, h = sh.units[uu]
            for g in range(sh.first_group[uu], sh.first_group[uu + 1]):
                _, j0, j1, act_has = sh.groups[g]
                if act_has != by_act:
                    continue
                gg = g if u >= 0 else g - NGR
                kk = k if u >= 0 else k - NK
                eng.wait_ge(turned_ready, i * NGR + gg + 1)
                if not (isinstance(i, int) and i == 0 and kk < 2):
                    eng.wait_ge(pv_ready, i * NK + kk - 1)
                q0 = (t % sh.tpc) * P
                copy(probT[k % 2][:, h, j0:j1, q0:q0 + P],
                     turned[:, g % 2, 0:j1 - j0, :]).then_inc(read_act if by_act else read_dve, 1)

        @block.vector
        def _(dve):
            side.vector_setup(dve)

            def evacuate(i, u):
                read_out(dve, dve.tensor_copy, i, u, False)

            def step(i, s, first, last):
                b, t, h = sh.units[s]
                n = (t + 1) * P
                if s >= 1 or not first:
                    recip(i, s - 1)
                dve.wait_ge(scores_ready, i * NU + s + 1)
                dve.reduce_max(negmax[:, s % RING_P:s % RING_P + 1], score_of(s, 0, n), AX,
                               negate=True).then_inc(negmax_ready, 1)
                if s >= LAG or not first:
                    evacuate(i, s - LAG)
                for at, k in splits:
                    if at == s and not (first and k < 0):
                        head_split(i, k)
                side.vector_step(dve, i, s)
                for item in items:
                    if item[0] == s and not skipped(item, first, last):
                        if item[1] == "proj":
                            add(i, item)
                        else:
                            side.vector_item(dve, i, item[1], item[2], place(item) % 2)

            def recip(i, u):
                dve.wait_ge(exp_done, i * NU + u + 1)
                r = u % RING_P
                dve.reciprocal(rinv[:, r:r + 1], rowsum[:, r:r + 1]).then_inc(rinv_ready, 1)

            def head_split(i, k):
                dve.wait_ge(head_out_ready, i * NK + k + 1)
                high_part(dve, head_high[:, k % 2, :], head_out[:]).then_inc(head_high_ready, 1)

            def add(i, item):
                n = item[2]
                tile = X[:, n % NT, :]
                dve.wait_ge(proj_ready, i * NT + n + 1)
                if not (isinstance(i, int) and i * NT + n == 0):
                    dve.wait_ge(x_added, i * NT + n)
                bank = place(item) % 2
                dve.tensor_tensor(tile, tile, misc[:, bank, :], ALU.add).then_inc(x_added, 1)

            for item in prologue:
                side.vector_item(dve, -1, item[1], item[2], place(item) % 2)

            def drain(end):
                for s in range(LAG + 3 + sh.tpc):
                    if s == 0:
                        recip(end, -1)
                    if s < LAG:
                        evacuate(end, s - LAG)
                    for at, k in splits:
                        if at == s and k < 0:
                            head_split(end, k)
                    for item in wrapped:
                        if item[0] == s and item[1] == "proj":
                            add(end, item)

            run(dve, step, drain)

        @block.scalar
        def _(act):
            side.scalar_setup(act)

            def head_copy(i, item):
                k = item[2]
                bank = place(item) % 2
                act.wait_ge(pv_ready, i * NK + k + 1)
                if not (isinstance(i, int) and i == 0 and k < 2):
                    act.wait_ge(proj_ready, i * NT + (k - 1) * sh.tpc)
                if not (isinstance(i, int) and i * NK + k == 0):
                    act.wait_ge(head_low_ready, i * NK + k)
                act.copy(head_out[:], misc[:, bank, 0:CW]).then_inc(head_out_ready, 1)

            def step(i, s, first, last):
                b, t, h = sh.units[s]
                n = (t + 1) * P
                r = s % RING_P
                act.wait_ge(negmax_ready, i * NU + s + 1)
                if not (first and s < RING_P):
                    act.wait_ge(turned_ready, i * NGR + turned_by(s - RING_P))
                act.activation(prob[:, r, 0:n], score_of(s, 0, n), ACT.Exp, bias=negmax[:, r:r + 1],
                               accum_out=rowsum[:, r:r + 1]).then_inc(exp_done, 1)
                if s >= LAG or not first:
                    read_out(act, act.copy, i, s - LAG, True)
                for item in items:
                    if item[0] == s and not skipped(item, first, last):
                        if item[1] == "pv":
                            head_copy(i, item)
                        else:
                            side.scalar_item(act, i, item[1], item[2], place(item) % 2)

            def turned_by(u):
                return sh.first_group[u % NU + 1] - (0 if u >= 0 else NGR)

            for item in prologue:
                side.scalar_item(act, -1, item[1], item[2], place(item) % 2)

            def drain(end):
                for s in range(LAG + 3 + sh.tpc):
                    if s < LAG:
                        read_out(act, act.copy, end, s - LAG, True)
                    for item in wrapped:
                        if item[0] == s and item[1] == "pv":
                            head_copy(end, item)

            run(act, step, drain)

        @block.gpsimd
        def _(pool):
            side.gpsimd_setup(pool)

            def normalise(i, u):
                uu = u % NU
                n = (sh.units[uu][1] + 1) * P
                r = uu % RING_P
                pool.wait_ge(rinv_ready, i * NU + u + 1)
                pool.sem_inc(units_begun, 1)
                pool.tensor_scalar(prob[:, r, 0:n], prob[:, r, 0:n], rinv[:, r:r + 1], 1.0,
                                   ALU.mult, ALU.mult).then_inc(prob_ready, 1)

            def head_split(i, k):
                pool.wait_ge(head_high_ready, i * NK + k + 1)
                low_part(pool, head_low[:, k % 2, :], head_out[:], head_high[:, k % 2, :]).then_inc(head_low_ready, 1)

            def step(i, s, first, last):
                if s >= 1 or not first:
                    normalise(i, s - 1)
                for at, k in splits:
                    if at == s and not (first and k < 0):
                        head_split(i, k)
                for item in items:
                    if item[0] == s and not skipped(item, first, last):
                        side.gpsimd_item(pool, i, item[1], item[2])
                side.gpsimd_step(pool, i, s, first, last)

            for item in prologue:
                side.gpsimd_item(pool, -1, item[1], item[2])

            def drain(end):
                normalise(end, -1)
                for _, k in splits:
                    if k < 0:
                        head_split(end, k)

            run(pool, step, drain)

        @block.sync
        def _(sp):
            side.loads(sp, turns)


class LatentSide:

    for_next = ("nopeT", "fold_q", "rope0", "lat0")
    items = [(1, "rope", 2), (2, "lat", 2), (3, "rope", 3), (4, "lat", 3), (9, "fold_v", 0),
             (9, "nopeT", 0), (10, "nopeT", 1), (16, "fold_q", 0),
             (18, "rope0", 0), (20, "lat0", 0), (22, "rope0", 1), (24, "lat0", 1)]

    def __init__(self, nc, io, consts, kt):
        self.nc, self.io, self.consts, self.kt = nc, io, consts, kt

    def allocate(self, sb, sem, misc, scores_ready, pv_ready, proj_ready):
        self.misc, self.scores_ready = misc, scores_ready
        self.proj_ready = proj_ready
        self.q = sb("q", [P, 2, T])
        self.w_nope = sb("w_nope", [QC, 2, 2 * DN])
        self.w_rope = sb("w_rope", [QC, 2, P])
        self.wuk = sb("wuk", [P, 2, KVL])
        self.wuv = sb("wuv", [P, 2, KVL])
        self.wo = sb("wo", [P, 2, D])
        self.nopeT = sb("nopeT", [P, 2, 2, QC])
        self.w_lat = sb("w_lat", [QC, 2, P])
        self.w_rope_parts = [sb(f"w_rope_{n}", [QC, 2, P], F32R) for n in ("high", "low")]
        self.w_lat_parts = [sb(f"w_lat_{n}", [QC, 2, P], F32R) for n in ("high", "low")]
        self.out_w = sb("out_w", [P, D])
        self.out_w_parts = [sb(f"out_w_{n}", [P, D], F32R) for n in ("high", "low")]
        self.cosq = sb("cosq", [P, S])
        self.sinq = sb("sinq", [P, S])
        self.partner = sb("partner", [P, 512])
        self.cosine = sb("cosine", [P, 512])
        self.tables = sem("tables")
        self.n_loaded, self.r_loaded, self.v_loaded = sem("n_loaded"), sem("r_loaded"), sem("v_loaded")
        self.nopeT_ready, self.nopeT_read = sem("nopeT_ready"), sem("nopeT_read")
        self.fold_q_ready, self.w_lat_ready = sem("fold_q_ready"), sem("w_lat_ready")
        self.fold_v_ready, self.out_w_ready = sem("fold_v_ready"), sem("out_w_ready")
        self.rope_ready, self.lat_ready = sem("rope_ready"), sem("lat_ready")
        self.w_rope_split, self.w_lat_split, self.out_w_split = sem("w_rope_split"), sem("w_lat_split"), sem("out_w_split")
        self.partner_ready, self.cosine_ready = sem("partner_ready"), sem("cosine_ready")
        self.sine_done, self.q_rope_done, self.q_lat_done = sem("sine_done"), sem("q_rope_done"), sem("q_lat_done")

    @staticmethod
    def chunk(i, what, c):
        return (i + 1, c) if what.endswith("0") else (i, c)

    def read_out(self, i, what, c):
        if what == "nopeT":
            return self.nopeT_read, 2 * (i + 1) + c + 1
        if what == "fold_q":
            return self.w_lat_ready, i + 2
        if what == "fold_v":
            return self.out_w_ready, i + 1
        pair, c = self.chunk(i, what, c)
        if what.startswith("rope"):
            return self.partner_ready, 4 * pair + c + 1
        return self.q_lat_done, 8 * pair + 2 * c + 2

    def loads(self, sp, turns):
        io = self.io

        def load_n(pair):
            sp.dma_start(self.w_nope[:], io["w_q_up_nope"].rearrange("(k p) n -> p k n", p=QC)
                         [:, :, bass.ds(pair * 2 * DN, 2 * DN)]).then_inc(self.n_loaded, 16)
            sp.dma_start(self.wuk[:], io["w_uk"][bass.ds(pair * 2 * DN, 2 * DN), :]
                         .rearrange("(h p) r -> p h r", p=P)).then_inc(self.n_loaded, 16)

        def load_r(pair):
            src = io["w_q_up_rope"].rearrange("(k p) n -> p k n", p=QC)[:, :, bass.ds(pair * P, P)]
            src = src.rearrange("p k (h f q i) -> p k h f q i", h=2, f=2, q=2)
            dst = self.w_rope[:].rearrange("p k (h q f i) -> p k h q f i", h=2, f=2, q=2)
            for h in range(2):
                for f in range(2):
                    for q in range(2):
                        sp.dma_start(dst[:, :, h, q, f, :], src[:, :, h, f, q, :]).then_inc(self.r_loaded, 16)

        def load_v(pair):
            sp.dma_start(self.wuv[:], io["w_uv"][bass.ds(pair * 2 * DV, 2 * DV), :]
                         .rearrange("(h p) r -> p h r", p=P)).then_inc(self.v_loaded, 16)
            sp.dma_start(self.wo[:], io["w_out"][bass.ds(pair * 2 * DV, 2 * DV), :]
                         .rearrange("(h p) r -> p h r", p=P)).then_inc(self.v_loaded, 16)

        load_n(0)
        load_r(0)
        sp.dma_start(self.cosq[:], io["cos_rows"]).then_inc(self.tables, 16)
        sp.dma_start(self.sinq[:], io["sin_rows"]).then_inc(self.tables, 16)
        load_v(0)
        with sp.Fori(0, turns - 1) as i:
            sp.wait_ge(self.fold_q_ready, i + 1)
            load_n(i + 1)
            sp.wait_ge(self.rope_ready, 4 * i + 4)
            load_r(i + 1)
            sp.wait_ge(self.fold_v_ready, i + 1)
            load_v(i + 1)

    def tensor_setup(self, pe):
        pass

    def vector_setup(self, dve):
        pass

    def scalar_setup(self, act):
        pass

    def gpsimd_setup(self, pool):
        pass

    def gpsimd_step(self, pool, i, s, first, last):
        pass

    def tensor_scores_wait(self, pe, i, s):
        if s % 8 == 0:
            pe.wait_ge(self.q_rope_done, 8 * i + 2 * (s // 8) + 2)
            pe.wait_ge(self.q_lat_done, 8 * i + 2 * (s // 8) + 2)

    def score_operands(self, b, t, h, c0, c1):
        keys = self.kt["k_rl"] if h == 0 else self.kt["k_lr"]
        return self.q[:, h, b * S + t * P:b * S + (t + 1) * P], keys[:, b * S + c0:b * S + c1]

    def tensor_pv_wait(self, pe, i, k):
        pass

    def value_operand(self, b, j, h):
        return self.kt["values"][:, b * TB + j, :]

    def tensor_proj_wait(self, pe, i, n):
        if n == 0:
            pe.wait_ge(self.out_w_split, 2 * i + 2)

    def tensor_item(self, pe, i, what, c, bank):
        misc = self.misc
        if what == "nopeT":
            pe.wait_ge(self.n_loaded, 32 * (i + 1) + 32)
            for k in range(2):
                last = pe.transpose(misc[:, bank, k * QC:(k + 1) * QC], self.w_nope[:, k, c * DN:(c + 1) * DN],
                                    self.consts["ident"][0:QC, 0:QC])
            last.then_inc(self.nopeT_ready, 1)
        elif what == "fold_q":
            pe.wait_ge(self.nopeT_read, 2 * (i + 1) + 2)
            for k in range(2):
                for h in range(2):
                    at = k * P + (1 - h) * KVL
                    last = pe.matmul(misc[0:QC, bank, at:at + KVL], self.nopeT[:, h, k, :], self.wuk[:, h, :],
                                     start=True, stop=True)
            last.then_inc(self.fold_q_ready, 1)
        elif what == "fold_v":
            pe.wait_ge(self.v_loaded, 32 * i + 32)
            for h in range(2):
                last = pe.matmul(misc[h * KVL:(h + 1) * KVL, bank, :], self.wuv[:, h, :], self.wo[:, h, :],
                                 start=True, stop=True, skip_group_check=True)
            last.then_inc(self.fold_v_ready, 1)
        else:
            pair, c = self.chunk(i, what, c)
            rope = what.startswith("rope")
            pe.wait_ge(self.w_rope_split if rope else self.w_lat_split, 2 * pair + 2)
            w = self.w_rope_parts if rope else self.w_lat_parts
            cq = (self.kt["cq_high"], self.kt["cq_low"])
            last = split_products(pe, misc[:, bank, :], [([part[:, k, :] for part in w],
                                                          [part[:, k, c * 512:(c + 1) * 512] for part in cq])
                                                         for k in range(2)])
            last.then_inc(self.rope_ready if rope else self.lat_ready, 1)

    def split(self, dve, w, parts, done, pair):
        high_part(dve, parts[0][:], w[:]).then_inc(done, 1)
        dve.wait_ge(done, 2 * pair + 1)
        low_part(dve, parts[1][:], w[:], parts[0][:]).then_inc(done, 1)

    def vector_step(self, dve, i, s):
        if s == 11:
            dve.wait_ge(self.out_w_ready, i + 1)
            self.split(dve, self.out_w, self.out_w_parts, self.out_w_split, i)

    def vector_item(self, dve, i, what, c, bank):
        if what == "fold_q":
            dve.wait_ge(self.r_loaded, 128 * (i + 1) + 128)
            if not (isinstance(i, int) and i == -1):
                dve.wait_ge(self.rope_ready, 4 * i + 4)
            self.split(dve, self.w_rope, self.w_rope_parts, self.w_rope_split, i + 1)
        if what == "rope0" and c == 0:
            dve.wait_ge(self.w_lat_ready, i + 2)
            self.split(dve, self.w_lat, self.w_lat_parts, self.w_lat_split, i + 1)
        if not what.startswith("rope"):
            return
        pair, c = self.chunk(i, what, c)
        n = pair * 4 + c
        first = isinstance(n, int) and n == 0
        if first:
            dve.wait_ge(self.tables, 32)
        else:
            dve.wait_ge(self.q_rope_done, 2 * n)
        dve.wait_ge(self.rope_ready, n + 1)
        cc = c % 2
        dve.tensor_tensor(self.cosine[:], self.misc[:, bank, :], self.cosq[:, cc * 512:(cc + 1) * 512], ALU.mult)\
           .then_inc(self.cosine_ready, 1)
        dve.stream_shuffle(self.partner[:], self.misc[:, bank, :], [(r + 16) % 32 for r in range(32)])\
           .then_inc(self.partner_ready, 1)

    def gpsimd_item(self, pool, i, what, c):
        if not what.startswith("rope"):
            return
        pair, c = self.chunk(i, what, c)
        n = pair * 4 + c
        cc = c % 2
        pool.wait_ge(self.partner_ready, n + 1)
        if isinstance(n, int) and n == 0:
            pool.wait_ge(self.tables, 32)
        pool.tensor_tensor(self.partner[:], self.partner[:], self.sinq[:, cc * 512:(cc + 1) * 512], ALU.mult)\
            .then_inc(self.sine_done, 1)
        pool.wait_ge(self.sine_done, n + 1)
        pool.wait_ge(self.cosine_ready, n + 1)
        self.wait_q_free(pool, pair, c)
        for h in range(2):
            rows = slice(h * DR, (h + 1) * DR)
            pool.tensor_tensor(self.q[rows, h, c * 512:(c + 1) * 512], self.cosine[rows, :], self.partner[rows, :],
                               ALU.add).then_inc(self.q_rope_done, 1)
        pool.wait_ge(self.q_rope_done, 2 * n + 2)

    def wait_q_free(self, eng, pair, c):
        if not (isinstance(pair, int) and pair == 0):
            eng.wait_ge(self.scores_ready, pair * 32 - 32 + 16 * (c // 2) + 16)

    def scalar_item(self, act, i, what, c, bank):
        misc = self.misc
        if what == "nopeT":
            n = (i + 1) * 2 + c
            act.wait_ge(self.nopeT_ready, n + 1)
            if not (isinstance(i, int) and i == -1):
                act.wait_ge(self.fold_q_ready, i + 1)
            act.copy(self.nopeT[:, c].rearrange("p k n -> p (k n)"), misc[:, bank, 0:2 * QC]).then_inc(
                self.nopeT_read, 1)
        elif what == "fold_q":
            act.wait_ge(self.fold_q_ready, i + 2)
            if not (isinstance(i, int) and i == -1):
                act.wait_ge(self.lat_ready, 4 * i + 4)
            act.copy(self.w_lat[:], misc[0:QC, bank, 0:2 * P].rearrange("p (k n) -> p k n", k=2)).then_inc(
                self.w_lat_ready, 1)
        elif what == "fold_v":
            act.wait_ge(self.fold_v_ready, i + 1)
            if not (isinstance(i, int) and i == 0):
                act.wait_ge(self.proj_ready, i * NT)
            act.copy(self.out_w[:], misc[:, bank, :]).then_inc(self.out_w_ready, 1)
        elif what.startswith("lat"):
            pair, c = self.chunk(i, what, c)
            n = pair * 4 + c
            act.wait_ge(self.lat_ready, n + 1)
            self.wait_q_free(act, pair, c)
            for h in range(2):
                rows = slice((1 - h) * KVL, (2 - h) * KVL)
                act.mul(self.q[rows, h, c * 512:(c + 1) * 512], misc[rows, bank, :], SCALE_A)\
                    .then_inc(self.q_lat_done, 1)


def latent_attention(nc, io, consts, kt):
    shape = Shape(2, 4, lambda n, u, j0, j1: n % 4 != 0)
    attention_loop(nc, consts, shape, "la", PAIRS, LatentSide(nc, io, consts, kt))


class Grouped:

    CW = 512
    CT = CW // P
    LAGQ = 3
    ZT = 8
    QUAD_COST, PIECE_COST = 1400, 64
    RING_Q = 4


MAXIMA = [(t, h, half) for t in (0, 7, 1, 6, 2, 5, 3, 4) for h in range(REP) for half in range(1 if t < 4 else 2)]
QUADS = [(c, j) for c in range(S // Grouped.CW) for j in range(Grouped.CT * (c + 1))]


def spread_maxima():
    n, zt = len(QUADS), Grouped.ZT
    window = list(range(zt + 1, n)) + list(range(zt))
    room = {z: Grouped.QUAD_COST + min(Grouped.CW, (QUADS[z][0] + 1) * Grouped.CW - QUADS[z][1] * P) for z in window}
    cost = [min(512, (t - 3) * P if half else (t + 1) * P) + Grouped.PIECE_COST for t, _, half in MAXIMA]
    at, p = {}, 0
    for x, z in enumerate(window):
        end = sum(cost) * sum(room[y] for y in window[:x + 1]) / sum(room.values())
        q = p
        while q < len(MAXIMA) and (x == len(window) - 1 or sum(cost[:q + 1]) <= end):
            q += 1
        at[z] = range(p, q)
        p = q
    return at


def grouped_attention(nc, io, consts, vtok, scratch):
    X, ident_b, causal_b = consts["X"], consts["ident_b"], consts["causal_b"]
    q3, k3, heads_d = scratch
    g = Grouped
    NQ, NM, CT, CW = len(QUADS), len(MAXIMA), g.CT, g.CW
    NP2 = NQ * REP
    RB = 3
    maxima_at, ZT = spread_maxima(), g.ZT
    assert NM % RB == 0 and NP2 % RB == 0 and NQ % g.RING_Q == 0

    with ExitStack() as ctx:
        sb, ps, sem = scope(nc, ctx, "ga")
        q1, q2 = (sb(f"q{n}", [99, NB, REP, S], BF16) for n in (1, 2))
        k1, k2 = (sb(f"k{n}", [99, NB, S], BF16) for n in (1, 2))
        v = sb("v", [P, NB, TB, 32])
        out_w = sb("out_w", [P, KD, D])
        heads_all = sb("heads_all", [P, KD, T])
        prob = sb("prob", [P, g.RING_Q, REP, CW])
        mx = sb("mx", [P, REP, TB])
        mx_far = sb("mx_far", [P, REP, TB // 2])
        neg_rest = sb("neg_rest", [P, REP * TB])
        neg_parts = sb("neg_parts", [P, 3, REP * TB], BF16)
        neg_rows = sb("neg_rows", [3 * REP * TB, P], BF16)
        turned = sb("turned", [P, CW // 32, 32])
        inverse = sb("inverse", [P, CW // 32])
        heads = sb("heads", [P, 2, CW])
        s1 = ps("s1", [P, RB, 512])
        s2 = ps("s2", [P, RB, 512])
        ov = ps("ov", [P, 2, 512])

        loaded1, loaded2, stored, heads_loaded = (
            [sem(f"{n}{b}") for b in range(NB)] for n in ("loaded1_", "loaded2_", "stored", "heads_loaded"))
        w_loaded, late_loaded = sem("w_loaded"), [sem("late_loaded0"), sem("late_loaded1")]
        zeroed, v_ready = sem("zeroed"), sem("v_ready")
        s1_ready, s1_read, mx_step = sem("s1_ready"), sem("s1_read"), sem("mx_step")
        neg_turned, neg_copied, neg_placed = sem("neg_turned"), sem("neg_copied"), sem("neg_placed")
        s2_ready, prob_ready, pv_done = sem("s2_ready"), sem("prob_ready"), sem("pv_done")
        turned_ready, inverse_ready, divided, heads_ready = (
            sem("turned_ready"), sem("inverse_ready"), sem("divided"), sem("heads_ready"))
        proj_ready, x_added = sem("proj_ready"), sem("x_added")

        def run(engine, body):
            body(0, True, False)
            with engine.Fori(1, G - 1) as i:
                body(i, False, False)
            body(G - 1, False, True)

        def ahead(i, b, z, first, last):
            if z == ZT or (last and (b == 1 or z > ZT)):
                return []
            step = 2 if z > ZT else 1
            return [(2 * i + b + step, i + (b + step) // 2, (b + step) % 2, p) for p in maxima_at[z]]

        ahead_of_all = [(0, 0, 0, p) for p in range(NM)], [(1, 0, 1, p) for z in range(ZT + 1, NQ) for p in maxima_at[z]]

        block = ctx.enter_context(nc.Block())

        @block.sync
        def _(sp):
            def load(q, k, i, b, landed):
                cols = slice(b * S, (b + 1) * S)
                for n, (qp, kp) in enumerate(((0, 0), (0, 1), (0, 2), (1, 0), (1, 1), (2, 0))):
                    rows = slice(n * HD, (n + 1) * HD)
                    sp.dma_start(q[rows, b], q3[qp, bass.ds(i * REP * HD, REP * HD), cols]
                                 .rearrange("(h d) t -> d h t", d=HD)).then_inc(landed, 16)
                    sp.dma_start(k[rows, b], k3[kp, bass.ds(b * G + i, 1)].rearrange("a d t -> (a d) t"))\
                        .then_inc(landed, 16)

            def store(i, b, back):
                ii, bb, c = (i, b, 0) if back == 0 else (i, 0, 1) if b else (i - 1, 1, 1)
                sp.wait_ge(heads_ready, 4 * i + 2 * b - back + 1)
                for h in range(REP):
                    sp.dma_start(heads_d[bass.ds((ii * REP + h) * HD, HD), bb * S + c * CW:bb * S + (c + 1) * CW],
                                 heads[32 * h:32 * h + HD, c, :]).then_inc(stored[c], 16)

            def load_last_rows(cols, landed):
                sp.dma_start(heads_all[P // 2:, KD - 1, cols], heads_d[D - P // 2:, cols]).then_inc(landed, 16)

            def load_earlier_rows():
                sp.wait_ge(stored[0], 64 * (2 * G - 1))
                sp.wait_ge(stored[1], 64 * (2 * G - 2))
                for b in range(NB):
                    cols = slice(b * S, (b + 1) * S)
                    sp.dma_start(heads_all[:, 0:KD - 1, cols],
                                 heads_d[0:D - P, cols].rearrange("(k p) t -> p k t", p=P))\
                        .then_inc(heads_loaded[b], 16)
                    sp.dma_start(heads_all[0:P // 2, KD - 1, cols], heads_d[D - P:D - P // 2, cols])\
                        .then_inc(heads_loaded[b], 16)

            load(q1, k1, 0, 0, loaded1[0])
            load(q1, k1, 0, 1, loaded1[1])
            load(q2, k2, 0, 0, loaded2[0])
            load(q2, k2, 0, 1, loaded2[1])
            sp.dma_start(out_w[:], io["b_Wo"].rearrange("(k p) n -> p k n", p=P)).then_inc(w_loaded, 16)

            def body(i, first, last):
                for b in range(NB):
                    if not (first and b == 0):
                        store(i, b, 1)
                    if last and b == 1:
                        sp.wait_ge(stored[1], 64 * (2 * G - 1))
                        load_last_rows(slice(0, S), heads_loaded[0])
                    if not last:
                        sp.wait_ge(s1_ready, 2 * NM * i + NM * (b + 1))
                        load(q1, k1, i + 1, b, loaded1[b])
                    store(i, b, 0)
                    if not last:
                        sp.wait_ge(s2_ready, 2 * NP2 * i + NP2 * (b + 1))
                        load(q2, k2, i + 1, b, loaded2[b])
                    if last and b == 0:
                        load_earlier_rows()

            run(sp, body)
            sp.wait_ge(stored[0], 64 * 2 * G)
            load_last_rows(slice(S, S + CW), late_loaded[0])
            store(G, 0, 1)
            sp.wait_ge(stored[1], 64 * 2 * G)
            load_last_rows(slice(S + CW, T), late_loaded[1])

        @block.gpsimd
        def _(pool):
            def values(i, b):
                pool.tensor_copy(v[:, b, :, 0:HD], vtok[:, bass.ds(b * G + i, 1)]
                                 .rearrange("p a t d -> p (a t) d")).then_inc(v_ready, 1)

            pool.memset(v[:], 1.0).then_inc(zeroed, 1)
            pool.wait_ge(zeroed, 1)
            pool.memset(k2[96:99], 1.0).then_inc(zeroed, 1)
            pool.wait_ge(zeroed, 2)
            values(0, 0)

            def divide(i, b, back):
                k = 4 * i + 2 * b - back
                pool.wait_ge(inverse_ready, k + 1)
                pool.tensor_tensor(turned[:], turned[:], inverse[:, :, None].to_broadcast([P, CW // 32, 32]),
                                   ALU.mult).then_inc(divided, 1)

            def body(i, first, last):
                for b in range(NB):
                    if not (first and b == 0):
                        divide(i, b, 1)
                    if not (last and b == 1):
                        if not (first and b == 0):
                            pool.wait_ge(pv_done, (2 * i + b) * NQ)
                        values(i + b, 1 - b)
                    divide(i, b, 0)

            run(pool, body)
            divide(G, 0, 1)

        @block.vector
        def _(dve):
            def maximum(n, i, b, p):
                t, h, half = MAXIMA[p]
                if p == 0 and not (isinstance(n, int) and n == 0):
                    dve.wait_ge(mx_step, 4 * n)
                to = mx_far[:, h, t - 4:t - 3] if half else mx[:, h, t:t + 1]
                cols = min(512, (t + 1) * P) if not half else (t - 3) * P
                dve.wait_ge(s1_ready, n * NM + p + 1)
                dve.reduce_max(to, s1[:, p % RB, 0:cols], AX).then_inc(s1_read, 1)

            def negate(n):
                flat = mx[:].rearrange("p h t -> p (h t)")
                if not (isinstance(n, int) and n == 0):
                    dve.wait_ge(neg_turned, n)
                dve.wait_ge(s1_read, n * (NM + 1) + NM)
                dve.tensor_tensor(mx[:, :, 4:8], mx[:, :, 4:8], mx_far[:], ALU.max).then_inc(s1_read, 1)
                dve.wait_ge(s1_read, (n + 1) * (NM + 1))
                dve.tensor_scalar(neg_parts[:, 0], flat, -1.0, None, ALU.mult).then_inc(mx_step, 1)
                dve.wait_ge(mx_step, 4 * n + 1)
                dve.scalar_tensor_tensor(neg_rest[:], flat, -1.0, neg_parts[:, 0], ALU.mult, ALU.subtract)\
                   .then_inc(mx_step, 1)
                dve.wait_ge(mx_step, 4 * n + 2)
                dve.tensor_copy(neg_parts[:, 1], neg_rest[:]).then_inc(mx_step, 1)
                dve.wait_ge(mx_step, 4 * n + 3)
                dve.tensor_tensor(neg_parts[:, 2], neg_rest[:], neg_parts[:, 1], ALU.subtract).then_inc(mx_step, 1)

            def turn_heads(i, b, back):
                k = 4 * i + 2 * b - back
                dve.wait_ge(pv_done, (2 * i + b) * NQ + (CT if back == 0 else 0))
                dve.transpose(turned[:].rearrange("p a c -> p (a c)"), ov[:, back, :]).then_inc(turned_ready, 1)
                dve.wait_ge(turned_ready, k + 1)
                dve.reciprocal(inverse[:], turned[:, :, HD]).then_inc(inverse_ready, 1)

            def turn_back(i, b, back):
                k = 4 * i + 2 * b - back
                if not (isinstance(k, int) and k < 2):
                    dve.wait_ge(stored[back], 64 * (2 * i + b - back))
                dve.wait_ge(divided, k + 1)
                dve.transpose(heads[:, back, :], turned[:].rearrange("p a c -> p (a c)")).then_inc(heads_ready, 1)

            def add_projection(tile):
                dve.wait_ge(proj_ready, tile + 1)
                dve.tensor_tensor(X[:, tile, :], X[:, tile, :], s1[:, tile % RB, :], ALU.add).then_inc(x_added, 1)

            for piece in ahead_of_all[0]:
                maximum(*piece)
            negate(0)
            for piece in ahead_of_all[1]:
                maximum(*piece)

            def body(i, first, last):
                for b in range(NB):
                    n = 2 * i + b
                    for z in range(NQ):
                        for piece in ahead(i, b, z, first, last):
                            maximum(*piece)
                        if z == ZT and not (last and b == 1):
                            negate(n + 1)
                        if z == 2 and not (first and b == 0):
                            turn_heads(i, b, 1)
                        if z == 3 and not (first and b == 0):
                            turn_back(i, b, 1)
                        if z == 6:
                            turn_heads(i, b, 0)
                        if z == 7:
                            turn_back(i, b, 0)
                        if last and b == 1 and z >= NQ - TB:
                            add_projection(z - (NQ - TB))

            run(dve, body)
            turn_heads(G, 0, 1)
            turn_back(G, 0, 1)
            for tile in range(TB, NT):
                add_projection(tile)

        @block.scalar
        def _(act):
            def weights(i, b, z):
                c, j = QUADS[z]
                q0 = max(0, j - CT * c) * P
                n = 2 * i + b
                if not (isinstance(n, int) and n == 0 and z < g.RING_Q):
                    act.wait_ge(pv_done, n * NQ + z - g.RING_Q + 1)
                for h in range(REP):
                    p = z * REP + h
                    act.wait_ge(s2_ready, n * NP2 + p + 1)
                    act.activation(prob[:, z % g.RING_Q, h, q0:CW], s2[:, p % RB, q0:CW], ACT.Exp)\
                       .then_inc(prob_ready, 1)

            def place_maxima(n, b):
                act.wait_ge(neg_turned, n + 1)
                if not (isinstance(n, int) and n == 0):
                    act.wait_ge(neg_placed, 48 * n)
                act.copy(neg_rows[:], s1[0:3 * REP * TB, 0, 0:P // 2].bitcast(BF16)).then_inc(neg_copied, 1)
                act.wait_ge(neg_copied, n + 1)
                if not (isinstance(n, int) and n < 2):
                    act.wait_ge(s2_ready, (n - 1) * NP2)
                for s in range(3):
                    act.dma_start(q2[96 + s:97 + s, b].rearrange("a h (t n) -> a (h t) n", n=P),
                                  neg_rows[s * REP * TB:(s + 1) * REP * TB, :]).then_inc(neg_placed, 16)

            place_maxima(0, 0)

            def body(i, first, last):
                for b in range(NB):
                    for z in range(NQ):
                        weights(i, b, z)
                        if z == ZT and not (last and b == 1):
                            place_maxima(2 * i + b + 1, 1 - b)

            run(act, body)

        @block.tensor
        def _(pe):
            def scores_for_maximum(n, i, b, p):
                t, h, half = MAXIMA[p]
                if p == 0:
                    pe.wait_ge(loaded1[b], 192 * (i + 1))
                if not (isinstance(n, int) and n == 0 and p < RB):
                    pe.wait_ge(s1_read, n * (NM + 1) + p - RB + 1)
                if p == 0 and not (isinstance(n, int) and n == 0):
                    pe.wait_ge(neg_copied, n)
                c0, c1 = (512, (t + 1) * P) if half else (0, min(512, (t + 1) * P))
                diagonal = c1 == (t + 1) * P
                last = pe.matmul(s1[:, p % RB, 0:c1 - c0], q1[0:96, b, h, t * P:(t + 1) * P], k1[0:96, b, c0:c1],
                                 start=True, stop=not diagonal)
                if diagonal:
                    last = pe.matmul(s1[:, p % RB, c1 - c0 - P:c1 - c0], ident_b[:], causal_b[:],
                                     start=False, stop=True)
                last.then_inc(s1_ready, 1)

            def turn_maxima(n):
                pe.wait_ge(mx_step, 4 * n + 4)
                pe.transpose(s1[0:3 * REP * TB, 0, 0:P // 2].bitcast(BF16),
                             neg_parts[:].rearrange("p s x -> p (s x)"), ident_b[:]).then_inc(neg_turned, 1)

            def scores(i, b, z, h):
                c, j = QUADS[z]
                q0 = max(0, j - CT * c) * P
                n, p = 2 * i + b, z * REP + h
                if p == 0:
                    pe.wait_ge(loaded2[b], 192 * (i + 1))
                    pe.wait_ge(neg_placed, 48 * (n + 1))
                if not (isinstance(n, int) and n == 0 and p < RB):
                    pe.wait_ge(prob_ready, n * NP2 + p - RB + 1)
                diagonal = j >= CT * c
                last = pe.matmul(s2[:, p % RB, q0:CW], k2[:, b, j * P:(j + 1) * P],
                                 q2[:, b, h, c * CW + q0:(c + 1) * CW], start=True, stop=not diagonal)
                if diagonal:
                    last = pe.matmul(s2[:, p % RB, q0:q0 + P], causal_b[:], ident_b[:], start=False, stop=True)
                last.then_inc(s2_ready, 1)

            def product(i, b, z):
                c, j = QUADS[z]
                q0 = max(0, j - CT * c) * P
                n = 2 * i + b
                pe.wait_ge(prob_ready, n * NP2 + (z + 1) * REP)
                if z == 0:
                    pe.wait_ge(v_ready, n + 1)
                if j == 0 and not (isinstance(n, int) and n == 0):
                    pe.wait_ge(turned_ready, 2 * n + c - 1)
                for h in range(REP):
                    last = pe.matmul(ov[32 * h:32 * h + 32, c, q0:CW], v[:, b, j, :],
                                     prob[:, z % g.RING_Q, h, q0:CW], start=(j == 0), stop=(j == CT * (c + 1) - 1),
                                     skip_group_check=True)
                last.then_inc(pv_done, 1)

            def project(tile):
                if tile == 0:
                    pe.wait_ge(w_loaded, 16)
                    pe.wait_ge(heads_loaded[0], 48)
                if tile == TB:
                    pe.wait_ge(heads_loaded[1], 32)
                if tile >= TB and tile % CT == 0:
                    pe.wait_ge(late_loaded[(tile - TB) // CT], 16)
                if tile >= RB:
                    pe.wait_ge(x_added, tile - RB + 1)
                for k in range(KD):
                    last = pe.matmul(s1[:, tile % RB, :], heads_all[:, k, tile * P:(tile + 1) * P], out_w[:, k, :],
                                     start=(k == 0), stop=(k == KD - 1))
                last.then_inc(proj_ready, 1)

            pe.wait_ge(zeroed, 2)
            for piece in ahead_of_all[0]:
                scores_for_maximum(*piece)
            turn_maxima(0)
            for piece in ahead_of_all[1]:
                scores_for_maximum(*piece)

            def body(i, first, last):
                for b in range(NB):
                    n = 2 * i + b
                    for z in range(NQ):
                        pieces = ahead(i, b, z, first, last)
                        for h in range(REP):
                            scores(i, b, z, h)
                            for piece in pieces[len(pieces) * h // REP:len(pieces) * (h + 1) // REP]:
                                scores_for_maximum(*piece)
                            if h == 1:
                                if z >= g.LAGQ:
                                    product(i, b, z - g.LAGQ)
                                elif not (first and b == 0):
                                    product(i if b else i - 1, 1 - b, z - g.LAGQ + NQ)
                        if z == ZT and not (last and b == 1):
                            turn_maxima(n + 1)
                        if last and b == 1 and z >= NQ - TB:
                            project(z - (NQ - TB))

            run(pe, body)
            for z in range(g.LAGQ):
                product(G - 1, 1, z - g.LAGQ + NQ)
            for tile in range(TB, NT):
                project(tile)


def grouped_inputs(nc, io, consts, vtok, scratch):
    q3, k3, _ = scratch
    with ExitStack() as ctx:
        sb, ps, sem = scope(nc, ctx, "gi")
        norm = Norm(nc, ctx, "gi", consts["X"], consts["ident"])
        wq = sb("wq", [P, KD, D])
        wk = sb("wk", [P, KD, P])
        wv = sb("wv", [P, KD, P])
        bo = sb("bo", [P, D])
        parts = sb("parts", [P, 2, 3, 512], BF16)
        rest = sb("rest", [P, 2, 512])
        pv = ps("pv", [P, 2, 512])
        pq = ps("pq", [P, 4, 512])
        wkv_loaded, w_loaded, v_ready, v_read = sem("wkv_loaded"), sem("w_loaded"), sem("v_ready"), sem("v_read")
        q_ready, high_ready, rest_ready, mid_ready, low_ready = (
            sem("q_ready"), sem("high_ready"), sem("rest_ready"), sem("mid_ready"), sem("low_ready"))
        stored = [sem("stored_even"), sem("stored_odd")]
        bias_added = sem("bias_added")
        NQ = 5 * 4
        block = ctx.enter_context(nc.Block())

        @block.sync
        def _(sp):
            wkv = io["b_Wkv"].rearrange("(k p) (g two d) -> p k g two d", p=P, two=2, d=HD)
            for k in range(KD):
                for n, w in enumerate((wk, wv)):
                    sp.dma_start(w[:, k, :].rearrange("p (g d) -> p g d", d=HD), wkv[:, k, :, n, :])\
                        .then_inc(wkv_loaded, 16)
            sp.dma_start(wq[:], io["b_Wq"].rearrange("(k p) n -> p k n", p=P)).then_inc(w_loaded, 16)
            sp.dma_start(bo[:], io["b_bo"].partition_broadcast(P)).then_inc(w_loaded, 16)
            for n in range(NQ):
                c, m = divmod(n, 5)
                sp.wait_ge(low_ready, n + 1)
                cols = slice(c * 512, (c + 1) * 512)
                b, part = divmod(c, 2)
                for s in range(3):
                    dst = q3[s, m * P:(m + 1) * P, cols] if m < 4 else (
                        k3[s].rearrange("(g b) d t -> b g d t", b=NB)[b, :, :, part * 512:(part + 1) * 512])
                    sp.dma_start(dst, parts[:, n % 2, s]).then_inc(stored[n % 2], 16)
            for s in stored:
                sp.wait_ge(s, 48 * (NQ // 2))

        @block.vector
        def _(dve):
            norm.vector_stats(dve, 0)

            def split(n):
                dve.wait_ge(high_ready, n + 1)
                if n >= 2:
                    dve.wait_ge(low_ready, n - 1)
                dve.scalar_tensor_tensor(rest[:, n % 2], pq[:, n % 4], 0.25 if n % 5 < 4 else 1.0,
                                         parts[:, n % 2, 0], ALU.mult, ALU.subtract).then_inc(rest_ready, 1)

            def values(t):
                dve.wait_ge(v_ready, t + 1)
                to = vtok[:].rearrange("p (g b) t d -> p b t g d", b=NB)[:, t // TB, t % TB]
                dve.tensor_copy(to, pv[:, t % 2, 0:P].rearrange("p (g d) -> p g d", d=HD)).then_inc(v_read, 1)

            for t in range(NT):
                norm.vector_h(dve, t)
                if norm.stats_behind(t):
                    norm.vector_stats(dve, t // 4 + 1)
                if t >= 2:
                    values(t - 2)
                if t % 4 == 1 and t > 4:
                    for m in range(5):
                        split((t // 4 - 1) * 5 + m)
            values(NT - 2)
            values(NT - 1)
            for m in range(5):
                split(15 + m)

        @block.scalar
        def _(act):
            norm.scalar_sqrt(act, 0)

            def high(n):
                act.wait_ge(q_ready, n + 1)
                if n >= 2:
                    act.wait_ge(stored[n % 2], 48 * (n // 2))
                act.mul(parts[:, n % 2, 0], pq[:, n % 4], 0.25 if n % 5 < 4 else 1.0).then_inc(high_ready, 1)

            def mid(n):
                act.wait_ge(rest_ready, n + 1)
                act.copy(parts[:, n % 2, 1], rest[:, n % 2]).then_inc(mid_ready, 1)

            for t in range(NT):
                norm.scalar_hT(act, t)
                if norm.stats_behind(t):
                    norm.scalar_sqrt(act, t // 4 + 1)
                if t % 4 == 1 and t > 4:
                    for m in range(5):
                        n = (t // 4 - 1) * 5 + m
                        high(n)
                        mid(n)
            for n in range(15, 20):
                high(n)
                mid(n)

        @block.gpsimd
        def _(pool):
            pool.wait_ge(w_loaded, 32)
            for n in range(NQ):
                if n % 5 == 0:
                    for t in range(4 * (n // 5), 4 * (n // 5) + 4):
                        pool.wait_ge(norm.s_h, t + 1)
                        pool.tensor_tensor(consts["X"][:, t, :], consts["X"][:, t, :], bo[:],
                                           ALU.add).then_inc(bias_added, 1)
                pool.wait_ge(mid_ready, n + 1)
                pool.tensor_tensor(parts[:, n % 2, 2], rest[:, n % 2], parts[:, n % 2, 1],
                                   ALU.subtract).then_inc(low_ready, 1)

        @block.tensor
        def _(pe):
            def values(t):
                pe.wait_ge(norm.s_hT, t + 1)
                if t == 0:
                    pe.wait_ge(wkv_loaded, 128)
                if t >= 2:
                    pe.wait_ge(v_read, t - 1)
                for k in range(KD):
                    last = pe.matmul(pv[:, t % 2, 0:P], norm.hT[:, k, t * P:(t + 1) * P], wv[:, k, :],
                                     start=(k == 0), stop=(k == KD - 1))
                last.then_inc(v_ready, 1)

            def project(c):
                for m in range(5):
                    n = 5 * c + m
                    if n == 0:
                        pe.wait_ge(w_loaded, 32)
                    if n >= 4:
                        pe.wait_ge(rest_ready, n - 3)
                    for k in range(KD):
                        w = wq[:, k, m * P:(m + 1) * P] if m < 4 else wk[:, k, :]
                        last = pe.matmul(pq[:, n % 4, :], w, norm.hT[:, k, c * 512:(c + 1) * 512],
                                         start=(k == 0), stop=(k == KD - 1))
                    last.then_inc(q_ready, 1)

            for t in range(NT):
                norm.tensor_transpose(pe, t)
                if t >= 1:
                    values(t - 1)
                if t % 4 == 1 and t > 4:
                    project(t // 4 - 1)
            values(NT - 1)
            project(3)


def memory_weights(nc, io, consts, mem):
    ident = consts["ident"]
    with ExitStack() as ctx:
        sb, ps, sem = scope(nc, ctx, "mw")
        raw = {n: sb(n, s) for n, s in (("Wq", [BOT, D]), ("Wr", [RDIM, BOT]), ("keys", [P, BOT]), ("vals", [P, D]),
                                        ("Wvd", [VB, D]), ("Wvu", [P, KD, VB]), ("Wu1", [P, D]))}
        rhs = sb("rhs", [BOT, 2 * P])
        keysT = sb("keysT", [BOT, P])
        WrT = sb("WrT", [BOT, RDIM])
        rkT = sb("rkT", [RDIM, P])
        valsT = sb("valsT", [P, KD, P])
        WvdT = sb("WvdT", [P, KD, VB])
        WvuT = sb("WvuT", [VB, D])
        lowT = sb("lowT", [VB, P])
        bank = ps("bank", [P, 2, 512])
        loaded, vectors_loaded = sem("loaded"), sem("vectors_loaded")
        made, read = sem("made"), sem("read")
        block = ctx.enter_context(nc.Block())
        NRAW = len(raw)

        @block.sync
        def _(sp):
            for n, (to, of) in enumerate(((raw["Wq"][:], io["f_Wq"]), (raw["Wr"][:], io["f_Wr"]), (raw["keys"][:], io["f_aux_keys"]),
                           (raw["vals"][:], io["f_aux_values"]), (raw["Wvd"][:], io["f_Wvd"]),
                           (raw["Wvu"][:], io["f_Wvu"].rearrange("(k p) v -> p k v", p=P)), (raw["Wu1"][:], io["f_Wu1"]),
                           (mem["logit_bias"][:, 0:P], io["f_log_rel"].partition_broadcast(P)),
                           (mem["logit_bias"][:, P:2 * P], io["f_log_rel"].partition_broadcast(P)),
                           (mem["logit_bias"][:, 2 * P:], io["f_bu1"].partition_broadcast(P)),
                           (mem["u2"][:], io["f_Wu2"].rearrange("a n -> (a n)").partition_broadcast(P)),
                           (mem["bu2"][:], io["f_bu2"].partition_broadcast(P)),
                           (mem["gw1"][:], io["f_gate_w1"].partition_broadcast(P)),
                           (mem["gbias"][:], io["f_gate_bias"].partition_broadcast(P)))):
                sp.dma_start(to, of).then_inc(loaded if n < NRAW else vectors_loaded, 16)
            sp.wait_ge(vectors_loaded, 16 * 7)

        def turned(dst, of, rows):
            return lambda pe, b: pe.transpose(bank[0:of.shape[-1], b, dst:dst + rows], of, ident[0:rows, 0:rows])

        def product(out, lhsT, rhs_, start=True, stop=True):
            return lambda pe, b: pe.matmul(out(b), lhsT, rhs_, start=start, stop=stop)

        stages = [
            ([turned(0, raw["keys"][:], P), turned(P, raw["Wr"][:], RDIM)],
             [(keysT[:], lambda b: bank[0:BOT, b, 0:P], 1.0), (WrT[:], lambda b: bank[0:BOT, b, P:P + RDIM], 1.0),
              (rhs[:, P:], lambda b: bank[0:BOT, b, 0:P], float(1.0 / np.sqrt(BOT)))]),
            ([turned(k * P, raw["vals"][:, k * P:(k + 1) * P], P) for k in range(KD)],
             [(valsT[:], lambda b: bank[:, b, :].rearrange("p (k n) -> p k n", k=KD), 1.0)]),
            ([turned(k * VB, raw["Wvd"][:, k * P:(k + 1) * P], VB) for k in range(KD)],
             [(WvdT[:], lambda b: bank[:, b, 0:KD * VB].rearrange("p (k n) -> p k n", k=KD), 1.0)]),
            ([turned(k * P, raw["Wvu"][:, k, :], P) for k in range(KD)],
             [(WvuT[:], lambda b: bank[0:VB, b, :], 1.0)]),
            ([turned(k * P, raw["Wu1"][:, k * P:(k + 1) * P], P) for k in range(KD)],
             [(mem["logit_w"][:, :, 2 * P:], lambda b: bank[:, b, :].rearrange("p (k n) -> p k n", k=KD), 1.0)]),
            ([product(lambda b: bank[0:RDIM, b, 0:P], WrT[:], keysT[:])],
             [(rkT[:], lambda b: bank[0:RDIM, b, 0:P], 1.0)]),
            ([product(lambda b: bank[0:VB, b, 0:P], WvdT[:, k, :], valsT[:, k, :], k == 0, k == KD - 1)
              for k in range(KD)],
             [(lowT[:], lambda b: bank[0:VB, b, 0:P], 1.0)]),
            ([product(lambda b: bank[0:BOT, b, 0:P], raw["Wr"][:], rkT[:])],
             [(rhs[:, 0:P], lambda b: bank[0:BOT, b, 0:P], float(1.0 / np.sqrt(RDIM)))]),
            ([product(lambda b: bank[:, b, :], lowT[:], WvuT[:])],
             [(mem["value_w"][:], lambda b: bank[:, b, :], 1.0)]),
        ] + [
            ([product(lambda b, o=o: bank[:, b, o * 256:o * 256 + 256], raw["Wq"][:, k * P:(k + 1) * P], rhs[:])
              for o, k in enumerate((kk, kk + 1))],
             [(mem["logit_w"][:, kk:kk + 2, 0:2 * P],
               lambda b: bank[:, b, :].rearrange("p (k n) -> p k n", k=2), 1.0)])
            for kk in (0, 2)
        ]
        reads = [sum(len(st[1]) for st in stages[:n + 1]) for n in range(len(stages))]
        needs = {5: 0, 6: 2, 7: 5, 8: 6, 9: 7, 10: 7}

        @block.tensor
        def _(pe):
            pe.wait_ge(loaded, 16 * NRAW)
            for n, (mms, _) in enumerate(stages):
                before = max(needs.get(n, 0), n - 2)
                if n >= 2:
                    pe.wait_ge(read, reads[before])
                for mm in mms:
                    last = mm(pe, n % 2)
                last.then_inc(made, 1)

        @block.vector
        def _(dve):
            for n, (_, outs) in enumerate(stages):
                dve.wait_ge(made, n + 1)
                for dst, src, scale in outs:
                    dve.tensor_scalar(dst, src(n % 2), scale, None, ALU.mult).then_inc(read, 1)


def memory_block(nc, io, consts, mem, tag, out):
    X, ident = consts["X"], consts["ident"]
    with ExitStack() as ctx:
        sb, ps, sem = scope(nc, ctx, tag)
        norm = Norm(nc, ctx, tag, X, ident)
        logits = sb("logits", [P, NT, 3 * P])
        top = sb("top", [P, NT, 8])
        rest = sb("rest", [P, 2, 4, P])
        chosen = sb("chosen", [P, 2, 4, P])
        negmax = sb("negmax", [P, NT])
        weight = sb("weight", [P, 2, 4, P])
        wsum = sb("wsum", [P, NT])
        weightT = sb("weightT", [P, T])
        small = sb("small", [P, 24, NT])
        gel = sb("gel", [P, 3, NT, UH])
        ones = sb("ones", [P, P])
        mean = sb("mean", [P, 2])
        gain = sb("gain", [P, NT])
        plog = ps("plog", [P, 2, 512])
        pturn = ps("pturn", [P, 512])
        pmean = ps("pmean", [P, 512])
        pout = ps("pout", [P, 2, 512])
        lg_ready, lg_read = sem("lg_ready"), sem("lg_read")
        top_ready, rest_ready, same_ready, chosen_ready, nm_ready = (
            sem("top_ready"), sem("rest_ready"), sem("same_ready"), sem("chosen_ready"), sem("nm_ready"))
        w_ready, wT_ready, wT_read = sem("w_ready"), sem("wT_ready"), sem("wT_read")
        ln_in, ln_done = sem("ln_in"), sem("ln_done")
        mean_in, mean_done, ones_ready = sem("mean_in"), sem("mean_done"), sem("ones_ready")
        tanh_in, tanh_done, sigmoid_in, cubed = sem("tanh_in"), sem("tanh_done"), sem("sigmoid_in"), sem("cubed")
        out_ready, x_ready, stored = sem("out_ready"), sem("x_ready"), sem("stored")
        gain_ready, normed_added = sem("gain_ready"), sem("normed_added")
        chain = sem("chain")
        banks = [pout[:, 0], pout[:, 1], plog[:, 0], plog[:, 1]]
        block = ctx.enter_context(nc.Block())

        def hidden(c):
            four = slice(4 * c, 4 * c + 4)
            return logits[:, four, 2 * P:3 * P], [gel[:, n, four] for n in range(3)]

        @block.vector
        def _(dve):
            linked = [0]

            def link(instruction):
                linked[0] += 1
                instruction.then_inc(chain, 1)
                dve.wait_ge(chain, linked[0])

            norm.vector_stats(dve, 0)
            (v2, v3, u, ln, less, zero, num, den, rden, lv, me, nv, lsum, lrn, lt, un, un2, gz, gt, gate, ok, rs,
             sc, shift) = (small[:, n, :] for n in range(24))
            def read_logits(t):
                dve.wait_ge(lg_ready, t + 1)
                dve.tensor_tensor(logits[:, t, :], plog[:, t % 2, 0:3 * P], mem["logit_bias"][:],
                                  ALU.add).then_inc(lg_read, 1)

            def find_best(c):
                tiles = range(4 * c, 4 * c + 4)
                par = c % 2
                for t in tiles:
                    dve.wait_ge(lg_read, t + 1)
                    dve.max(top[:, t, :], logits[:, t, 0:P]).then_inc(top_ready, 1)
                for t in tiles:
                    dve.wait_ge(top_ready, t + 1)
                    dve.match_replace(rest[:, par, t % 4, :], top[:, t, :], logits[:, t, 0:P], -3.4e38)\
                        .then_inc(rest_ready, 1)

            def bar_others(c):
                par = c % 2
                dve.wait_ge(rest_ready, 4 * c + 4)
                if c >= 2:
                    dve.wait_ge(w_ready, 4 * c - 4)
                four = slice(4 * c, 4 * c + 4)
                dve.tensor_tensor(chosen[:, par], rest[:, par], logits[:, four, 0:P], ALU.is_equal)\
                    .then_inc(same_ready, 1)
                dve.wait_ge(same_ready, c + 1)
                dve.scalar_tensor_tensor(chosen[:, par], chosen[:, par], NEG, logits[:, four, P:2 * P],
                                         ALU.mult, ALU.add).then_inc(chosen_ready, 1)
                dve.wait_ge(chosen_ready, c + 1)
                dve.reduce_max(negmax[:, four], chosen[:, par], AX, negate=True).then_inc(nm_ready, 1)

            def gelu(c):
                hid, (sq, z, th) = hidden(c)
                dve.wait_ge(tanh_done, c + 1)
                link(dve.scalar_tensor_tensor(sq, th, 1.0, hid, ALU.add, ALU.mult))
                link(dve.tensor_tensor(z, sq, mem["u2"][:].unsqueeze(1).broadcast_to([P, 4, UH]), ALU.mult))
                link(dve.reduce_sum(lsum[:, 4 * c:4 * c + 4], z, AX))

            for t in range(NT):
                norm.vector_h(dve, t)
                if norm.stats_behind(t):
                    norm.vector_stats(dve, t // 4 + 1)
                if t == NT - 2:
                    link(dve.tensor_tensor(v2, norm.mv[:, :, 1], norm.rstd[:], ALU.mult))
                    link(dve.tensor_tensor(v3, v2, norm.rstd[:], ALU.mult))
                    dve.tensor_scalar(u, v3, 1.0, None, ALU.add).then_inc(ln_in, 1)
                    link(dve.tensor_tensor(shift, norm.mv[:, :, 0], norm.rstd[:], ALU.mult))
                    link(dve.tensor_scalar(shift, shift, -1.0, None, ALU.mult))
                    dve.tensor_scalar(gain[:], norm.rstd[:], 1.0, None, ALU.add).then_inc(gain_ready, 1)
                if t < 2:
                    continue
                read_logits(t - 2)
                if t % 4 == 2 and t > 6:
                    gelu(t // 4 - 2)
                if t % 4 == 2 and t > 2:
                    find_best(t // 4 - 1)
                if t % 4 == 3 and t > 4:
                    bar_others(t // 4 - 1)
            read_logits(NT - 2)
            read_logits(NT - 1)
            find_best(3)
            bar_others(3)
            dve.wait_ge(ln_in, 1)
            link(dve.tensor_scalar(less, u, 1.0, None, ALU.subtract))
            link(dve.tensor_scalar(zero, less, 0.0, None, ALU.is_equal))
            link(dve.tensor_tensor(den, less, zero, ALU.add))
            link(dve.reciprocal(rden, den))
            dve.wait_ge(ln_done, 1)
            link(dve.tensor_tensor(num, ln, zero, ALU.add))
            link(dve.tensor_tensor(num, num, v3, ALU.mult))
            link(dve.tensor_tensor(lv, num, rden, ALU.mult))
            dve.reduce_sum(mean[:, 0:1], lv, AX).then_inc(mean_in, 1)
            gelu(2)
            gelu(3)

            dve.wait_ge(mean_done, 1)
            link(dve.tensor_scalar(me[:, 0:1], pmean[:, 0:1], 1e-6, None, ALU.add))
            link(dve.reciprocal(mean[:, 1:2], me[:, 0:1]))
            link(dve.tensor_scalar(nv, lv, mean[:, 1:2], 0.5, ALU.mult, ALU.mult))
            dve.tensor_scalar(lrn, lsum, 0.5, mem["bu2"][:, 0:1], ALU.mult, ALU.add).then_inc(sigmoid_in, 1)
            dve.wait_ge(tanh_done, 5)
            link(dve.tensor_scalar(un, lt, 1.25, 1.25, ALU.mult, ALU.add))
            link(dve.tensor_tensor(un, un, nv, ALU.add))
            link(dve.tensor_scalar(un, un, 0.0, 5.0, ALU.max, ALU.min))
            link(dve.tensor_scalar(un, un, 0.5, 1.0 / 1.5, ALU.subtract, ALU.mult))
            link(dve.tensor_scalar(un2, un, 0.0, 1.0, ALU.max, ALU.min))
            dve.tensor_scalar(gz, un2, mem["gw1"][:, 0:1], mem["gbias"][:, 0:1], ALU.mult, ALU.add)\
                .then_inc(sigmoid_in, 1)
            dve.wait_ge(tanh_done, 6)
            link(dve.tensor_scalar(gate, gt, 0.5, 0.5, ALU.mult, ALU.add))
            link(dve.tensor_scalar(ok, gate, 0.05, None, ALU.is_ge))
            link(dve.tensor_tensor(gate, gate, ok, ALU.mult))
            dve.wait_ge(w_ready, NT)
            link(dve.reciprocal(rs, wsum[:]))
            link(dve.tensor_tensor(sc, gate, rs, ALU.mult))
            for t in range(NT):
                dve.wait_ge(out_ready, t + 1)
                dve.wait_ge(normed_added, t + 1)
                dve.scalar_tensor_tensor(X[:, t, :], banks[t % 4], sc[:, t:t + 1], X[:, t, :],
                                         ALU.mult, ALU.add).then_inc(x_ready, 1)

        @block.scalar
        def _(act):
            norm.scalar_sqrt(act, 0)
            def weights(c):
                for t in range(4 * c, 4 * c + 4):
                    act.wait_ge(nm_ready, c + 1)
                    if c >= 2:
                        act.wait_ge(wT_ready, c - 1)
                    act.activation(weight[:, c % 2, t % 4, :], chosen[:, c % 2, t % 4, :], ACT.Exp,
                                   bias=negmax[:, t:t + 1], accum_out=wsum[:, t:t + 1]).then_inc(w_ready, 1)

            def tanh(c):
                act.wait_ge(tanh_in, c + 1)
                act.activation(gel[:, 2, 4 * c:4 * c + 4], gel[:, 1, 4 * c:4 * c + 4], ACT.Tanh,
                               scale=float(np.sqrt(2.0 / np.pi))).then_inc(tanh_done, 1)

            def read_turned(c):
                act.wait_ge(wT_ready, c + 1)
                act.copy(weightT[:, c * 512:(c + 1) * 512], pturn[:]).then_inc(wT_read, 1)

            for t in range(NT):
                norm.scalar_hT(act, t)
                if norm.stats_behind(t):
                    norm.scalar_sqrt(act, t // 4 + 1)
                if t % 4 == 0 and t > 4:
                    weights(t // 4 - 2)
                    tanh(t // 4 - 2)
                if t % 4 == 2 and t > 8:
                    read_turned(t // 4 - 2)
            weights(2)
            tanh(2)
            act.wait_ge(ln_in, 1)
            act.activation(small[:, 3, :], small[:, 2, :], ACT.Ln).then_inc(ln_done, 1)
            read_turned(2)
            weights(3)
            tanh(3)
            read_turned(3)
            act.wait_ge(sigmoid_in, 1)
            act.activation(small[:, 14, :], small[:, 13, :], ACT.Tanh, scale=0.5).then_inc(tanh_done, 1)
            act.wait_ge(sigmoid_in, 2)
            act.activation(small[:, 18, :], small[:, 17, :], ACT.Tanh, scale=0.5).then_inc(tanh_done, 1)

        @block.gpsimd
        def _(pool):
            pool.memset(ones[:], 1.0 / T).then_inc(ones_ready, 1)

            def tanh_argument(c):
                hid, (sq, z, _) = hidden(c)
                pool.wait_ge(lg_read, 4 * c + 4)
                pool.tensor_tensor(sq, hid, hid, ALU.mult).then_inc(cubed, 1)
                pool.wait_ge(cubed, 2 * c + 1)
                pool.tensor_scalar(sq, sq, 0.044715, 1.0, ALU.mult, ALU.add).then_inc(cubed, 1)
                pool.wait_ge(cubed, 2 * c + 2)
                pool.tensor_tensor(z, sq, hid, ALU.mult).then_inc(tanh_in, 1)

            for c in range(3):
                tanh_argument(c)
            pool.wait_ge(gain_ready, 1)
            for t in range(NT):
                if t == 2:
                    tanh_argument(3)
                pool.wait_ge(norm.s_h, t + 1)
                pool.tensor_scalar(X[:, t, :], X[:, t, :], gain[:, t:t + 1], small[:, 23, t:t + 1],
                                   ALU.mult, ALU.add).then_inc(normed_added, 1)

        @block.tensor
        def _(pe):
            def logit(t):
                pe.wait_ge(norm.s_hT, t + 1)
                if t >= 2:
                    pe.wait_ge(lg_read, t - 1)
                for k in range(KD):
                    last = pe.matmul(plog[:, t % 2, 0:3 * P], norm.hT[:, k, t * P:(t + 1) * P],
                                     mem["logit_w"][:, k, :], start=(k == 0), stop=(k == KD - 1))
                last.then_inc(lg_ready, 1)

            def turn(c):
                pe.wait_ge(w_ready, 4 * c + 4)
                if c >= 1:
                    pe.wait_ge(wT_read, c)
                for j in range(4):
                    last = pe.transpose(pturn[:, j * P:(j + 1) * P], weight[:, c % 2, j, :], ident[:])
                last.then_inc(wT_ready, 1)

            for t in range(NT):
                norm.tensor_transpose(pe, t)
                if t >= 1:
                    logit(t - 1)
                if t % 4 == 1 and t >= 8:
                    turn(t // 4 - 2)
            logit(NT - 1)
            turn(2)
            pe.wait_ge(ones_ready, 1)
            pe.wait_ge(mean_in, 1)
            pe.matmul(pmean[:, 0:1], ones[:], mean[:, 0:1], start=True, stop=True).then_inc(mean_done, 1)
            turn(3)
            for t in range(NT):
                pe.wait_ge(wT_read, t // 4 + 1)
                if t == 0:
                    pe.wait_ge(lg_read, NT)
                if t >= 4:
                    pe.wait_ge(x_ready, t - 3)
                pe.matmul(banks[t % 4], weightT[:, t * P:(t + 1) * P], mem["value_w"][:],
                          start=True, stop=True).then_inc(out_ready, 1)

        @block.sync
        def _(sp):
            if out is not None:
                o = out.rearrange("b (t p) d -> p (b t) d", p=P)
                for t in range(0, NT, 2):
                    sp.wait_ge(x_ready, t + 2)
                    sp.dma_start(o[:, t:t + 2, :], X[:, t:t + 2, :]).then_inc(stored, 16)
                sp.wait_ge(stored, 16 * (NT // 2))


_NAMES = {"L0_attn_a_hidden_states": "x", "L0_attn_a_w_q_down": "w_q_down", "L0_attn_a_w_q_up_nope": "w_q_up_nope",
          "L0_attn_a_w_q_up_rope": "w_q_up_rope", "L0_attn_a_w_kv_down": "w_kv_down",
          "L0_attn_a_w_k_rope": "w_k_rope", "L0_attn_a_w_uk": "w_uk", "L0_attn_a_w_uv": "w_uv",
          "L0_attn_a_w_out": "w_out", "L0_attn_b_Wq": "b_Wq", "L0_attn_b_Wkv": "b_Wkv", "L0_attn_b_Wo": "b_Wo",
          "L0_attn_b_bo": "b_bo", "L0_ffn_Wq": "f_Wq", "L0_ffn_Wr": "f_Wr", "L0_ffn_aux_keys": "f_aux_keys",
          "L0_ffn_aux_values": "f_aux_values", "L0_ffn_Wvd": "f_Wvd", "L0_ffn_Wvu": "f_Wvu", "L0_ffn_Wu1": "f_Wu1",
          "L0_ffn_bu1": "f_bu1", "L0_ffn_Wu2": "f_Wu2", "L0_ffn_bu2": "f_bu2", "L0_ffn_gate_w1": "f_gate_w1",
          "L0_ffn_gate_bias": "f_gate_bias", "L0_ffn_log_rel": "f_log_rel"}


def _tables():
    f = np.float32
    freqs = f(1.0) / np.power(f(10000.0), np.arange(0, DR, 2, dtype=f) / f(DR))
    wavelengths = f(2.0 * np.pi) / freqs
    ramp = np.clip((wavelengths / f(4096.0) - f(1.0)) / f(31.0), f(0), f(1)).astype(f)
    inv_freq = (freqs / (f(1.0) - ramp + ramp * f(40.0))).astype(f)
    angle = (np.arange(S, dtype=f)[:, None] * inv_freq[None, :]).astype(f)
    cos, sin = np.cos(angle).astype(f), np.sin(angle).astype(f)
    tok = lambda a: np.ascontiguousarray(np.tile(a.reshape(TB, P, 32).transpose(1, 0, 2), (1, NB, 1)))
    scaled = f(SCALE_A)

    def rows(low, high):
        quads = [part[:, 16 * q:16 * q + 16].T for q in range(2) for part in (low, high)]
        return np.ascontiguousarray(np.concatenate(quads * 2, axis=0) * scaled)

    i = np.arange(P)
    return {"identity": np.eye(P, dtype=f), "causal": np.where(i[None, :] > i[:, None], f(NEG), f(0)).astype(f),
            "cos_tok": tok(cos), "sin_tok": tok(sin), "cos_rows": rows(cos, cos), "sin_rows": rows(-sin, sin)}


def kernel(**inputs):
    import numpy as _np
    import concourse.bacc as _bacc
    from concourse import mybir as _mybir
    from concourse.bass_utils import run_bass_kernel_spmd as _run

    nc = _bacc.Bacc("TRN2", target_bir_lowering=False, num_devices=1)
    arrays, io = {}, {}
    given = {short: _np.atleast_1d(_np.ascontiguousarray(inputs[name])) for name, short in _NAMES.items()}
    for short, a in {**given, **_tables()}.items():
        arrays[f"in_{short}"] = a
        io[short] = nc.dram_tensor(f"in_{short}", a.shape, _mybir.dt.from_np(a.dtype), kind="ExternalInput").ap()
    io["out"] = nc.dram_tensor("out_dram", (NB, S, D), _mybir.dt.float32, kind="ExternalOutput").ap()
    build(nc, io)
    r = _run(nc, [arrays], core_ids=[0])
    return r.results[0]["out_dram"]
```
